# Optimizing a Trainium2 kernel written in Bass

```python
import numpy as np
import jax
import jax.numpy as jnp

def _softmax(x, axis=-1):
    return jax.nn.softmax(x, axis=axis)

def _gelu(x):
    return jax.nn.gelu(x, approximate=True)

def _silu(x):
    return jax.nn.silu(x)

def _sigmoid(x):
    return jax.nn.sigmoid(x)

def _layernorm(x, axis=-1, eps=1e-05):
    m = jnp.mean(x, axis=axis, keepdims=True)
    v = jnp.var(x, axis=axis, keepdims=True)
    return (x - m) / jnp.sqrt(v + eps)

def _scatter_add(tgt, idx, src, axis=0):
    return tgt.at[idx].add(src)

def _segment_sum(src, seg, n):
    return jax.ops.segment_sum(src, seg, n)
kernel_name = 'mk_perceiver_d1_seqx_r4_973fd2'

def setup_inputs(seed: int=0):
    np.random.seed(seed)
    _w = jnp.asarray

    def _rec_inputs():
        import jax
        import jax.numpy as jnp
        _rk = jax.random.key(seed)
        x = 7.22e-05 + 1 * jax.random.normal(jax.random.fold_in(_rk, 1), (16, 64, 512), jnp.float32)
        _lenS = 64 - jax.random.randint(jax.random.fold_in(_rk, 7), (16,), 0, max(1, 64 // 4) + 1, jnp.int32)
        _lenS2 = 1601 - jax.random.randint(jax.random.fold_in(_rk, 8), (16,), 0, max(1, 1601 // 4) + 1, jnp.int32)
        _ctx_1024P = jax.random.normal(jax.random.fold_in(_rk, 11), (16, 16, 256), jnp.float32)
        _ctx_1024c = jax.random.dirichlet(jax.random.fold_in(_rk, 511), 0.3 * jnp.ones((16,), jnp.float32), (16, 1601))
        _ctx_1024t = jnp.einsum('bsk,bkd->bsd', _ctx_1024c, _ctx_1024P)
        _ctx_1024t = _ctx_1024t * jax.lax.rsqrt(jnp.mean(jnp.square(_ctx_1024t)) + 1e-12) * 0.953939
        ctx_1024 = -0.000673644 + 1.00013 * (_ctx_1024t + 0.3 * jax.random.normal(jax.random.fold_in(_rk, 611), (16, 1601, 256), jnp.float32))
        return (x, ctx_1024)
    x, ctx_1024 = _rec_inputs()

    def _L0_xattn_setup():
        import jax, jax.numpy as jnp
        import numpy as np
        B, S1, S2, DCA = (2, 512, 256, 16)
        QDIM, KDIM, H = (512, 256, 16)
        HD = QDIM // H
        SCALE = HD ** (-0.5)
        EPS = 1e-06
        DCA_WEIGHT = 1.0

        def _ln(t, w, b):
            m = jnp.mean(t, axis=-1, keepdims=True)
            v = jnp.var(t, axis=-1, keepdims=True)
            return (t - m) * jax.lax.rsqrt(v + EPS) * w + b

        def _attn(q, k, v):
            s = jnp.einsum('bhqd,bhkd->bhqk', q, k) * SCALE
            p = jax.nn.softmax(s, axis=-1)
            return jnp.einsum('bhqk,bhkd->bhqd', p, v)
        key = jax.random.key(seed)
        ks = jax.random.split(key, 8)
        w = lambda k, shape: jax.random.normal(k, shape, jnp.float32) * 0.02
        return {'x': jax.random.normal(ks[0], (B, S1, QDIM), jnp.float32), 'y': jax.random.normal(ks[1], (B, S2 + DCA, KDIM), jnp.float32), 'Wq': w(ks[2], (QDIM, QDIM)), 'bq': jnp.zeros((QDIM,), jnp.float32), 'Wk': w(ks[3], (KDIM, QDIM)), 'bk': jnp.zeros((QDIM,), jnp.float32), 'Wv': w(ks[4], (KDIM, QDIM)), 'bv': jnp.zeros((QDIM,), jnp.float32), 'Wkv_dca': w(ks[5], (KDIM, 2 * QDIM)), 'bkv_dca': jnp.zeros((2 * QDIM,), jnp.float32), 'qn_w': jnp.ones((HD,), jnp.float32), 'qn_b': jnp.zeros((HD,), jnp.float32), 'kn_w': jnp.ones((HD,), jnp.float32), 'kn_b': jnp.zeros((HD,), jnp.float32), 'kn_dca_w': jnp.ones((HD,), jnp.float32), 'kn_dca_b': jnp.zeros((HD,), jnp.float32), 'Wo': w(ks[6], (QDIM, QDIM)), 'bo': jnp.zeros((QDIM,), jnp.float32)}
    _L0_xattn_all = _L0_xattn_setup()
    _L0_xattn_in = {k: v for k, v in _L0_xattn_all.items() if k in ('Wq', 'bq', 'Wk', 'bk', 'Wv', 'bv', 'Wkv_dca', 'bkv_dca', 'qn_w', 'qn_b', 'kn_w', 'kn_b', 'kn_dca_w', 'kn_dca_b', 'Wo', 'bo')}
    del _L0_xattn_all

    def _L0_attn_setup():
        import jax, jax.numpy as jnp
        import numpy as np
        DIM = 512
        NUM_HEADS = 16
        NUM_KV_HEADS = 4
        HEAD_DIM = DIM // NUM_HEADS
        SCALE = HEAD_DIM ** (-0.5)
        key = jax.random.key(seed)
        ks = jax.random.split(key, 5)
        B, N = (2, 512)
        init = 0.02
        x = jax.random.normal(ks[0], (B, N, DIM), dtype=jnp.float32)
        Wq = jax.random.normal(ks[1], (DIM, DIM), dtype=jnp.float32) * init
        Wk = jax.random.normal(ks[2], (DIM, NUM_KV_HEADS * HEAD_DIM), dtype=jnp.float32) * init
        Wv = jax.random.normal(ks[3], (DIM, NUM_KV_HEADS * HEAD_DIM), dtype=jnp.float32) * init
        Wo = jax.random.normal(ks[4], (DIM, DIM), dtype=jnp.float32) * init
        return {'x': x, 'Wq': Wq, 'Wk': Wk, 'Wv': Wv, 'Wo': Wo}
    _L0_attn_all = _L0_attn_setup()
    _L0_attn_in = {k: v for k, v in _L0_attn_all.items() if k in ('Wq', 'Wk', 'Wv', 'Wo')}
    del _L0_attn_all

    def _L0_ffn_setup():
        import jax, jax.numpy as jnp
        import numpy as np
        TOP_K = 2

        def moe_forward(x, w_gate_router, w_gate_proj, w_up_proj, w_down_proj):
            E = w_gate_router.shape[0]
            scores = jnp.einsum('bsd,ed->bse', x, w_gate_router)
            topk_scores, topk_idx = jax.lax.top_k(scores, TOP_K)
            topk_probs = jax.nn.softmax(topk_scores, axis=-1)
            weights = jnp.sum(topk_probs[..., None] * jax.nn.one_hot(topk_idx, E, dtype=x.dtype), axis=-2)
            gate = jnp.einsum('bsd,efd->bsef', x, w_gate_proj)
            up = jnp.einsum('bsd,efd->bsef', x, w_up_proj)
            hidden = jax.nn.silu(gate) * up
            out = jnp.einsum('bsef,edf,bse->bsd', hidden, w_down_proj, weights)
            return out
        key = jax.random.key(seed)
        k1, k2, k3, k4, k5 = jax.random.split(key, 5)
        B, S, D, E, F = (2, 256, 512, 8, 192)
        scale_in = 1.0 / np.sqrt(D)
        scale_ff = 1.0 / np.sqrt(F)
        return {'x': jax.random.normal(k1, (B, S, D), dtype=jnp.float32), 'w_gate_router': jax.random.normal(k2, (E, D), dtype=jnp.float32) * scale_in, 'w_gate_proj': jax.random.normal(k3, (E, F, D), dtype=jnp.float32) * scale_in, 'w_up_proj': jax.random.normal(k4, (E, F, D), dtype=jnp.float32) * scale_in, 'w_down_proj': jax.random.normal(k5, (E, D, F), dtype=jnp.float32) * scale_ff}
    _L0_ffn_all = _L0_ffn_setup()
    _L0_ffn_in = {k: v for k, v in _L0_ffn_all.items() if k in ('w_gate_router', 'w_gate_proj', 'w_up_proj', 'w_down_proj')}
    del _L0_ffn_all
    return {'x': x, 'ctx_1024': ctx_1024, 'L0_xattn_Wq': _L0_xattn_in['Wq'], 'L0_xattn_bq': _L0_xattn_in['bq'], 'L0_xattn_Wk': _L0_xattn_in['Wk'], 'L0_xattn_bk': _L0_xattn_in['bk'], 'L0_xattn_Wv': _L0_xattn_in['Wv'], 'L0_xattn_bv': _L0_xattn_in['bv'], 'L0_xattn_Wkv_dca': _L0_xattn_in['Wkv_dca'], 'L0_xattn_bkv_dca': _L0_xattn_in['bkv_dca'], 'L0_xattn_qn_w': _L0_xattn_in['qn_w'], 'L0_xattn_qn_b': _L0_xattn_in['qn_b'], 'L0_xattn_kn_w': _L0_xattn_in['kn_w'], 'L0_xattn_kn_b': _L0_xattn_in['kn_b'], 'L0_xattn_kn_dca_w': _L0_xattn_in['kn_dca_w'], 'L0_xattn_kn_dca_b': _L0_xattn_in['kn_dca_b'], 'L0_xattn_Wo': _L0_xattn_in['Wo'], 'L0_xattn_bo': _L0_xattn_in['bo'], 'L0_attn_Wq': _L0_attn_in['Wq'], 'L0_attn_Wk': _L0_attn_in['Wk'], 'L0_attn_Wv': _L0_attn_in['Wv'], 'L0_attn_Wo': _L0_attn_in['Wo'], 'L0_ffn_w_gate_router': _L0_ffn_in['w_gate_router'], 'L0_ffn_w_gate_proj': _L0_ffn_in['w_gate_proj'], 'L0_ffn_w_up_proj': _L0_ffn_in['w_up_proj'], 'L0_ffn_w_down_proj': _L0_ffn_in['w_down_proj']}

def reference(x, ctx_1024, L0_xattn_Wq, L0_xattn_bq, L0_xattn_Wk, L0_xattn_bk, L0_xattn_Wv, L0_xattn_bv, L0_xattn_Wkv_dca, L0_xattn_bkv_dca, L0_xattn_qn_w, L0_xattn_qn_b, L0_xattn_kn_w, L0_xattn_kn_b, L0_xattn_kn_dca_w, L0_xattn_kn_dca_b, L0_xattn_Wo, L0_xattn_bo, L0_attn_Wq, L0_attn_Wk, L0_attn_Wv, L0_attn_Wo, L0_ffn_w_gate_router, L0_ffn_w_gate_proj, L0_ffn_w_up_proj, L0_ffn_w_down_proj):
    import jax
    import jax.numpy as jnp

    def _L0_xattn_ref(x, y, Wq, bq, Wk, bk, Wv, bv, Wkv_dca, bkv_dca, qn_w, qn_b, kn_w, kn_b, kn_dca_w, kn_dca_b, Wo, bo):
        import jax, jax.numpy as jnp
        import numpy as np
        B, S1, S2, DCA = (2, 512, 256, 16)
        QDIM, KDIM, H = (512, 256, 16)
        HD = QDIM // H
        SCALE = HD ** (-0.5)
        EPS = 1e-06
        DCA_WEIGHT = 1.0

        def _ln(t, w, b):
            m = jnp.mean(t, axis=-1, keepdims=True)
            v = jnp.var(t, axis=-1, keepdims=True)
            return (t - m) * jax.lax.rsqrt(v + EPS) * w + b

        def _attn(q, k, v):
            s = jnp.einsum('bhqd,bhkd->bhqk', q, k) * SCALE
            p = jax.nn.softmax(s, axis=-1)
            return jnp.einsum('bhqk,bhkd->bhqd', p, v)
        b, s1, _ = x.shape
        y_dca = y[:, -DCA:, :]
        y_main = y[:, :-DCA, :]
        kv_dca = (y_dca @ Wkv_dca + bkv_dca).reshape(b, DCA, 2, H, HD)
        k_dca = _ln(kv_dca[:, :, 0], kn_dca_w, kn_dca_b)
        v_dca = kv_dca[:, :, 1]
        s2 = y_main.shape[1]
        q = _ln((x @ Wq + bq).reshape(b, s1, H, HD), qn_w, qn_b)
        kv = jnp.concatenate([y_main @ Wk + bk, y_main @ Wv + bv], axis=-1)
        kv = kv.reshape(b, s2, H, 2 * HD)
        k = _ln(kv[..., :HD], kn_w, kn_b)
        v = kv[..., HD:]
        qT = q.transpose(0, 2, 1, 3)
        ctx = _attn(qT, k.transpose(0, 2, 1, 3), v.transpose(0, 2, 1, 3))
        ctx = ctx.transpose(0, 2, 1, 3).reshape(b, s1, QDIM)
        ctx_dca = _attn(qT, k_dca.transpose(0, 2, 1, 3), v_dca.transpose(0, 2, 1, 3))
        ctx_dca = ctx_dca.transpose(0, 2, 1, 3).reshape(b, s1, QDIM)
        ctx = ctx + DCA_WEIGHT * ctx_dca
        return ctx @ Wo + bo

    def _L0_attn_ref(x, Wq, Wk, Wv, Wo):
        import jax, jax.numpy as jnp
        import numpy as np
        DIM = 512
        NUM_HEADS = 16
        NUM_KV_HEADS = 4
        HEAD_DIM = DIM // NUM_HEADS
        SCALE = HEAD_DIM ** (-0.5)
        B, N, _ = x.shape
        g = NUM_HEADS // NUM_KV_HEADS
        q = (x @ Wq).reshape(B, N, NUM_HEADS, HEAD_DIM).transpose(0, 2, 1, 3)
        k = (x @ Wk).reshape(B, N, NUM_KV_HEADS, HEAD_DIM).transpose(0, 2, 1, 3)
        v = (x @ Wv).reshape(B, N, NUM_KV_HEADS, HEAD_DIM).transpose(0, 2, 1, 3)
        k = jnp.repeat(k, g, axis=1)
        v = jnp.repeat(v, g, axis=1)
        attn = jnp.einsum('bhqd,bhkd->bhqk', q, k) * SCALE
        causal = jnp.triu(jnp.ones((N, N), dtype=bool), k=1)
        attn = jnp.where(causal, -jnp.inf, attn)
        attn = jax.nn.softmax(attn, axis=-1)
        out = jnp.einsum('bhqk,bhkd->bhqd', attn, v)
        out = out.transpose(0, 2, 1, 3).reshape(B, N, DIM)
        return out @ Wo

    def _L0_ffn_ref(x, w_gate_router, w_gate_proj, w_up_proj, w_down_proj):
        import jax, jax.numpy as jnp
        import numpy as np
        TOP_K = 2

        def moe_forward(x, w_gate_router, w_gate_proj, w_up_proj, w_down_proj):
            E = w_gate_router.shape[0]
            scores = jnp.einsum('bsd,ed->bse', x, w_gate_router)
            topk_scores, topk_idx = jax.lax.top_k(scores, TOP_K)
            topk_probs = jax.nn.softmax(topk_scores, axis=-1)
            weights = jnp.sum(topk_probs[..., None] * jax.nn.one_hot(topk_idx, E, dtype=x.dtype), axis=-2)
            gate = jnp.einsum('bsd,efd->bsef', x, w_gate_proj)
            up = jnp.einsum('bsd,efd->bsef', x, w_up_proj)
            hidden = jax.nn.silu(gate) * up
            out = jnp.einsum('bsef,edf,bse->bsd', hidden, w_down_proj, weights)
            return out
        return moe_forward(x, w_gate_router, w_gate_proj, w_up_proj, w_down_proj)
    x = x + _L0_xattn_ref(_layernorm(x, axis=-1), ctx_1024, L0_xattn_Wq, L0_xattn_bq, L0_xattn_Wk, L0_xattn_bk, L0_xattn_Wv, L0_xattn_bv, L0_xattn_Wkv_dca, L0_xattn_bkv_dca, L0_xattn_qn_w, L0_xattn_qn_b, L0_xattn_kn_w, L0_xattn_kn_b, L0_xattn_kn_dca_w, L0_xattn_kn_dca_b, L0_xattn_Wo, L0_xattn_bo)
    x = x + _L0_attn_ref(_layernorm(x, axis=-1), L0_attn_Wq, L0_attn_Wk, L0_attn_Wv, L0_attn_Wo)
    x = x + _L0_ffn_ref(_layernorm(x, axis=-1), L0_ffn_w_gate_router, L0_ffn_w_gate_proj, L0_ffn_w_up_proj, L0_ffn_w_down_proj)
    return x

_drawn_inputs = setup_inputs


def setup_inputs(seed=0):
    import zlib

    import numpy as np

    out = dict(_drawn_inputs(seed))
    spreads = {'L0_xattn_bq': (0.0, 0.1),
     'L0_xattn_bk': (0.0, 0.1),
     'L0_xattn_bv': (0.0, 0.1),
     'L0_xattn_bkv_dca': (0.0, 0.1),
     'L0_xattn_qn_w': (1.0, 0.2),
     'L0_xattn_qn_b': (0.0, 0.351),
     'L0_xattn_kn_w': (1.0, 0.6),
     'L0_xattn_kn_b': (0.0, 0.8),
     'L0_xattn_kn_dca_w': (1.0, 0.2),
     'L0_xattn_kn_dca_b': (0.0, 0.8),
     'L0_xattn_bo': (0.0, 0.1)}
    factors = {}
    for name, (base, spread) in spreads.items():
        noise = np.random.default_rng([zlib.crc32(name.encode()), seed]).standard_normal(out[name].shape)
        drawn = base * np.exp(spread * noise) if base else spread * noise
        out[name] = jnp.asarray(drawn.astype(out[name].dtype))
    for name, factor in factors.items():
        out[name] = (out[name] * factor).astype(out[name].dtype)
    return out
```

```python
from contextlib import ExitStack

import concourse.bass as bass
from concourse import mybir

ALU = mybir.AluOpType
ACT = mybir.ActivationFunctionType
AX_X = mybir.AxisListType.X
F32 = mybir.dt.float32
F32R = mybir.dt.float32r
U32 = mybir.dt.uint32

P = 128
B, SQ, D = 16, 64, 512
SK, DC, DCA = 1601, 256, 16
H, HD = 16, 32
T = B * SQ
NT = T // P
KD = D // P
KC = DC // P
SM = SK - DCA
CH = -(-SM // P)
LAST = CH - 1
LM = SM - LAST * P
DCA_ROW = 64
PAIRS = H // 2
GROUPS = H // 4
PW = 2 * HD + 1
KV = 4
E_, F = 8, 192
EP = 4
EW = 2 * F
EC = EW // P
SCALE = HD ** -0.5
LN_EPS = 1e-5
HEAD_EPS = 1e-6
MASKED = -1e30
TABLES = "natural_log_exp_and_others"


def head_view(ap):
    return ap.rearrange("p (h d) -> p h d", d=HD)


def spread(ap, n):
    return ap.unsqueeze(2).to_broadcast([ap.shape[0], ap.shape[1], n])


class Sems:

    def __init__(self, nc, ctx, phase):
        self.nc, self.ctx, self.phase, self.made = nc, ctx, phase, {}

    def __getitem__(self, name):
        if name not in self.made:
            self.made[name] = self.ctx.enter_context(self.nc.semaphore(f"{self.phase}_{name}"))
        return self.made[name]


def transposes(pe, bank, src, ident, n=KD):
    for k in range(n):
        last = pe.transpose(bank[:, k * P:(k + 1) * P], src[:, k * P:(k + 1) * P], ident)
    return last


def product(pe, bank, lhs, rhs):
    n = rhs.shape[1]
    for k in range(n):
        last = pe.matmul(bank, lhs[:, k, :], rhs[:, k, :], start=(k == 0), stop=(k == n - 1))
    return last


def split_product(pe, bank, terms):
    todo = []
    for lhi, llo, rhi, rlo in terms:
        todo += [(lhi, rhi), (lhi, rlo), (llo, rhi)]
    for n, (lhs, rhs) in enumerate(todo):
        last = pe.matmul(bank, lhs, rhs, start=(n == 0), stop=(n == len(todo) - 1))
    return last


def rsqrt_seed(nc, act, seed, log, v, eps, done, count):
    nc.scalar.activation(log, v, ACT.Ln, bias=eps).then_inc(done, 1)
    act.wait_ge(done, count)
    return nc.scalar.activation(seed, log, ACT.Exp, scale=-0.5)


def rsqrt_refine(nc, dve, out, tmp, v, eps, seed, first, second, count):
    nc.vector.scalar_tensor_tensor(out=tmp, in0=v, scalar=eps, in1=seed, op0=ALU.add, op1=ALU.mult).then_inc(first, 1)
    dve.wait_ge(first, count)
    nc.vector.scalar_tensor_tensor(out=tmp, in0=tmp, scalar=-0.5, in1=seed, op0=ALU.mult, op1=ALU.mult).then_inc(second, 1)
    dve.wait_ge(second, count)
    return nc.vector.scalar_tensor_tensor(out=out, in0=tmp, scalar=1.5, in1=seed, op0=ALU.add, op1=ALU.mult)


def prepare(nc, io, g, psum):
    with ExitStack() as ctx:
        def sb(name, shape, dt=F32):
            return ctx.enter_context(nc.sbuf_tensor(name, shape, dt))

        s = Sems(nc, ctx, "prep")
        wk = sb("wk_raw", [P, KC, D])
        wv = sb("wv_raw", [P, KC, D])
        wkd = sb("wkd", [P, KC, D])
        wvd = sb("wvd", [P, KC, D])
        wq = sb("wq", [P, KD, D])
        yd = sb("yd", [P, KC, B * DCA])
        bq = sb("bq", [P, D])
        bkd = sb("bkd", [P, D])
        bvs = sb("bvs", [P, 2 * KD])
        bvt = sb("bvt", [P, KD])
        bvb = sb("bvb", [P, KD, P])
        wo_p = sb("wo_p", [P, KD, D])
        msum = sb("msum", [P, KD, H])
        st = sb("st", [P, NT, 6])
        mv = sb("mv", [P, NT, 2])
        rs = sb("rs", [P, NT])
        rlog = sb("rlog", [P, NT])
        rseed = sb("rseed", [P, NT])
        rtmp = sb("rtmp", [P, NT])
        qlog = sb("qlog", [P, 2, H])
        qseed = sb("qseed", [P, 2, H])
        qtmp = sb("qtmp", [P, 2, H])
        xn = sb("xn", [P, 2, D])
        xT = sb("xT", [P, 2, KD, P])
        qc = sb("qc", [P, 2, D])
        sq = sb("sq", [P, 2, D])
        ss = sb("ss", [P, 2, H])
        qr = sb("qr", [P, 2, H])
        qn = sb("qn", [P, 2, D])
        q32 = sb("q32", [P, 2, GROUPS, P])
        vd = sb("vd", [P, 2, D])

        NQ = NT + 2

        def done(i, u):
            return i * 2 + (u + 3)

        def before(i, u):
            return i * 2 + (u + 1)

        with nc.Block() as block:
            @block.sync
            def _(sp):
                sp.dma_start(g.x[:], io["x"].rearrange("(t p) d -> p t d", p=P)).then_inc(s["x"], 16)
                sp.dma_start(wq[:], io["wq"].rearrange("(k p) n -> p k n", p=P)).then_inc(s["wq"], 16)
                sp.dma_start(wkd[:], io["wkd"].rearrange("(k p) n -> p k n", p=P)).then_inc(s["wkd"], 16)
                sp.dma_start(wk[:], io["wk"].rearrange("(k p) n -> p k n", p=P)).then_inc(s["wk"], 16)
                sp.dma_start(wv[:], io["wv"].rearrange("(k p) n -> p k n", p=P)).then_inc(s["wv"], 16)
                for u in range(2):
                    sp.wait_ge(s["vd"], u + 1)
                    sp.dma_start(io["vd"][u * P:(u + 1) * P, :], vd[:, u, :]).then_inc(s["vd_out"], 16)
                sp.wait_ge(s["vd_out"], 32)

            @block.scalar
            def _(act):
                act.preload_act_table_set(TABLES)
                act.dma_start(g.ident[:], io["ident"]).then_inc(s["ident"], 16)
                act.dma_start(bq[:], io["bq"].partition_broadcast(P)).then_inc(s["bias"], 16)
                act.dma_start(bkd[:], io["bkd"].partition_broadcast(P)).then_inc(s["bias"], 16)
                act.dma_start(g.bk[:], io["bk"].partition_broadcast(P)).then_inc(s["bias"], 16)
                act.dma_start(g.cols[:], io["cols"]).then_inc(s["cols"], 16)
                act.dma_start(yd[:], io["yd"].rearrange("(k p) n -> p k n", p=P)).then_inc(s["yd"], 16)
                act.dma_start(wvd[:], io["wvd"].rearrange("(k p) n -> p k n", p=P)).then_inc(s["wvd"], 16)
                act.dma_start(bvs[:], io["bv"]).then_inc(s["bv"], 16)
                act.dma_start(wo_p[:], io["wo"].rearrange("k p n -> p k n")).then_inc(s["wo"], 16)
                act.dma_start(g.bo[:], io["bo"].partition_broadcast(P)).then_inc(s["bo"], 16)
                act.wait_ge(s["cols"], 16)
                for stage in ("xe", "qe", "qlog", "qseed"):
                    act.sem_inc(s[stage], 2)
                act.wait_ge(s["ba"], NT)
                rsqrt_seed(nc, act, rseed[:], rlog[:], mv[:, :, 1], g.cols[:, 9:10], s["rlog"], 1).then_inc(s["rseed"], 1)

                def evac_xT(i, u):
                    act.wait_ge(s["trx"], done(i, u))
                    act.wait_ge(s["qp"], before(i, u))
                    nc.scalar.copy(xT[:, u], psum[:, u, :].rearrange("p (k t) -> p k t", k=KD)).then_inc(s["xe"], 1)

                def evac_heads(i, u, w, b):
                    act.wait_ge(s["trq"], done(i, u))
                    act.wait_ge(s["qlo"], before(i, u))
                    nc.scalar.activation(q32[:, u], psum[:, 4 + u, :].rearrange("p (k t) -> p k t", k=GROUPS),
                                         ACT.Identity, scale=g.cols[:, w:w + 1], bias=g.cols[:, b:b + 1]).then_inc(s["qe"], 1)

                def seed(i, u):
                    act.wait_ge(s["qrd"], done(i, u))
                    act.wait_ge(s["qm"], before(i, u))
                    rsqrt_seed(nc, act, qseed[:, u], qlog[:, u], ss[:, u], g.cols[:, 8:9], s["qlog"],
                               done(i, u)).then_inc(s["qseed"], 1)

                with act.Fori(0, NT // 2) as i:
                    evac_xT(i, 0)
                    evac_xT(i, 1)
                    seed(i, 0)
                    seed(i, 1)
                    evac_heads(i, 0, 0, 1)
                    evac_heads(i, 1, 0, 1)
                for u in range(2):
                    seed(NT // 2, u)
                for u in range(2):
                    act.wait_ge(s["vdp"], u + 1)
                    nc.scalar.copy(vd[:, u, :], psum[:, 6 + u, :]).then_inc(s["vd"], 1)
                    evac_heads(NT // 2, u, 4, 5)

            @block.gpsimd
            def _(pool):
                pool.sem_inc(s["qsq"], 2)

                def square(i, u):
                    pool.wait_ge(s["qb"], done(i, u))
                    pool.wait_ge(s["qrd"], before(i, u))
                    nc.gpsimd.tensor_tensor(sq[:, u], qc[:, u], qc[:, u], ALU.mult).then_inc(s["qsq"], 1)

                with pool.Fori(0, NT // 2) as i:
                    square(i, 0)
                    square(i, 1)
                for u in range(2):
                    square(NT // 2, u)
                nc.gpsimd.memset(g.qbd_hi[:].bitcast(F32), 0.0)
                nc.gpsimd.memset(g.qbd_lo[:].bitcast(F32), 0.0)
                nc.gpsimd.memset(g.y_hi[:, 2].bitcast(F32), 0.0)
                nc.gpsimd.memset(g.y_lo[:, 2].bitcast(F32), 0.0)
                nc.gpsimd.memset(g.k_hi[:, 2].bitcast(F32), 0.0)
                nc.gpsimd.memset(g.k_lo[:, 2].bitcast(F32), 0.0)
                nc.gpsimd.memset(g.v[:], 1.0)
                nc.gpsimd.memset(g.ctx[:], 0.0)
                nc.gpsimd.memset(g.v_last[:], 0.0).then_inc(s["zero"], 1)
                pool.wait_ge(s["zero"], 1)
                pool.wait_ge(s["cols"], 16)
                for n, col in enumerate((PW - 1, 2 * PW - 1)):
                    nc.gpsimd.tensor_tensor(g.v_last[:, :, col], g.v_last[:, :, col],
                                            g.cols[:, 6 + n:7 + n].to_broadcast([P, PAIRS]), ALU.add)

            @block.vector
            def _(dve):
                chain = [0]

                def link(ins):
                    chain[0] += 1
                    ins.then_inc(s["chain"], 1)
                    dve.wait_ge(s["chain"], chain[0])

                for stage in ("xn", "qb", "qrd", "qn1", "qn2", "qrs", "qm", "qhi", "qlo"):
                    dve.sem_inc(s[stage], 2)
                dve.wait_ge(s["x"], 16)
                for t in range(NT):
                    nc.vector.bn_stats(st[:, t, :], g.x[:, t, :]).then_inc(s["bs"], 1)
                for t in range(NT):
                    dve.wait_ge(s["bs"], t + 1)
                    nc.vector.bn_aggr(mv[:, t, :], st[:, t, :]).then_inc(s["ba"], 1)

                def center(w):
                    rows, n = w.shape[0], w.shape[1] // HD
                    sums = msum[:].rearrange("p k h -> p (k h)")[0:rows, 0:n]
                    link(nc.vector.tensor_reduce(sums, head_view(w), AX_X, ALU.add))
                    link(nc.vector.scalar_tensor_tensor(out=head_view(w), in0=spread(sums, HD), scalar=-1.0 / HD,
                                                        in1=head_view(w), op0=ALU.mult, op1=ALU.add))

                def split(hi, lo, w):
                    link(nc.vector.tensor_copy(hi, w))
                    nc.vector.tensor_tensor(lo, w, hi.bitcast(F32), ALU.subtract)

                dve.wait_ge(s["bias"], 48)
                center(bq[:])
                center(bkd[:])
                center(g.bk[:])
                dve.wait_ge(s["wq"], 16)
                center(wq[:].rearrange("p k n -> p (k n)"))
                dve.sem_inc(s["wq_c"], 1)

                def normalise_x(i, u):
                    if isinstance(i, int) is False:
                        dve.wait_ge(s["trx"], before(i, u))
                    nc.vector.tensor_scalar(xn[:, u], g.x[:, i * 2 + u, :], mv[:, i * 2 + u, 0:1],
                                            rs_col(i * 2 + u), ALU.subtract, ALU.mult).then_inc(s["xn"], 1)

                def rs_col(t):
                    return rs[:].unsqueeze(2)[:, t, :]

                def bias(i, u, b):
                    dve.wait_ge(s["qp"], done(i, u))
                    dve.wait_ge(s["qm"], before(i, u))
                    nc.vector.tensor_tensor(qc[:, u], psum[:, 2 + u, :], b, ALU.add).then_inc(s["qb"], 1)

                def reduce(i, u):
                    dve.wait_ge(s["qsq"], done(i, u))
                    dve.wait_ge(s["qrs"], before(i, u))
                    nc.vector.tensor_reduce(ss[:, u], head_view(sq[:, u]), AX_X, ALU.add).then_inc(s["qrd"], 1)

                def scale_heads(i, u):
                    dve.wait_ge(s["qseed"], done(i, u))
                    rsqrt_refine(nc, dve, qr[:, u], qtmp[:, u], ss[:, u], HD * HEAD_EPS, qseed[:, u],
                                 s["qn1"], s["qn2"], done(i, u)).then_inc(s["qrs"], 1)
                    dve.wait_ge(s["qrs"], done(i, u))
                    dve.wait_ge(s["trq"], before(i, u))
                    nc.vector.scalar_tensor_tensor(out=head_view(qn[:, u]), in0=head_view(qc[:, u]), scalar=HD ** 0.5,
                                                   in1=spread(qr[:, u], HD), op0=ALU.mult, op1=ALU.mult).then_inc(s["qm"], 1)

                def split_heads(i, u, hi, lo):
                    dve.wait_ge(s["qe"], done(i, u))
                    nc.vector.tensor_copy(hi, q32[:, u]).then_inc(s["qhi"], 1)
                    dve.wait_ge(s["qhi"], done(i, u))
                    nc.vector.tensor_tensor(lo, q32[:, u], hi.bitcast(F32), ALU.subtract).then_inc(s["qlo"], 1)

                dve.wait_ge(s["rseed"], 1)
                link(rsqrt_refine(nc, dve, rs[:], rtmp[:], mv[:, :, 1], LN_EPS, rseed[:], s["rn1"], s["rn2"], 1))
                with dve.Fori(0, NT // 2) as i:
                    normalise_x(i, 0)
                    normalise_x(i, 1)
                    for stage in (bias, reduce, scale_heads):
                        for u in range(2):
                            stage(i, u, *([bq[:]] if stage is bias else []))
                    for u in range(2):
                        at = (i * 2 + u) * P
                        split_heads(i, u, g.q_hi[:, :, bass.ds(at, P)], g.q_lo[:, :, bass.ds(at, P)])
                dve.wait_ge(s["wkd"], 16)
                center(wkd[:].rearrange("p k n -> p (k n)"))
                dve.sem_inc(s["wkd_c"], 1)
                for stage in (bias, reduce, scale_heads):
                    for u in range(2):
                        stage(NT // 2, u, *([bkd[:]] if stage is bias else []))
                for u in range(2):
                    split_heads(NT // 2, u, g.kd_hi[:, :, u * P:(u + 1) * P], g.kd_lo[:, :, u * P:(u + 1) * P])
                dve.wait_ge(s["wk"], 16)
                center(wk[:].rearrange("p k n -> p (k n)"))
                split(g.wk_hi[:], g.wk_lo[:], wk[:])
                dve.wait_ge(s["wv"], 16)
                split(g.wv_hi[:], g.wv_lo[:], wv[:])
                dve.wait_ge(s["bv"], 16)
                link(nc.vector.tensor_tensor(bvt[:], bvs[:, 0:KD], bvs[:, KD:2 * KD], ALU.add))
                nc.vector.tensor_copy(bvb[:], spread(bvt[:], P)).then_inc(s["bvb"], 1)
                dve.wait_ge(s["bop"], 1)
                dve.wait_ge(s["bo"], 16)
                nc.vector.tensor_tensor(g.bo[:], g.bo[:], psum[:, 0, :], ALU.add)

            @block.tensor
            def _(pe):
                for stage in ("trx", "qp", "trq"):
                    pe.sem_inc(s[stage], 2)
                pe.wait_ge(s["ident"], 16)

                def turn_x(i, u):
                    pe.wait_ge(s["xn"], done(i, u))
                    pe.wait_ge(s["xe"], before(i, u))
                    transposes(pe, psum[:, u, :], xn[:, u, :], g.ident[:]).then_inc(s["trx"], 1)

                def project(i, u):
                    pe.wait_ge(s["xe"], done(i, u))
                    pe.wait_ge(s["qb"], before(i, u))
                    product(pe, psum[:, 2 + u, :], xT[:, u], wq[:]).then_inc(s["qp"], 1)

                def turn_heads(i, u):
                    pe.wait_ge(s["qm"], done(i, u))
                    pe.wait_ge(s["qe"], before(i, u))
                    transposes(pe, psum[:, 4 + u, :], qn[:, u, :], g.ident[:]).then_inc(s["trq"], 1)

                pe.wait_ge(s["wq_c"], 1)
                with pe.Fori(0, NT // 2) as i:
                    for stage in (turn_x, project, turn_heads):
                        for u in range(2):
                            stage(i, u)
                pe.wait_ge(s["yd"], 16)
                pe.wait_ge(s["wvd"], 16)
                pe.wait_ge(s["wkd_c"], 1)
                i = NT // 2
                for u in range(2):
                    pe.wait_ge(s["qb"], before(i, u))
                    product(pe, psum[:, 2 + u, :], yd[:, :, u * P:(u + 1) * P], wkd[:]).then_inc(s["qp"], 1)
                for u in range(2):
                    product(pe, psum[:, 6 + u, :], yd[:, :, u * P:(u + 1) * P], wvd[:]).then_inc(s["vdp"], 1)
                for u in range(2):
                    turn_heads(i, u)
                pe.wait_ge(s["bvb"], 1)
                pe.wait_ge(s["wo"], 16)
                pe.wait_ge(s["xe"], done(NT // 2 - 1, 1))
                product(pe, psum[:, 0, :], bvb[:], wo_p[:]).then_inc(s["bop"], 1)


def cross_attention(nc, io, g, psum):
    K_BANK, V_BANK, TR_BANK, S_BANK, O_BANK = 0, 1, 2, 3, 5
    LANDING = ((0, 4), (4, 8), (8, CH))

    with ExitStack() as ctx:
        def sb(name, shape, dt=F32):
            return ctx.enter_context(nc.sbuf_tensor(name, shape, dt))

        s = Sems(nc, ctx, "xa")
        y = sb("y", [P, KC, SM])
        kc = sb("kc", [P, 3, D])
        sq = sb("ksq", [P, 3, D])
        ss = sb("kss", [P, 3, H])
        kr = sb("kr", [P, 3, H])
        klog = sb("klog", [P, 3, H])
        kseed = sb("kseed", [P, 3, H])
        ktmp = sb("ktmp", [P, 3, H])
        kn = sb("kn", [P, 3, D])
        k32 = sb("k32", [P, 3, GROUPS, P])
        probs = sb("probs", [P, 3, H * SQ])
        o_sb = sb("o_sb", [P, PAIRS, 2 * PW])
        rinv = sb("rinv", [P, PAIRS, 2])
        od = sb("od", [P, PAIRS, HD])

        def buf(c):
            return 2 if c == LAST else c % 2

        def at(b, c):
            return (b, c) if c < CH else (b + 1, c - CH)

        def done(b, c):
            return b * CH + (CH + c + 1)

        def before(b, c):
            return done(b, c - CH if c == LAST else c - 2 if c >= 2 else c - 3)

        def batches(eng, body):
            with eng.Fori(0, B - 1) as b:
                body(b, CH)
            body(B - 1, 0)

        def ahead(c, n, room):
            return c + n < CH + room

        o_bank = [psum[:, O_BANK + p // 3, (p % 3) * 2 * PW:(p % 3 + 1) * 2 * PW] for p in range(PAIRS)]

        with nc.Block() as block:
            @block.sync
            def _(sp):
                with sp.Fori(0, B) as b:
                    for n, (lo, hi) in enumerate(LANDING):
                        end = min(hi * P, SM)
                        sp.wait_ge(s["yhi"], done(b, hi - 1 - CH))
                        sp.wait_ge(s["ylo"], done(b, hi - 1 - CH))
                        sp.dma_start(y[:, :, lo * P:end],
                                     io["y"][b].rearrange("(k p) t -> p k t", p=P)[:, :, lo * P:end])\
                            .then_inc(s[f"y{n}"], 16)
                    sp.wait_ge(s["pv"], done(b, -1))
                    sp.dma_start(g.v_last[DCA_ROW:DCA_ROW + DCA, :, PW:2 * PW - 1],
                                 io["vd"][bass.ds(b * DCA, DCA), :].rearrange("t (p n) -> t p n", p=PAIRS))\
                        .then_inc(s["vd"], 16)

            @block.scalar
            def _(act):
                act.preload_act_table_set(TABLES)
                for stage in ("yhi", "ke", "ve", "ex", "klog", "kseed"):
                    act.sem_inc(s[stage], CH)
                act.sem_inc(s["oe"], 1)

                def y_high(b, c):
                    b, c = at(b, c)
                    n = next(n for n, (lo, hi) in enumerate(LANDING) if lo <= c < hi)
                    w = min(P, SM - c * P)
                    act.wait_ge(s[f"y{n}"], b * 16 + 16)
                    act.wait_ge(s["vp"], before(b, c))
                    nc.scalar.copy(g.y_hi[:, buf(c), :, 0:w], y[:, :, c * P:c * P + w]).then_inc(s["yhi"], 1)

                def k_evac(b, c):
                    b, c = at(b, c)
                    w = DCA_ROW if c == LAST else P
                    act.wait_ge(s["tr"], done(b, c))
                    act.wait_ge(s["klo"], before(b, c))
                    nc.scalar.activation(k32[:, buf(c), :, 0:w],
                                         psum[:, TR_BANK, :].rearrange("p (g t) -> p g t", g=GROUPS)[:, :, 0:w],
                                         ACT.Identity, scale=g.cols[:, 2:3], bias=g.cols[:, 3:4]).then_inc(s["ke"], 1)

                def v_evac(b, c):
                    b, c = at(b, c)
                    bank = psum[:, V_BANK, :].rearrange("p (q n) -> p q n", q=PAIRS)
                    act.wait_ge(s["vp"], done(b, c))
                    act.wait_ge(s["pv"], before(b, c))
                    if c == LAST:
                        nc.scalar.copy(g.v_last[0:DCA_ROW, :, 0:PW - 1], bank[0:DCA_ROW]).then_inc(s["ve"], 1)
                    else:
                        nc.scalar.copy(g.v[:, buf(c), :, 0:PW - 1], bank).then_inc(s["ve"], 1)

                def seed(b, c):
                    b, c = at(b, c)
                    act.wait_ge(s["krd"], done(b, c))
                    act.wait_ge(s["krs"], before(b, c))
                    rsqrt_seed(nc, act, kseed[:, buf(c)], klog[:, buf(c)], ss[:, buf(c)], g.cols[:, 8:9], s["klog"],
                               done(b, c)).then_inc(s["kseed"], 1)

                def exps(b, c):
                    b, c = at(b, c)
                    act.wait_ge(s["sc"], done(b, c))
                    act.wait_ge(s["pv"], before(b, c))
                    nc.scalar.activation(probs[:, buf(c), :], psum[:, S_BANK:S_BANK + 2, :].rearrange("p a n -> p (a n)"),
                                         ACT.Exp, scale=SCALE).then_inc(s["ex"], 1)

                def o_evac(b):
                    act.wait_ge(s["pv"], done(b, LAST))
                    act.wait_ge(s["on"], b * 1 + 1)
                    for bank, (lo, hi) in enumerate(((0, 3), (3, 6), (6, PAIRS))):
                        last = nc.scalar.copy(o_sb[:, lo:hi, :],
                                              psum[:, O_BANK + bank, 0:(hi - lo) * 2 * PW]
                                              .rearrange("p (q n) -> p q n", n=2 * PW))
                    last.then_inc(s["oe"], 1)

                def ctx_evac(b):
                    act.wait_ge(s["ct"], b + 1)
                    nc.scalar.copy(g.ctxT[:, :, :, bass.ds(b * SQ, SQ)],
                                   psum[:, TR_BANK, 0:2 * P].rearrange("p (g j q) -> p g j q", g=2, j=2)).then_inc(s["ce"], 1)

                y_high(0, 0)
                y_high(0, 1)
                y_high(0, 2)
                v_evac(0, 0)
                seed(0, 0)
                k_evac(0, 0)
                v_evac(0, 1)
                seed(0, 1)
                exps(0, 0)

                def steps(b, room):
                    for c in range(CH):
                        if ahead(c, 3, room):
                            y_high(b, c + 3)
                        if ahead(c, 1, room):
                            k_evac(b, c + 1)
                        if ahead(c, 2, room):
                            v_evac(b, c + 2)
                            seed(b, c + 2)
                        if c == LAST:
                            o_evac(b)
                        if ahead(c, 1, room):
                            exps(b, c + 1)
                        if c == 2:
                            ctx_evac(b)

                batches(act, steps)
                ctx_evac(B)

            @block.gpsimd
            def _(pool):
                for stage in ("ylo", "ksq"):
                    pool.sem_inc(s[stage], CH)
                pool.sem_inc(s["on"], 1)

                def y_low(b, c):
                    b, c = at(b, c)
                    w = min(P, SM - c * P)
                    pool.wait_ge(s["yhi"], done(b, c))
                    pool.wait_ge(s["vp"], before(b, c))
                    nc.gpsimd.tensor_tensor(g.y_lo[:, buf(c), :, 0:w], y[:, :, c * P:c * P + w],
                                            g.y_hi[:, buf(c), :, 0:w].bitcast(F32), ALU.subtract).then_inc(s["ylo"], 1)

                def square(b, c):
                    b, c = at(b, c)
                    pool.wait_ge(s["kb"], done(b, c))
                    pool.wait_ge(s["krd"], before(b, c))
                    nc.gpsimd.tensor_tensor(sq[:, buf(c)], kc[:, buf(c)], kc[:, buf(c)], ALU.mult).then_inc(s["ksq"], 1)

                def normalise(b):
                    pool.wait_ge(s["rc"], b + 1)
                    pool.wait_ge(s["ct"], b + 1)
                    for j in range(2):
                        rows = slice(j * SQ, (j + 1) * SQ)
                        for n, dst in enumerate((g.ctx, od)):
                            nc.gpsimd.tensor_tensor(dst[rows], o_sb[rows, :, n * PW + j * HD:n * PW + (j + 1) * HD],
                                                    rinv[rows, :, n:n + 1].to_broadcast([SQ, PAIRS, HD]),
                                                    ALU.mult).then_inc(s["onp"], 1)
                    pool.wait_ge(s["onp"], b * 4 + 4)
                    nc.gpsimd.tensor_tensor(g.ctx[:], g.ctx[:], od[:], ALU.add).then_inc(s["on"], 1)

                y_low(0, 0)
                y_low(0, 1)
                square(0, 0)
                y_low(0, 2)
                square(0, 1)

                def steps(b, room):
                    for c in range(CH):
                        if ahead(c, 3, room):
                            y_low(b, c + 3)
                        if ahead(c, 2, room):
                            square(b, c + 2)
                        if c == LAST:
                            normalise(b)

                batches(pool, steps)

            @block.vector
            def _(dve):
                for stage in ("kb", "krd", "kn1", "kn2", "krs", "km", "khi", "klo"):
                    dve.sem_inc(s[stage], CH)

                def k_bias(b, c):
                    b, c = at(b, c)
                    dve.wait_ge(s["kp"], done(b, c))
                    dve.wait_ge(s["km"], before(b, c))
                    nc.vector.tensor_tensor(kc[:, buf(c)], psum[:, K_BANK, :], g.bk[:], ALU.add).then_inc(s["kb"], 1)

                def k_reduce(b, c):
                    b, c = at(b, c)
                    dve.wait_ge(s["ksq"], done(b, c))
                    dve.wait_ge(s["krs"], before(b, c))
                    nc.vector.tensor_reduce(ss[:, buf(c)], head_view(sq[:, buf(c)]), AX_X, ALU.add).then_inc(s["krd"], 1)

                def k_norm(b, c):
                    b, c = at(b, c)
                    dve.wait_ge(s["kseed"], done(b, c))
                    rsqrt_refine(nc, dve, kr[:, buf(c)], ktmp[:, buf(c)], ss[:, buf(c)], HD * HEAD_EPS, kseed[:, buf(c)],
                                 s["kn1"], s["kn2"], done(b, c)).then_inc(s["krs"], 1)
                    dve.wait_ge(s["krs"], done(b, c))
                    dve.wait_ge(s["tr"], before(b, c))
                    nc.vector.scalar_tensor_tensor(out=head_view(kn[:, buf(c)]), in0=head_view(kc[:, buf(c)]),
                                                   scalar=HD ** 0.5, in1=spread(kr[:, buf(c)], HD),
                                                   op0=ALU.mult, op1=ALU.mult).then_inc(s["km"], 1)

                def k_split(b, c):
                    b, c = at(b, c)
                    w = DCA_ROW if c == LAST else P
                    src = k32[:, buf(c), :, 0:w]
                    hi, lo = g.k_hi[:, buf(c), :, 0:w], g.k_lo[:, buf(c), :, 0:w]
                    dve.wait_ge(s["ke"], done(b, c))
                    dve.wait_ge(s["sc"], before(b, c))
                    nc.vector.tensor_copy(hi, src).then_inc(s["khi"], 1)
                    dve.wait_ge(s["khi"], done(b, c))
                    nc.vector.tensor_tensor(lo, src, hi.bitcast(F32), ALU.subtract).then_inc(s["klo"], 1)

                def queries(b):
                    dve.wait_ge(s["sc"], done(b, -1))
                    for qbd, q in ((g.qbd_hi, g.q_hi), (g.qbd_lo, g.q_lo)):
                        for i in range(4):
                            rows = slice(i * HD, (i + 1) * HD)
                            nc.vector.tensor_copy(qbd[rows, :, i * SQ:(i + 1) * SQ],
                                                  q[rows, :, bass.ds(b * SQ, SQ)]).then_inc(s["qb"], 1)

                def second_keys(b):
                    dve.wait_ge(s["sc"], done(b, -1))
                    for k, kd in ((g.k_hi, g.kd_hi), (g.k_lo, g.kd_lo)):
                        nc.vector.tensor_copy(k[:, 2, :, DCA_ROW:DCA_ROW + DCA],
                                              kd[:, :, bass.ds(b * DCA, DCA)]).then_inc(s["kd"], 1)

                queries(0)
                k_bias(0, 0)
                k_reduce(0, 0)
                k_norm(0, 0)
                k_bias(0, 1)
                k_split(0, 0)
                k_reduce(0, 1)
                k_norm(0, 1)

                def steps(b, room):
                    for c in range(CH):
                        if c == LAST and room:
                            queries(b + 1)
                        if ahead(c, 2, room):
                            k_bias(b, c + 2)
                        if ahead(c, 1, room):
                            k_split(b, c + 1)
                        if ahead(c, 2, room):
                            k_reduce(b, c + 2)
                            k_norm(b, c + 2)
                        if c == 5:
                            second_keys(b)
                        if c == LAST:
                            dve.wait_ge(s["oe"], b + 2)
                            nc.vector.reciprocal(rinv[:], o_sb[:, :, PW - 1:2 * PW:PW]).then_inc(s["rc"], 1)

                batches(dve, steps)

            @block.tensor
            def _(pe):
                for stage in ("kp", "vp", "tr", "sc", "pv"):
                    pe.sem_inc(s[stage], CH)

                def project(b, c, bank, w_hi, w_lo, free, stage):
                    b, c = at(b, c)
                    pe.wait_ge(s["yhi"], done(b, c))
                    pe.wait_ge(s["ylo"], done(b, c))
                    pe.wait_ge(s[free], done(b, c - 1))
                    split_product(pe, psum[:, bank, :],
                                  [(g.y_hi[:, buf(c), k, :], g.y_lo[:, buf(c), k, :], w_hi[:, k, :], w_lo[:, k, :])
                                   for k in range(KC)]).then_inc(s[stage], 1)

                def keys(b, c):
                    project(b, c, K_BANK, g.wk_hi, g.wk_lo, "kb", "kp")

                def values(b, c):
                    project(b, c, V_BANK, g.wv_hi, g.wv_lo, "ve", "vp")

                def turn(b, c):
                    b, c = at(b, c)
                    pe.wait_ge(s["km"], done(b, c))
                    pe.wait_ge(s["ke"], done(b, c - 1))
                    if c == 4:
                        pe.wait_ge(s["ce"], b + 1)
                    transposes(pe, psum[:, TR_BANK, :], kn[:, buf(c), :], g.ident[:]).then_inc(s["tr"], 1)

                def scores(b, c):
                    b, c = at(b, c)
                    pe.wait_ge(s["khi"], done(b, c))
                    pe.wait_ge(s["klo"], done(b, c))
                    pe.wait_ge(s["ex"], done(b, c - 1))
                    if c == 0:
                        pe.wait_ge(s["qb"], b * 8 + 8)
                    if c == LAST:
                        pe.wait_ge(s["kd"], b * 2 + 2)
                    for n in range(GROUPS):
                        out = psum[:, S_BANK + n // 2, (n % 2) * 4 * SQ:(n % 2 + 1) * 4 * SQ]
                        last = split_product(pe, out, [(g.k_hi[:, buf(c), n, :], g.k_lo[:, buf(c), n, :],
                                                        g.qbd_hi[:, n, :], g.qbd_lo[:, n, :])])
                    last.then_inc(s["sc"], 1)

                def weighted(b, c):
                    pe.wait_ge(s["ex"], done(b, c))
                    pe.wait_ge(s["ve"], done(b, c))
                    if c == 0:
                        pe.wait_ge(s["oe"], b + 1)
                    if c == LAST:
                        pe.wait_ge(s["vd"], b * 16 + 16)
                    for p in range(PAIRS):
                        v = g.v_last[:, p, :] if c == LAST else g.v[:, buf(c), p, :]
                        last = pe.matmul(o_bank[p][:, 0:v.shape[1]], probs[:, buf(c), p * P:(p + 1) * P], v,
                                         start=(c == 0 and p % 3 == 0), stop=(c == LAST), skip_group_check=True)
                    last.then_inc(s["pv"], 1)

                def turn_ctx(b):
                    pe.wait_ge(s["on"], b + 1)
                    if isinstance(b, int) and b == B:
                        pe.wait_ge(s["ke"], done(B - 1, LAST))
                    else:
                        pe.wait_ge(s["ke"], done(b, 3))
                    transposes(pe, psum[:, TR_BANK, :], g.ctx[:].rearrange("p q d -> p (q d)"), g.ident[:],
                               2).then_inc(s["ct"], 1)

                keys(0, 0)
                values(0, 0)
                keys(0, 1)
                turn(0, 0)
                values(0, 1)
                scores(0, 0)

                def steps(b, room):
                    for c in range(CH):
                        if ahead(c, 2, room):
                            keys(b, c + 2)
                        if ahead(c, 1, room):
                            turn(b, c + 1)
                        if ahead(c, 2, room):
                            values(b, c + 2)
                        weighted(b, c)
                        if ahead(c, 1, room):
                            scores(b, c + 1)
                        if c == 2:
                            turn_ctx(b)

                batches(pe, steps)
                turn_ctx(B)


def self_attention(nc, io, g, psum):
    VW = HD + 1
    OP, TR, QB, KB, SB, PB = 0, 1, 2, 3, 4, 6

    with ExitStack() as ctx:
        def sb(name, shape, dt=F32):
            return ctx.enter_context(nc.sbuf_tensor(name, shape, dt))

        s = Sems(nc, ctx, "sa")
        wo = sb("xa_wo", [P, KD, D])
        wq = sb("sa_wq", [P, KD, D])
        wk = sb("sa_wk", [P, KD, D])
        wv = sb("sa_wv", [P, KD, P])
        wo2 = sb("sa_wo", [P, KD, D])
        mask = sb("mask", [P, SQ])
        cx = sb("cx", [P, 2, KD, P])
        t1 = sb("t1", [P, 2, D])
        st = sb("sa_st", [P, 2, 6])
        mv = sb("sa_mv", [P, 2, 2])
        rs = sb("sa_rs", [P, 2, 1])
        rlog = sb("sa_rlog", [P, 2, 1])
        rseed = sb("sa_rseed", [P, 2, 1])
        rtmp = sb("sa_rtmp", [P, 2, 1])
        xn = sb("sa_xn", [P, 2, D])
        xT = sb("sa_xT", [P, 2, KD, P])
        qT = sb("sa_qT", [P, 2, GROUPS, P])
        kT = sb("sa_kT", [P, 2, KV, 2, 4, SQ])
        vv = sb("sa_v", [P, 2, KV, VW])
        sm = sb("sa_s", [P, 2, H, SQ])
        mx = sb("sa_mx", [P, 2, H])
        pr = sb("sa_p", [P, 2, H, P])
        pT = sb("sa_pT", [P, 2, H, P])
        ri = sb("sa_ri", [P, 2, H])
        co = sb("sa_o", [P, 2, D])
        cT = sb("sa_oT", [P, 2, KD, P])

        def done(i, u):
            return i * 2 + (u + 3)

        def before(i, u):
            return i * 2 + (u + 1)

        def last_one(i, u):
            return i * 2 + (u + 2)

        with nc.Block() as block:
            @block.sync
            def _(sp):
                for name, dst, src in (("wo", wo, io["wo"].rearrange("k p n -> p k n")),
                                       ("wq", wq, io["sa_wq"].rearrange("(k p) n -> p k n", p=P)),
                                       ("wk", wk, io["sa_wk"].rearrange("(k p) n -> p k n", p=P)),
                                       ("wv", wv, io["sa_wv"].rearrange("(k p) n -> p k n", p=P)),
                                       ("mask", mask, io["mask"]),
                                       ("wo2", wo2, io["sa_wo"].rearrange("(k p) n -> p k n", p=P))):
                    sp.dma_start(dst[:], src).then_inc(s[name], 16)

            @block.gpsimd
            def _(pool):
                nc.gpsimd.memset(vv[:], 1.0).then_inc(s["set"], 1)
                nc.gpsimd.memset(pr[:], 0.0).then_inc(s["set"], 1)
                nc.gpsimd.memset(kT[:], 0.0).then_inc(s["set"], 1)

            @block.scalar
            def _(act):
                act.preload_act_table_set(TABLES)
                for stage in ("cx", "xe", "qe", "ve", "ex", "pe0", "pe1", "pe2", "pe3", "cte", "rlog", "rseed"):
                    act.sem_inc(s[stage], 2)
                act.wait_ge(s["set"], 3)

                def ctx_chunk(i, u):
                    act.wait_ge(s["op"], before(i, u))
                    nc.scalar.copy(cx[:, u].rearrange("p (g j) t -> p g j t", g=2),
                                   g.ctxT[:, :, :, bass.ds((i * 2 + u) * P + SQ, P)]).then_inc(s["cx"], 1)

                def seed(i, u):
                    act.wait_ge(s["ba"], done(i, u))
                    act.wait_ge(s["rs"], before(i, u))
                    rsqrt_seed(nc, act, rseed[:, u], rlog[:, u], mv[:, u, 1:2], g.cols[:, 9:10], s["rlog"],
                               done(i, u)).then_inc(s["rseed"], 1)

                def x_evac(i, u):
                    act.wait_ge(s["trx"], done(i, u))
                    act.wait_ge(s["vp"], before(i, u))
                    nc.scalar.copy(xT[:, u], psum[:, TR, :].rearrange("p (k t) -> p k t", k=KD)).then_inc(s["xe"], 1)

                def qv_evac(i, u):
                    act.wait_ge(s["qp"], done(i, u))
                    act.wait_ge(s["sp"], before(i, u))
                    nc.scalar.copy(qT[:, u], psum[:, QB, :].rearrange("p (g t) -> p g t", g=GROUPS)).then_inc(s["qe"], 1)
                    act.wait_ge(s["vp"], done(i, u))
                    act.wait_ge(s["pv"], before(i, u))
                    nc.scalar.copy(vv[:, u, :, 0:HD], psum[:, OP, 0:P].rearrange("p (h d) -> p h d", h=KV)).then_inc(s["ve"], 1)

                def exps(i, u):
                    act.wait_ge(s["sb"], done(i, u))
                    act.wait_ge(s["pt3"], before(i, u))
                    for j in range(2):
                        rows = slice(j * SQ, (j + 1) * SQ)
                        last = nc.scalar.activation(pr[rows, u, :, rows], sm[rows, u], ACT.Exp)
                    last.then_inc(s["ex"], 1)

                def p_evac(i, u, n):
                    act.wait_ge(s[f"pt{n}"], done(i, u))
                    act.wait_ge(s["pv"], before(i, u))
                    nc.scalar.copy(pT[:, u, 4 * n:4 * n + 4, :],
                                   psum[:, (QB, KB)[n % 2], :].rearrange("p (h t) -> p h t", h=4)).then_inc(s[f"pe{n}"], 1)

                def o_evac(i, u):
                    act.wait_ge(s["trc"], done(i, u))
                    act.wait_ge(s["op2"], before(i, u))
                    nc.scalar.copy(cT[:, u], psum[:, TR, :].rearrange("p (k t) -> p k t", k=KD)).then_inc(s["cte"], 1)

                with act.Fori(0, NT // 2) as i:
                    for u in range(2):
                        ctx_chunk(i, u)
                    for u in range(2):
                        seed(i, u)
                    for u in range(2):
                        x_evac(i, u)
                    for u in range(2):
                        qv_evac(i, u)
                    for u in range(2):
                        exps(i, u)
                        for n in range(4):
                            p_evac(i, u, n)
                    for u in range(2):
                        o_evac(i, u)

            @block.vector
            def _(dve):
                for stage in ("tp", "x1", "bs", "ba", "rn1", "rn2", "rs", "xn", "ke", "sm", "mx", "sb", "ri", "co", "x2"):
                    dve.sem_inc(s[stage], 2)
                dve.wait_ge(s["mask"], 16)
                dve.wait_ge(s["set"], 3)

                def residual(i, u):
                    dve.wait_ge(s["op"], done(i, u))
                    dve.wait_ge(s["x1"], before(i, u))
                    nc.vector.tensor_tensor(t1[:, u], psum[:, OP, :], g.bo[:], ALU.add).then_inc(s["tp"], 1)
                    dve.wait_ge(s["tp"], done(i, u))
                    x = g.x[:, i * 2 + u, :]
                    nc.vector.tensor_tensor(x, x, t1[:, u], ALU.add).then_inc(s["x1"], 1)

                def stats(i, u):
                    dve.wait_ge(s["x1"], done(i, u))
                    dve.wait_ge(s["ba"], before(i, u))
                    dve.sem_inc(s["gate"], 1)
                    nc.vector.bn_stats(st[:, u], g.x[:, i * 2 + u, :]).then_inc(s["bs"], 1)
                    dve.wait_ge(s["bs"], done(i, u))
                    dve.wait_ge(s["xn"], before(i, u))
                    dve.sem_inc(s["gate"], 1)
                    nc.vector.bn_aggr(mv[:, u], st[:, u]).then_inc(s["ba"], 1)

                def norm(i, u):
                    dve.wait_ge(s["rseed"], done(i, u))
                    rsqrt_refine(nc, dve, rs[:, u], rtmp[:, u], mv[:, u, 1:2], LN_EPS, rseed[:, u],
                                 s["rn1"], s["rn2"], done(i, u)).then_inc(s["rs"], 1)
                    dve.wait_ge(s["rs"], done(i, u))
                    dve.wait_ge(s["trx"], before(i, u))
                    nc.vector.tensor_scalar(xn[:, u], g.x[:, i * 2 + u, :], mv[:, u, 0:1], rs[:, u],
                                            ALU.subtract, ALU.mult).then_inc(s["xn"], 1)

                def keys(i, u):
                    dve.wait_ge(s["kp"], done(i, u))
                    dve.wait_ge(s["sp"], before(i, u))
                    bank = psum[:, KB, :].rearrange("p (h b t) -> p h b t", h=KV, b=2)
                    for n in range(4):
                        rows = slice(n * HD, (n + 1) * HD)
                        last = nc.vector.tensor_copy(kT[rows, u, :, :, n, :], bank[rows])
                    last.then_inc(s["ke"], 1)

                def softmax(i, u):
                    dve.wait_ge(s["sp"], done(i, u))
                    dve.wait_ge(s["ex"], before(i, u))
                    nc.vector.scalar_tensor_tensor(
                        out=sm[:, u], in0=psum[:, SB:SB + 2, :].rearrange("p a (h t) -> p (a h) t", t=SQ), scalar=SCALE,
                        in1=mask[:].unsqueeze(1).to_broadcast([P, H, SQ]), op0=ALU.mult, op1=ALU.add).then_inc(s["sm"], 1)
                    dve.wait_ge(s["sm"], done(i, u))
                    dve.wait_ge(s["sb"], before(i, u))
                    nc.vector.tensor_reduce(mx[:, u], sm[:, u], AX_X, ALU.max).then_inc(s["mx"], 1)
                    dve.wait_ge(s["mx"], done(i, u))
                    nc.vector.tensor_tensor(sm[:, u], sm[:, u], spread(mx[:, u], SQ), ALU.subtract).then_inc(s["sb"], 1)

                def normalise(i, u):
                    dve.wait_ge(s["pv"], done(i, u))
                    dve.wait_ge(s["co"], before(i, u))
                    for a in range(2):
                        bank = psum[:, PB + a, 0:8 * VW].rearrange("p (h n) -> p h n", n=VW)
                        last = nc.vector.reciprocal(ri[:, u, 8 * a:8 * a + 8], bank[:, :, HD])
                    last.then_inc(s["ri"], 1)
                    dve.wait_ge(s["ri"], done(i, u))
                    dve.wait_ge(s["trc"], before(i, u))
                    for a in range(2):
                        bank = psum[:, PB + a, 0:8 * VW].rearrange("p (h n) -> p h n", n=VW)
                        last = nc.vector.tensor_tensor(head_view(co[:, u])[:, 8 * a:8 * a + 8, :], bank[:, :, 0:HD],
                                                       spread(ri[:, u, 8 * a:8 * a + 8], HD), ALU.mult)
                    last.then_inc(s["co"], 1)

                def residual2(i, u):
                    dve.wait_ge(s["op2"], done(i, u))
                    x = g.x[:, i * 2 + u, :]
                    nc.vector.tensor_tensor(x, x, psum[:, OP, :], ALU.add).then_inc(s["x2"], 1)

                with dve.Fori(0, NT // 2) as i:
                    for u in range(2):
                        residual(i, u)
                    for u in range(2):
                        stats(i, u)
                    for u in range(2):
                        norm(i, u)
                    for u in range(2):
                        keys(i, u)
                        softmax(i, u)
                    for u in range(2):
                        normalise(i, u)
                    for u in range(2):
                        residual2(i, u)

            @block.tensor
            def _(pe):
                for stage in ("op", "trx", "qp", "kp", "vp", "sp", "pt0", "pt1", "pt2", "pt3", "pv", "trc", "op2"):
                    pe.sem_inc(s[stage], 2)

                def out_product(i, u):
                    pe.wait_ge(s["cx"], done(i, u))
                    if u:
                        pe.wait_ge(s["tp"], last_one(i, u))
                    else:
                        pe.wait_ge(s["x2"], last_one(i, u))
                    product(pe, psum[:, OP, :], cx[:, u], wo[:]).then_inc(s["op"], 1)

                def turn_x(i, u):
                    pe.wait_ge(s["xn"], done(i, u))
                    if u:
                        pe.wait_ge(s["xe"], last_one(i, u))
                    else:
                        pe.wait_ge(s["cte"], last_one(i, u))
                    transposes(pe, psum[:, TR, :], xn[:, u, :], g.ident[:]).then_inc(s["trx"], 1)

                def heads_T(bank, w, u):
                    for n in range(GROUPS):
                        for k in range(KD):
                            last = pe.matmul(psum[:, bank, n * P:(n + 1) * P], w[:, k, n * P:(n + 1) * P], xT[:, u, k, :],
                                             start=(k == 0), stop=(k == KD - 1))
                    return last

                def qkv(i, u):
                    pe.wait_ge(s["xe"], done(i, u))
                    if u:
                        pe.wait_ge(s["qe"], last_one(i, u))
                        pe.wait_ge(s["ke"], last_one(i, u))
                        pe.wait_ge(s["ve"], last_one(i, u))
                    else:
                        pe.wait_ge(s["pe2"], last_one(i, u))
                        pe.wait_ge(s["pe3"], last_one(i, u))
                        pe.wait_ge(s["tp"], done(i, 1))
                    heads_T(QB, wq, u).then_inc(s["qp"], 1)
                    heads_T(KB, wk, u).then_inc(s["kp"], 1)
                    product(pe, psum[:, OP, 0:P], xT[:, u], wv[:]).then_inc(s["vp"], 1)

                def scores(i, u):
                    pe.wait_ge(s["qe"], done(i, u))
                    pe.wait_ge(s["ke"], done(i, u))
                    pe.wait_ge(s["sm"], last_one(i, u))
                    for n in range(GROUPS):
                        for j in range(2):
                            rows = slice(j * SQ, (j + 1) * SQ)
                            last = pe.matmul(psum[rows, SB + n // 2, (n % 2) * 4 * SQ:(n % 2 + 1) * 4 * SQ],
                                             qT[:, u, n, rows], kT[:, u, n, j].rearrange("p a t -> p (a t)"),
                                             start=True, stop=True)
                    last.then_inc(s["sp"], 1)

                def turn_probs(i, u):
                    pe.wait_ge(s["ex"], done(i, u))
                    for n in range(4):
                        if n >= 2:
                            pe.wait_ge(s[f"pe{n - 2}"], done(i, u))
                        elif u:
                            pe.wait_ge(s[f"pe{n + 2}"], last_one(i, u))
                        else:
                            pe.wait_ge(s[("qe", "ke")[n]], done(i, 1))
                        transposes(pe, psum[:, (QB, KB)[n % 2], :],
                                   pr[:, u, 4 * n:4 * n + 4, :].rearrange("p h t -> p (h t)"), g.ident[:]).then_inc(s[f"pt{n}"], 1)

                def weighted(i, u):
                    pe.wait_ge(s["ve"], done(i, u))
                    pe.wait_ge(s["co"], last_one(i, u))
                    for h in range(H):
                        if h % 4 == 0:
                            pe.wait_ge(s[f"pe{h // 4}"], done(i, u))
                        last = pe.matmul(psum[:, PB + h // 8, (h % 8) * VW:(h % 8 + 1) * VW], pT[:, u, h, :],
                                         vv[:, u, h // 4, :], start=True, stop=True)
                    last.then_inc(s["pv"], 1)

                def turn_out(i, u):
                    pe.wait_ge(s["co"], done(i, u))
                    if u:
                        pe.wait_ge(s["cte"], last_one(i, u))
                    else:
                        pe.wait_ge(s["xe"], done(i, 1))
                    transposes(pe, psum[:, TR, :], co[:, u, :], g.ident[:]).then_inc(s["trc"], 1)

                def out_product2(i, u):
                    pe.wait_ge(s["cte"], done(i, u))
                    if u:
                        pe.wait_ge(s["x2"], last_one(i, u))
                    else:
                        pe.wait_ge(s["ve"], done(i, 1))
                    product(pe, psum[:, OP, :], cT[:, u], wo2[:]).then_inc(s["op2"], 1)

                for name in ("wo", "wq", "wk", "wv", "wo2"):
                    pe.wait_ge(s[name], 16)
                with pe.Fori(0, NT // 2) as i:
                    for stage in (out_product, turn_x):
                        for u in range(2):
                            stage(i, u)
                    for u in range(2):
                        qkv(i, u)
                        scores(i, u)
                    for u in range(2):
                        turn_probs(i, u)
                        weighted(i, u)
                    for stage in (turn_out, out_product2):
                        for u in range(2):
                            stage(i, u)


def experts(nc, io, g, psum):
    UP, TR, DN = 2, 4, 6

    with ExitStack() as ctx:
        def sb(name, shape, dt=F32):
            return ctx.enter_context(nc.sbuf_tensor(name, shape, dt))

        s = Sems(nc, ctx, "moe")
        wr = sb("wr", [P, KD, E_])
        iota = sb("iota", [P, E_])
        st = sb("moe_st", [P, NT, 6])
        mv = sb("moe_mv", [P, NT, 2])
        rs = sb("moe_rs", [P, NT])
        rlog = sb("moe_rlog", [P, NT])
        rseed = sb("moe_rseed", [P, NT])
        rtmp = sb("moe_rtmp", [P, NT])
        xn = sb("moe_xn", [P, 2, D])
        xT = sb("moe_xT", [P, 2, KD, P])
        x_hi = sb("moe_xhi", [P, NT, KD, P], F32R)
        x_lo = sb("moe_xlo", [P, NT, KD, P], F32R)
        sc = sb("moe_sc", [P, NT, E_])
        top = sb("moe_top", [P, NT, 8])
        idx = sb("moe_idx", [P, NT, 8], U32)
        idf = sb("moe_idf", [P, NT, 2])
        gap = sb("moe_gap", [P, NT])
        ex = sb("moe_ex", [P, NT])
        ex1 = sb("moe_ex1", [P, NT])
        w12 = sb("moe_w12", [P, 2, NT])
        pick = sb("moe_pick", [P, 2, NT, E_])
        wt = sb("moe_wt", [P, NT, E_])
        raw = sb("moe_raw", [P, 3, KD * EW])
        wg_hi = sb("wg_hi", [P, 2, KD, EW], F32R)
        wg_lo = sb("wg_lo", [P, 2, KD, EW], F32R)
        wu_hi = sb("wu_hi", [P, 2, KD, EW], F32R)
        wu_lo = sb("wu_lo", [P, 2, KD, EW], F32R)
        wd_hi = sb("wd_hi", [P, 2, EC, D], F32R)
        wd_lo = sb("wd_lo", [P, 2, EC, D], F32R)
        act_g = sb("moe_g", [P, 2, EW])
        hid = sb("moe_h", [P, 2, EW])
        h_hi = sb("moe_hhi", [P, 2, EC, P], F32R)
        h_lo = sb("moe_hlo", [P, 2, EC, P], F32R)
        weights = ((wg_hi, wg_lo), (wu_hi, wu_lo), (wd_hi, wd_lo))

        def chunk(i, v, t):
            return i * (2 * NT) + (v * NT + t + 3)

        with nc.Block() as block:
            @block.sync
            def _(sp):
                sp.dma_start(wr[:], io["wr"].rearrange("(k p) n -> p k n", p=P)).then_inc(s["wr"], 16)
                sp.dma_start(iota[:], io["iota"].partition_broadcast(P)).then_inc(s["wr"], 16)
                with sp.Fori(0, EP) as e:
                    for n, name in enumerate(("wg", "wu")):
                        sp.wait_ge(s["wlo"], e * 3 + (n + 1))
                        sp.dma_start(raw[:, n, :].rearrange("p (k n) -> p k n", k=KD),
                                     io[name].rearrange("(k p) n -> p k n", p=P)[:, :, bass.ds(e * EW, EW)])\
                            .then_inc(s[name], 16)
                    sp.wait_ge(s["wlo"], e * 3 + 3)
                    sp.dma_start(raw[:, 2, :].rearrange("p (k n) -> p k n", k=EC),
                                 io["wd"][bass.ds(e * EW, EW), :].rearrange("(k p) n -> p k n", p=P)).then_inc(s["wd"], 16)
                for t in range(NT):
                    sp.wait_ge(s["ya"], chunk(1, 1, t))
                    sp.dma_start(io["out"].rearrange("(t p) d -> p t d", p=P)[:, t, :], g.x[:, t, :]).then_inc(s["out"], 16)
                sp.wait_ge(s["out"], 16 * NT)

            @block.gpsimd
            def _(pool):
                pool.sem_inc(s["wlo"], 3)
                with pool.Fori(0, EP // 2) as i:
                    for v in range(2):
                        for n, (hi, lo) in enumerate(weights):
                            pool.wait_ge(s["whi"], i * 6 + (v * 3 + n + 1))
                            nc.gpsimd.tensor_tensor(lo[:, v].rearrange("p k n -> p (k n)"), raw[:, n, :],
                                                    hi[:, v].rearrange("p k n -> p (k n)").bitcast(F32),
                                                    ALU.subtract).then_inc(s["wlo"], 1)

            @block.scalar
            def _(act):
                act.preload_act_table_set(TABLES)
                act.wait_ge(s["ba"], NT)
                rsqrt_seed(nc, act, rseed[:], rlog[:], mv[:, :, 1], g.cols[:, 9:10], s["rlog"], 1).then_inc(s["rseed"], 1)
                for t in range(NT):
                    u = t % 2
                    act.wait_ge(s["trx"], t + 1)
                    if t >= 2:
                        act.wait_ge(s["rp"], t - 1)
                        act.wait_ge(s["xlo"], t - 1)
                    nc.scalar.copy(xT[:, u], psum[:, u, :].rearrange("p (k t) -> p k t", k=KD)).then_inc(s["xe"], 1)
                    act.wait_ge(s["xe"], t + 1)
                    nc.scalar.copy(x_hi[:, t], xT[:, u]).then_inc(s["xhi"], 1)
                act.wait_ge(s["gap"], 1)
                nc.scalar.activation(ex[:], gap[:], ACT.Exp).then_inc(s["ex"], 1)
                for stage in ("sg", "hhi"):
                    act.sem_inc(s[stage], 2)
                act.preload_act_table(ACT.Silu)

                def silu(i, v, t):
                    act.wait_ge(s["gp"], chunk(i, v, t))
                    act.wait_ge(s["hd"], chunk(i, v, t - 2))
                    nc.scalar.activation(act_g[:, t % 2], psum[:, t % 2, 0:EW], ACT.Silu).then_inc(s["sg"], 1)

                def high(i, v, t):
                    act.wait_ge(s["trh"], chunk(i, v, t))
                    act.wait_ge(s["dp"], chunk(i, v, t - 2))
                    nc.scalar.copy(h_hi[:, t % 2], psum[:, TR + t % 2, 0:EW].rearrange("p (k t) -> p k t", k=EC)).then_inc(s["hhi"], 1)

                with act.Fori(0, EP // 2) as i:
                    for v in range(2):
                        for t in range(NT):
                            silu(i, v, t)
                            if t:
                                high(i, v, t - 1)
                        high(i, v, NT - 1)

            @block.vector
            def _(dve):
                for stage in ("hd", "hlo", "ya"):
                    dve.sem_inc(s[stage], 2)
                for t in range(NT):
                    nc.vector.bn_stats(st[:, t, :], g.x[:, t, :]).then_inc(s["bs"], 1)
                for t in range(NT):
                    dve.wait_ge(s["bs"], t + 1)
                    nc.vector.bn_aggr(mv[:, t, :], st[:, t, :]).then_inc(s["ba"], 1)
                dve.wait_ge(s["rseed"], 1)
                rsqrt_refine(nc, dve, rs[:], rtmp[:], mv[:, :, 1], LN_EPS, rseed[:], s["rn1"], s["rn2"], 1).then_inc(s["rs"], 1)
                dve.wait_ge(s["rs"], 1)
                for t in range(NT):
                    if t >= 2:
                        dve.wait_ge(s["trx"], t - 1)
                    nc.vector.tensor_scalar(xn[:, t % 2], g.x[:, t, :], mv[:, t, 0:1], rs[:, t:t + 1],
                                            ALU.subtract, ALU.mult).then_inc(s["xn"], 1)
                    if t:
                        dve.wait_ge(s["xhi"], t)
                        nc.vector.tensor_tensor(x_lo[:, t - 1], xT[:, (t - 1) % 2], x_hi[:, t - 1].bitcast(F32),
                                                ALU.subtract).then_inc(s["xlo"], 1)
                dve.wait_ge(s["xhi"], NT)
                nc.vector.tensor_tensor(x_lo[:, NT - 1], xT[:, (NT - 1) % 2], x_hi[:, NT - 1].bitcast(F32),
                                        ALU.subtract).then_inc(s["xlo"], 1)

                chain = [0]

                def link(ins):
                    chain[0] += 1
                    ins.then_inc(s["chain"], 1)
                    dve.wait_ge(s["chain"], chain[0])

                dve.wait_ge(s["rp"], NT)
                dve.wait_ge(s["wr"], 32)
                link(nc.vector.tensor_copy(sc[:], psum[:, 2, 0:NT * E_].rearrange("p (t e) -> p t e", t=NT)))
                for t in range(NT):
                    last = nc.vector.max(out=top[:, t, :], in_=sc[:, t, :])
                link(last)
                for t in range(NT):
                    last = nc.vector.max_index(out=idx[:, t, :], in_max=top[:, t, :], in_values=sc[:, t, :])
                link(last)
                link(nc.vector.tensor_copy(idf[:], idx[:, :, 0:2]))
                nc.vector.tensor_tensor(gap[:], top[:, :, 1], top[:, :, 0], ALU.subtract).then_inc(s["gap"], 1)
                dve.wait_ge(s["ex"], 1)
                link(nc.vector.tensor_scalar(ex1[:], ex[:], 1.0, None, ALU.add))
                link(nc.vector.reciprocal(w12[:, 0], ex1[:]))
                link(nc.vector.tensor_tensor(w12[:, 1], ex[:], w12[:, 0], ALU.mult))
                for n in range(2):
                    link(nc.vector.tensor_tensor(pick[:, n], iota[:].unsqueeze(1).to_broadcast([P, NT, E_]),
                                                 spread(idf[:, :, n], E_), ALU.is_equal))
                    link(nc.vector.tensor_tensor(pick[:, n], pick[:, n], spread(w12[:, n], E_), ALU.mult))
                link(nc.vector.tensor_tensor(wt[:], pick[:, 0], pick[:, 1], ALU.add))

                def weights_high(i, v):
                    for n, (hi, _) in enumerate(weights):
                        dve.wait_ge(s[("wg", "wu", "wd")[n]], i * 32 + (v * 16 + 16))
                        nc.vector.tensor_copy(hi[:, v].rearrange("p k n -> p (k n)"), raw[:, n, :]).then_inc(s["whi"], 1)

                def hidden(i, v, t):
                    dve.wait_ge(s["sg"], chunk(i, v, t))
                    dve.wait_ge(s["gp"], chunk(i, v, t))
                    dve.wait_ge(s["trh"], chunk(i, v, t - 2))
                    for n in range(2):
                        cols = slice(n * F, (n + 1) * F)
                        last = nc.vector.scalar_tensor_tensor(
                            out=hid[:, t % 2, cols], in0=act_g[:, t % 2, cols],
                            scalar=wt[:, t, bass.ds(i * 4 + (v * 2 + n), 1)],
                            in1=psum[:, UP + t % 2, cols], op0=ALU.mult, op1=ALU.mult)
                    last.then_inc(s["hd"], 1)

                def low(i, v, t):
                    dve.wait_ge(s["hhi"], chunk(i, v, t))
                    dve.wait_ge(s["dp"], chunk(i, v, t - 2))
                    nc.vector.tensor_tensor(h_lo[:, t % 2], psum[:, TR + t % 2, 0:EW].rearrange("p (k t) -> p k t", k=EC),
                                            h_hi[:, t % 2].bitcast(F32), ALU.subtract).then_inc(s["hlo"], 1)

                def add(i, v, t):
                    dve.wait_ge(s["dp"], chunk(i, v, t))
                    nc.vector.tensor_tensor(g.x[:, t, :], g.x[:, t, :], psum[:, DN + t % 2, :], ALU.add).then_inc(s["ya"], 1)

                with dve.Fori(0, EP // 2) as i:
                    for v in range(2):
                        weights_high(i, v)
                        for t in range(NT):
                            hidden(i, v, t)
                            if t:
                                low(i, v, t - 1)
                            if t >= 2:
                                add(i, v, t - 2)
                        low(i, v, NT - 1)
                        add(i, v, NT - 2)
                        add(i, v, NT - 1)

            @block.tensor
            def _(pe):
                for t in range(NT):
                    u = t % 2
                    pe.wait_ge(s["xn"], t + 1)
                    if t >= 2:
                        pe.wait_ge(s["xe"], t - 1)
                    transposes(pe, psum[:, u, :], xn[:, u, :], g.ident[:]).then_inc(s["trx"], 1)
                    if t == 0:
                        pe.wait_ge(s["wr"], 32)
                    pe.wait_ge(s["xe"], t + 1)
                    product(pe, psum[:, 2, t * E_:(t + 1) * E_], xT[:, u], wr[:]).then_inc(s["rp"], 1)
                for stage in ("gp", "trh", "dp"):
                    pe.sem_inc(s[stage], 2)
                pe.wait_ge(s["xlo"], NT)
                pe.wait_ge(s["chain"], 1)

                def gate_up(i, v, t):
                    pe.wait_ge(s["hd"], chunk(i, v, t - 2))
                    for bank, (hi, lo) in ((t % 2, weights[0]), (UP + t % 2, weights[1])):
                        last = split_product(pe, psum[:, bank, 0:EW],
                                             [(x_hi[:, t, k, :], x_lo[:, t, k, :], hi[:, v, k, :], lo[:, v, k, :])
                                              for k in range(KD)])
                    last.then_inc(s["gp"], 1)

                def down(i, v, t):
                    pe.wait_ge(s["hd"], chunk(i, v, t))
                    pe.wait_ge(s["hlo"], chunk(i, v, t - 2))
                    transposes(pe, psum[:, TR + t % 2, :], hid[:, t % 2, :], g.ident[:], EC).then_inc(s["trh"], 1)

                def down2(i, v, t):
                    pe.wait_ge(s["hhi"], chunk(i, v, t))
                    pe.wait_ge(s["hlo"], chunk(i, v, t))
                    pe.wait_ge(s["ya"], chunk(i, v, t - 2))
                    split_product(pe, psum[:, DN + t % 2, :],
                                  [(h_hi[:, t % 2, k, :], h_lo[:, t % 2, k, :], wd_hi[:, v, k, :], wd_lo[:, v, k, :])
                                   for k in range(EC)]).then_inc(s["dp"], 1)

                with pe.Fori(0, EP // 2) as i:
                    for v in range(2):
                        pe.wait_ge(s["wlo"], i * 6 + (v * 3 + 6))
                        for t in range(NT + 2):
                            if t < NT:
                                gate_up(i, v, t)
                            if 1 <= t <= NT:
                                down(i, v, t - 1)
                            if t >= 2:
                                down2(i, v, t - 2)


def build(nc, io):
    with ExitStack() as ctx:
        psum = ctx.enter_context(nc.psum_tensor("psum", [P, 8, 512], F32))

        class Shared:
            pass
        g = Shared()

        def sb(stack, name, shape, dt=F32):
            return stack.enter_context(nc.sbuf_tensor(name, shape, dt))

        g.x = sb(ctx, "x_sb", [P, NT, D])
        g.ident = sb(ctx, "ident_sb", [P, P])
        g.cols = sb(ctx, "cols_sb", [P, 10])
        with ExitStack() as out_ctx:
            g.bo = sb(out_ctx, "bo_sb", [P, D])
            g.ctxT = sb(out_ctx, "ctxT", [P, 2, 2, T + SQ])
            with ExitStack() as xa:
                g.bk = sb(xa, "bk_sb", [P, D])
                g.wk_hi = sb(xa, "wk_hi", [P, KC, D], F32R)
                g.wk_lo = sb(xa, "wk_lo", [P, KC, D], F32R)
                g.wv_hi = sb(xa, "wv_hi", [P, KC, D], F32R)
                g.wv_lo = sb(xa, "wv_lo", [P, KC, D], F32R)
                g.q_hi = sb(xa, "q_hi", [P, GROUPS, T], F32R)
                g.q_lo = sb(xa, "q_lo", [P, GROUPS, T], F32R)
                g.kd_hi = sb(xa, "kd_hi", [P, GROUPS, B * DCA], F32R)
                g.kd_lo = sb(xa, "kd_lo", [P, GROUPS, B * DCA], F32R)
                g.qbd_hi = sb(xa, "qbd_hi", [P, GROUPS, 4 * SQ], F32R)
                g.qbd_lo = sb(xa, "qbd_lo", [P, GROUPS, 4 * SQ], F32R)
                g.y_hi = sb(xa, "y_hi", [P, 3, KC, P], F32R)
                g.y_lo = sb(xa, "y_lo", [P, 3, KC, P], F32R)
                g.k_hi = sb(xa, "k_hi", [P, 3, GROUPS, P], F32R)
                g.k_lo = sb(xa, "k_lo", [P, 3, GROUPS, P], F32R)
                g.v = sb(xa, "v_sb", [P, 2, PAIRS, PW])
                g.v_last = sb(xa, "v_last", [P, PAIRS, 2 * PW])
                g.ctx = sb(xa, "ctx_sb", [P, PAIRS, HD])
                prepare(nc, io, g, psum)
                cross_attention(nc, io, g, psum)
            self_attention(nc, io, g, psum)
        experts(nc, io, g, psum)


def kernel(**inputs):
    import numpy as np
    import concourse.bacc as bacc
    from concourse.bass_utils import run_bass_kernel_spmd

    a = {k: np.asarray(v) for k, v in inputs.items()}
    f32 = np.float32
    G2 = PAIRS // 4

    kv_w = np.concatenate([a["L0_xattn_Wk"], a["L0_xattn_Wv"]], 1).reshape(DC, H, 2, HD)
    kv_b = np.concatenate([a["L0_xattn_bk"], a["L0_xattn_bv"]]).reshape(H, 2, HD)
    dca_w = a["L0_xattn_Wkv_dca"].reshape(DC, 2, D)
    dca_b = a["L0_xattn_bkv_dca"].reshape(2, D)

    def by_pair(v):
        return v.reshape((G2, 4, 2, HD) + v.shape[1:]).swapaxes(1, 2).reshape((KD, P) + v.shape[1:])

    rows = np.arange(P)
    cols = np.stack([np.tile(a[f"L0_xattn_{n}"], 4) for n in ("qn_w", "qn_b", "kn_w", "kn_b", "kn_dca_w", "kn_dca_b")]
                    + [(rows < LM).astype(f32), ((rows >= DCA_ROW) & (rows < DCA_ROW + DCA)).astype(f32),
                       np.full(P, HD * HEAD_EPS, f32), np.full(P, LN_EPS, f32)], 1)
    context = a["ctx_1024"]
    arrays = {
        "x": a["x"].reshape(T, D),
        "y": context[:, :SM].transpose(0, 2, 1),
        "yd": context[:, SM:].transpose(2, 0, 1).reshape(DC, B * DCA),
        "wq": a["L0_xattn_Wq"], "bq": a["L0_xattn_bq"],
        "wk": kv_w[:, :, 0].reshape(DC, D), "wv": kv_w[:, :, 1].reshape(DC, D), "bk": kv_b[:, 0].reshape(D),
        "wkd": dca_w[:, 0], "wvd": dca_w[:, 1], "bkd": dca_b[0],
        "bv": np.concatenate([by_pair(kv_b[:, 1].reshape(D)), by_pair(dca_b[1])], 0).T,
        "wo": by_pair(a["L0_xattn_Wo"]), "bo": a["L0_xattn_bo"],
        "cols": cols,
        "ident": np.eye(P, dtype=f32),
        "mask": np.where(np.arange(SQ)[None] <= rows[:, None] % SQ, 0.0, MASKED).astype(f32),
        "iota": np.arange(E_, dtype=f32),
        "sa_wq": a["L0_attn_Wq"],
        "sa_wk": np.repeat(a["L0_attn_Wk"].reshape(D, KV, 1, HD), 4, 2).reshape(D, D),
        "sa_wv": a["L0_attn_Wv"], "sa_wo": a["L0_attn_Wo"],
        "wr": a["L0_ffn_w_gate_router"].T,
        "wg": a["L0_ffn_w_gate_proj"].transpose(2, 0, 1).reshape(D, E_ * F),
        "wu": a["L0_ffn_w_up_proj"].transpose(2, 0, 1).reshape(D, E_ * F),
        "wd": a["L0_ffn_w_down_proj"].transpose(0, 2, 1).reshape(E_ * F, D),
    }
    arrays = {f"in_{k}": np.ascontiguousarray(v) for k, v in arrays.items()}
    nc = bacc.Bacc("TRN2", target_bir_lowering=False, num_devices=1)
    io = {k[3:]: nc.dram_tensor(k, v.shape, F32, kind="ExternalInput").ap() for k, v in arrays.items()}
    io["out"] = nc.dram_tensor("out_dram", (T, D), F32, kind="ExternalOutput").ap()
    io["vd"] = nc.dram_tensor("vd_dram", (B * DCA, D), F32, kind="Internal").ap()
    build(nc, io)
    r = run_bass_kernel_spmd(nc, [arrays], core_ids=[0])
    return r.results[0]["out_dram"].reshape(B, SQ, D)
```

```python
from contextlib import ExitStack

import concourse.bass as bass
from concourse import mybir

ALU = mybir.AluOpType
ACT = mybir.ActivationFunctionType
AX_X = mybir.AxisListType.X
F32 = mybir.dt.float32
F32R = mybir.dt.float32r
U32 = mybir.dt.uint32
I32 = mybir.dt.int32

P = 128
B, SQ, D = 16, 64, 512
SK, DC, DCA = 1601, 256, 16
H, HD = 16, 32
T = B * SQ
NT = T // P
KD = D // P
KC = DC // P
SM = SK - DCA
CH = -(-SM // P)
LAST = CH - 1
LM = SM - LAST * P
DCA_ROW = 64
PAIRS = H // 2
GROUPS = H // 4
PW = 2 * HD + 1
KV = 4
E_, F = 8, 192
EP = 4
EW = 2 * F
EC = EW // P
SCALE = HD ** -0.5
LN_EPS = 1e-5
HEAD_EPS = 1e-6
MASKED = -1e30
SAFE_SCORE = 70.0
TABLES = "natural_log_exp_and_others"


def head_view(ap):
    return ap.rearrange("p (h d) -> p h d", d=HD)


def spread(ap, n):
    return ap.unsqueeze(2).to_broadcast([ap.shape[0], ap.shape[1], n])


class Sems:

    def __init__(self, nc, ctx, phase):
        self.nc, self.ctx, self.phase, self.made = nc, ctx, phase, {}

    def __getitem__(self, name):
        if name not in self.made:
            self.made[name] = self.ctx.enter_context(self.nc.semaphore(f"{self.phase}_{name}"))
        return self.made[name]


def transposes(pe, bank, src, ident, n=KD):
    for k in range(n):
        last = pe.transpose(bank[:, k * P:(k + 1) * P], src[:, k * P:(k + 1) * P], ident)
    return last


def product(pe, bank, lhs, rhs):
    n = rhs.shape[1]
    for k in range(n):
        last = pe.matmul(bank, lhs[:, k, :], rhs[:, k, :], start=(k == 0), stop=(k == n - 1))
    return last


def split_product(pe, bank, terms, exact=()):
    todo = list(exact)
    for lhi, llo, rhi, rlo in terms:
        todo += [(lhi, rhi), (lhi, rlo), (llo, rhi)]
    for n, (lhs, rhs) in enumerate(todo):
        last = pe.matmul(bank, lhs, rhs, start=(n == 0), stop=(n == len(todo) - 1))
    return last


def rsqrt_seed(nc, act, seed, log, v, eps, done, count):
    nc.scalar.activation(log, v, ACT.Ln, bias=eps).then_inc(done, 1)
    act.wait_ge(done, count)
    return nc.scalar.activation(seed, log, ACT.Exp, scale=-0.5)


def rsqrt_refine(nc, dve, out, tmp, v, eps, seed, first, second, count):
    nc.vector.scalar_tensor_tensor(out=tmp, in0=v, scalar=eps, in1=seed, op0=ALU.add, op1=ALU.mult).then_inc(first, 1)
    dve.wait_ge(first, count)
    nc.vector.scalar_tensor_tensor(out=tmp, in0=tmp, scalar=-0.5, in1=seed, op0=ALU.mult, op1=ALU.mult).then_inc(second, 1)
    dve.wait_ge(second, count)
    return nc.vector.scalar_tensor_tensor(out=out, in0=tmp, scalar=1.5, in1=seed, op0=ALU.add, op1=ALU.mult)


LANDING = ((0, 4), (4, 8), (8, CH))


def load_context(sp, io, g, b, free=None):
    for n, (lo, hi) in enumerate(LANDING):
        end = min(hi * P, SM)
        if free:
            free(hi - 1)
        sp.dma_start(g.y[:, :, lo * P:end], io["y"][b].rearrange("(k p) t -> p k t", p=P)[:, :, lo * P:end])\
            .then_inc(g.landed[n], 16)


def prepare(nc, io, g, psum):
    with ExitStack() as ctx:
        def sb(name, shape, dt=F32):
            return ctx.enter_context(nc.sbuf_tensor(name, shape, dt))

        s = Sems(nc, ctx, "prep")
        wk = sb("wk_raw", [P, KC, D])
        wv = sb("wv_raw", [P, KC, D])
        wkd = sb("wkd", [P, KC, D])
        wvd = sb("wvd", [P, KC, D])
        wq = sb("wq", [P, KD, D])
        yd = sb("yd", [P, KC, B * DCA])
        bq = sb("bq", [P, D])
        bkd = sb("bkd", [P, D])
        bvs = sb("bvs", [P, 2 * KD])
        bvt = sb("bvt", [P, KD])
        bvb = sb("bvb", [P, KD, P])
        msum = sb("msum", [P, KD, H])
        st = sb("st", [P, NT, 6])
        mv = sb("mv", [P, NT, 2])
        rs = sb("rs", [P, NT])
        rlog = sb("rlog", [P, NT])
        rseed = sb("rseed", [P, NT])
        rtmp = sb("rtmp", [P, NT])
        qlog = sb("qlog", [P, 2, H])
        qseed = sb("qseed", [P, 2, H])
        qtmp = sb("qtmp", [P, 2, H])
        xn = sb("xn", [P, 2, D])
        xT = sb("xT", [P, 2, KD, P])
        qc = sb("qc", [P, 2, D])
        sq = sb("sq", [P, 2, D])
        ss = sb("ss", [P, 2, H])
        qr = sb("qr", [P, 2, H])
        qn = sb("qn", [P, 2, D])
        norms = g.ctxT[0:1, 0, 1, 0:6 * HD].rearrange("p (n d) -> p n d", n=6)
        cross = g.ctxT[0:1, 0, 0, 0:8 * HD].rearrange("p (i n d) -> p i n d", i=2, n=4)
        peak = sb("peak", [1, 2, 4])
        power = sb("power", [1, 2, 4])
        vd = xn

        PARTS = ((0, 2), (2, NT))

        def done(i, u):
            return i * 2 + (u + 3)

        def before(i, u):
            return i * 2 + (u + 1)

        with nc.Block() as block:
            @block.sync
            def _(sp):
                for n, (lo, hi) in enumerate(PARTS):
                    sp.dma_start(g.x[:, lo:hi, :], io["x"].rearrange("(t p) d -> p t d", p=P)[:, lo:hi, :]).then_inc(s[f"x{n}"], 16)
                    if n == 0:
                        sp.dma_start(wq[:], io["wq"].rearrange("(k p) n -> p k n", p=P)).then_inc(s["wq"], 16)
                sp.dma_start(wkd[:], io["wkd"].rearrange("(k p) n -> p k n", p=P)).then_inc(s["wkd"], 16)
                sp.dma_start(wvd[:], io["wvd"].rearrange("(k p) n -> p k n", p=P)).then_inc(s["wvd"], 16)
                sp.dma_start(yd[:], io["yd"].rearrange("(k p) n -> p k n", p=P)).then_inc(s["yd"], 16)
                sp.dma_start(wk[:], io["wk"].rearrange("(k p) n -> p k n", p=P)).then_inc(s["wk"], 16)
                sp.dma_start(wv[:], io["wv"].rearrange("(k p) n -> p k n", p=P)).then_inc(s["wv"], 16)
                sp.dma_start(g.wo[:], io["wo"].rearrange("k p n -> p k n")).then_inc(s["wo"], 16)
                load_context(sp, io, g, 0)
                for u in range(2):
                    sp.wait_ge(s["vd"], u + 1)
                    sp.dma_start(io["vd"][u * P:(u + 1) * P, :], vd[:, u, :]).then_inc(s["vd_out"], 16)
                sp.wait_ge(s["vd_out"], 32)

            @block.scalar
            def _(act):
                act.preload_act_table_set(TABLES)
                act.dma_start(g.ident[:], io["ident"]).then_inc(s["ident"], 16)
                act.dma_start(bq[:], io["bq"].partition_broadcast(P)).then_inc(s["bias"], 16)
                act.dma_start(bkd[:], io["bkd"].partition_broadcast(P)).then_inc(s["bias"], 16)
                act.dma_start(g.bk[:], io["bk"].partition_broadcast(P)).then_inc(s["bias"], 16)
                act.dma_start(g.cols[:], io["cols"]).then_inc(s["cols"], 16)
                act.dma_start(norms, io["norms"].rearrange("p (n d) -> p n d", n=6)).then_inc(s["norms"], 16)
                act.dma_start(bvs[:], io["bv"]).then_inc(s["bv"], 16)
                act.dma_start(g.bo[:], io["bo"].partition_broadcast(P)).then_inc(s["bo"], 16)
                act.wait_ge(s["cols"], 16)
                for stage in ("xe", "qe", "qlog", "qseed"):
                    act.sem_inc(s[stage], 2)
                for n, (lo, hi) in enumerate(PARTS):
                    act.wait_ge(s["ba"], hi)
                    rsqrt_seed(nc, act, rseed[:, lo:hi], rlog[:, lo:hi], mv[:, lo:hi, 1], g.cols[:, 9:10],
                               s["rlog"], n + 1).then_inc(s["rseed"], 1)

                def evac_xT(i, u):
                    act.wait_ge(s["trx"], done(i, u))
                    act.wait_ge(s["qp"], before(i, u))
                    nc.scalar.copy(xT[:, u], psum[:, u, :].rearrange("p (k t) -> p k t", k=KD)).then_inc(s["xe"], 1)

                def evac_heads(i, u, dst, w, b):
                    act.wait_ge(s["trq"], done(i, u))
                    nc.scalar.activation(dst, psum[:, 4 + u, :].rearrange("p (k t) -> p k t", k=GROUPS),
                                         ACT.Identity, scale=g.cols[:, w:w + 1], bias=g.cols[:, b:b + 1]).then_inc(s["qe"], 1)

                def evac_queries(i, u):
                    evac_heads(i, u, g.q[:, :, bass.ds((i * 2 + u) * P, P)], 0, 1)

                def seed(i, u):
                    act.wait_ge(s["qrd"], done(i, u))
                    act.wait_ge(s["qm"], before(i, u))
                    rsqrt_seed(nc, act, qseed[:, u], qlog[:, u], ss[:, u], g.cols[:, 8:9], s["qlog"],
                               done(i, u)).then_inc(s["qseed"], 1)

                evac_xT(0, 0)
                evac_xT(0, 1)
                seed(0, 0)
                seed(0, 1)
                with act.Fori(1, NT // 2) as i:
                    evac_xT(i, 0)
                    evac_xT(i, 1)
                    evac_queries(i - 1, 0)
                    seed(i, 0)
                    evac_queries(i - 1, 1)
                    seed(i, 1)
                end = NT // 2
                evac_queries(end - 1, 0)
                seed(end, 0)
                evac_queries(end - 1, 1)
                seed(end, 1)
                for u in range(2):
                    act.wait_ge(s["vdp"], u + 1)
                    nc.scalar.copy(vd[:, u, :], psum[:, 6 + u, :]).then_inc(s["vd"], 1)
                for u in range(2):
                    evac_heads(end, u, g.kd[:, :, u * P:(u + 1) * P], 4, 5)

            @block.gpsimd
            def _(pool):
                pool.sem_inc(s["qsq"], 2)

                def square(i, u):
                    pool.wait_ge(s["qb"], done(i, u))
                    pool.wait_ge(s["qrd"], before(i, u))
                    nc.gpsimd.tensor_tensor(sq[:, u], qc[:, u], qc[:, u], ALU.mult).then_inc(s["qsq"], 1)

                nc.gpsimd.memset(g.qbd_hi[:].bitcast(F32), 0.0)
                nc.gpsimd.memset(g.qbd_lo[:].bitcast(F32), 0.0)
                nc.gpsimd.memset(g.y_hi[:, 2].bitcast(F32), 0.0)
                nc.gpsimd.memset(g.y_lo[:, 2].bitcast(F32), 0.0)
                nc.gpsimd.memset(g.k_hi[:, 2].bitcast(F32), 0.0)
                nc.gpsimd.memset(g.k_lo[:, 2].bitcast(F32), 0.0)
                nc.gpsimd.memset(g.v[:], 1.0)
                nc.gpsimd.memset(g.ctx[:], 0.0)
                nc.gpsimd.memset(g.v_last[:], 0.0).then_inc(s["zero"], 1)
                pool.wait_ge(s["zero"], 1)
                pool.wait_ge(s["cols"], 16)
                for n, col in enumerate((PW - 1, 2 * PW - 1)):
                    nc.gpsimd.tensor_tensor(g.v_last[:, :, col], g.v_last[:, :, col],
                                            g.cols[:, 6 + n:7 + n].to_broadcast([P, PAIRS]), ALU.add)
                square(0, 0)
                square(0, 1)
                pool.wait_ge(s["wv"], 16)
                nc.gpsimd.tensor_copy(g.wv_hi[:], wv[:]).then_inc(s["wv_hi"], 1)
                with pool.Fori(1, NT // 2) as i:
                    square(i, 0)
                    square(i, 1)
                for u in range(2):
                    square(NT // 2, u)
                pool.wait_ge(s["wv_hi"], 1)
                nc.gpsimd.tensor_tensor(g.wv_lo[:], wv[:], g.wv_hi[:].bitcast(F32), ALU.subtract)

            @block.vector
            def _(dve):
                chain = [0]

                def link(ins):
                    chain[0] += 1
                    ins.then_inc(s["chain"], 1)
                    dve.wait_ge(s["chain"], chain[0])

                for stage in ("xn", "qb", "qrd", "qn1", "qn2", "qrs", "qm"):
                    dve.sem_inc(s[stage], 2)

                def statistics(n):
                    lo, hi = PARTS[n]
                    dve.wait_ge(s[f"x{n}"], 16)
                    for t in range(lo, hi):
                        nc.vector.bn_stats(st[:, t, :], g.x[:, t, :]).then_inc(s["bs"], 1)
                    for t in range(lo, hi):
                        dve.wait_ge(s["bs"], t + 1)
                        nc.vector.bn_aggr(mv[:, t, :], st[:, t, :]).then_inc(s["ba"], 1)

                def x_rstd(n):
                    lo, hi = PARTS[n]
                    dve.wait_ge(s["rseed"], n + 1)
                    link(rsqrt_refine(nc, dve, rs[:, lo:hi], rtmp[:, lo:hi], mv[:, lo:hi, 1], LN_EPS, rseed[:, lo:hi],
                                      s["rn1"], s["rn2"], n + 1))

                def normalise_x(i, u):
                    t = i * 2 + u
                    dve.wait_ge(s["trx"], before(i, u))
                    nc.vector.tensor_scalar(xn[:, u], g.x[:, t, :], mv[:, t, 0:1], rs[:].unsqueeze(2)[:, t, :],
                                            ALU.subtract, ALU.mult).then_inc(s["xn"], 1)

                def center(w):
                    rows, n = w.shape[0], w.shape[1] // HD
                    sums = msum[:].rearrange("p k h -> p (k h)")[0:rows, 0:n]
                    link(nc.vector.tensor_reduce(sums, head_view(w), AX_X, ALU.add))
                    link(nc.vector.scalar_tensor_tensor(out=head_view(w), in0=spread(sums, HD), scalar=-1.0 / HD,
                                                        in1=head_view(w), op0=ALU.mult, op1=ALU.add))

                def split(hi, lo, w):
                    link(nc.vector.tensor_copy(hi, w))
                    nc.vector.tensor_tensor(lo, w, hi.bitcast(F32), ALU.subtract)

                statistics(0)
                x_rstd(0)
                for u in range(2):
                    normalise_x(0, u)
                dve.wait_ge(s["bias"], 48)
                center(bq[:])
                dve.wait_ge(s["wq"], 16)
                center(wq[:].rearrange("p k n -> p (k n)"))
                dve.sem_inc(s["wq_c"], 1)

                def score_range():
                    dve.wait_ge(s["norms"], 16)
                    for n in range(2):
                        last = nc.vector.tensor_tensor(cross[:, n], norms[:, 2:6, :], norms[:, n:n + 1, :].to_broadcast([1, 4, HD]),
                                                       ALU.mult)
                    link(last)
                    link(nc.vector.tensor_tensor(cross, cross, cross, ALU.mult))
                    nc.vector.tensor_reduce(peak[:], cross, AX_X, ALU.max)
                    link(nc.vector.tensor_reduce(power[:], cross, AX_X, ALU.add))
                    link(nc.vector.tensor_scalar(power[:, 0, 0:4:2], peak[:, 0, 0:4:2], 1.25 * HD / 15, None, ALU.mult))
                    link(nc.vector.tensor_tensor(power[:, 0], power[:, 0], power[:, 1], ALU.add))
                    link(nc.vector.tensor_tensor(power[:, 0, 0:4:2], power[:, 0, 0:4:2], power[:, 0, 1:4:2], ALU.add))
                    link(nc.vector.tensor_tensor(power[:, 0, 0:1], power[:, 0, 0:1], power[:, 0, 2:3], ALU.max))
                    link(nc.vector.tensor_scalar(power[:, 0, 0:1], power[:, 0, 0:1], SAFE_SCORE ** 2 / (SCALE ** 2 * HD * 15),
                                                 None, ALU.is_gt))
                    nc.vector.tensor_copy(g.guard[:], power[:, 0, 0:1])

                def bias(i, u, b):
                    dve.wait_ge(s["qp"], done(i, u))
                    dve.wait_ge(s["qm"], before(i, u))
                    nc.vector.tensor_tensor(qc[:, u], psum[:, 2 + u, :], b, ALU.add).then_inc(s["qb"], 1)

                def reduce(i, u):
                    dve.wait_ge(s["qsq"], done(i, u))
                    dve.wait_ge(s["qrs"], before(i, u))
                    nc.vector.tensor_reduce(ss[:, u], head_view(sq[:, u]), AX_X, ALU.add).then_inc(s["qrd"], 1)

                def scale_heads(i, u):
                    dve.wait_ge(s["qseed"], done(i, u))
                    rsqrt_refine(nc, dve, qr[:, u], qtmp[:, u], ss[:, u], HD * HEAD_EPS, qseed[:, u],
                                 s["qn1"], s["qn2"], done(i, u)).then_inc(s["qrs"], 1)
                    dve.wait_ge(s["qrs"], done(i, u))
                    dve.wait_ge(s["trq"], before(i, u))
                    nc.vector.scalar_tensor_tensor(out=head_view(qn[:, u]), in0=head_view(qc[:, u]), scalar=HD ** 0.5,
                                                   in1=spread(qr[:, u], HD), op0=ALU.mult, op1=ALU.mult).then_inc(s["qm"], 1)

                def head_norm(i, b):
                    for u in range(2):
                        bias(i, u, b)
                        reduce(i, u)
                        scale_heads(i, u)

                statistics(1)
                x_rstd(1)
                for u in range(2):
                    normalise_x(1, u)
                head_norm(0, bq[:])
                center(bkd[:])
                center(g.bk[:])
                dve.wait_ge(s["wkd"], 16)
                center(wkd[:].rearrange("p k n -> p (k n)"))
                dve.sem_inc(s["wkd_c"], 1)
                dve.wait_ge(s["bv"], 16)
                link(nc.vector.tensor_tensor(bvt[:], bvs[:, 0:KD], bvs[:, KD:2 * KD], ALU.add))
                nc.vector.tensor_copy(bvb[:], spread(bvt[:], P)).then_inc(s["bvb"], 1)
                with dve.Fori(1, NT // 2 - 1) as i:
                    for u in range(2):
                        normalise_x(i + 1, u)
                    head_norm(i, bq[:])
                head_norm(NT // 2 - 1, bq[:])
                dve.wait_ge(s["wk"], 16)
                center(wk[:].rearrange("p k n -> p (k n)"))
                head_norm(NT // 2, bkd[:])
                split(g.wk_hi[:], g.wk_lo[:], wk[:])
                score_range()
                dve.wait_ge(s["bop"], 1)
                dve.wait_ge(s["bo"], 16)
                nc.vector.tensor_tensor(g.bo[:], g.bo[:], psum[:, 0, :], ALU.add)

            @block.tensor
            def _(pe):
                for stage in ("trx", "qp", "trq"):
                    pe.sem_inc(s[stage], 2)
                pe.wait_ge(s["ident"], 16)

                def turn_x(i, u):
                    pe.wait_ge(s["xn"], done(i, u))
                    pe.wait_ge(s["xe"], before(i, u))
                    transposes(pe, psum[:, u, :], xn[:, u, :], g.ident[:]).then_inc(s["trx"], 1)

                def project(i, u):
                    pe.wait_ge(s["xe"], done(i, u))
                    pe.wait_ge(s["qb"], before(i, u))
                    product(pe, psum[:, 2 + u, :], xT[:, u], wq[:]).then_inc(s["qp"], 1)

                def turn_heads(i, u):
                    pe.wait_ge(s["qm"], done(i, u))
                    pe.wait_ge(s["qe"], before(i, u))
                    transposes(pe, psum[:, 4 + u, :], qn[:, u, :], g.ident[:]).then_inc(s["trq"], 1)

                pe.wait_ge(s["wq_c"], 1)
                for stage in (turn_x, project):
                    for u in range(2):
                        stage(0, u)
                with pe.Fori(1, NT // 2) as i:
                    for u in range(2):
                        turn_x(i, u)
                    for u in range(2):
                        project(i, u)
                        turn_heads(i - 1, u)
                pe.wait_ge(s["yd"], 16)
                pe.wait_ge(s["wvd"], 16)
                pe.wait_ge(s["wkd_c"], 1)
                i = NT // 2
                for u in range(2):
                    pe.wait_ge(s["qb"], before(i, u))
                    product(pe, psum[:, 2 + u, :], yd[:, :, u * P:(u + 1) * P], wkd[:]).then_inc(s["qp"], 1)
                    turn_heads(i - 1, u)
                for u in range(2):
                    product(pe, psum[:, 6 + u, :], yd[:, :, u * P:(u + 1) * P], wvd[:]).then_inc(s["vdp"], 1)
                pe.wait_ge(s["bvb"], 1)
                pe.wait_ge(s["wo"], 16)
                pe.wait_ge(s["xe"], done(i - 1, 0))
                product(pe, psum[:, 0, :], bvb[:], g.wo[:]).then_inc(s["bop"], 1)
                for u in range(2):
                    turn_heads(i, u)
        g.spent = list(s.made.values())


def score_maxima(nc, io, g, psum):
    K_BANK, TR_BANK, S_BANK, M_BANK = 0, 1, 2, 4
    ONE = 1

    with ExitStack() as ctx:
        def sb(name, shape, dt=F32):
            return ctx.enter_context(nc.sbuf_tensor(name, shape, dt))

        s = Sems(nc, ctx, "max")
        y = sb("max_y", [P, KC, P])
        kc = sb("max_kc", [P, D])
        sq = sb("max_sq", [P, D])
        ss = sb("max_ss", [P, H])
        klog = sb("max_log", [P, H])
        seed = sb("max_seed", [P, H])
        tmp = sb("max_tmp", [P, H])
        kr = sb("max_kr", [P, H])
        kn = sb("max_kn", [P, D])
        kT = sb("max_kT", [P, GROUPS, P])
        top = sb("max_top", [P, PAIRS])
        best = sb("max_best", [P, 2, PAIRS])
        turned = sb("max_turned", [2 * PAIRS, P])
        queries = sb("max_q", [P, GROUPS, 4 * SQ])

        def step(b, c):
            return b * CH + (c + 1)

        def rounds(eng, start, chunk, finish):
            guard = eng.value_load(g.guard[0:1, 0:1], min_val=0, max_val=1)
            with eng.If(guard != 0):
                with eng.Fori(0, B) as b:
                    start(b)
                    with eng.Fori(0, LAST) as c:
                        chunk(b, c, P)
                    chunk(b, LAST, LM)
                    finish(b)
            eng.sem_inc(s["over"], ONE)

        def nothing(*_):
            pass

        with nc.Block() as block:
            @block.sync
            def _(sp):
                def chunk(b, c, w):
                    sp.wait_ge(s["krd"], step(b, c))
                    sp.sem_inc(s["gate_sp"], 1)
                    sp.dma_start(y[:, :, 0:w], io["y"][b].rearrange("(k p) t -> p k t", p=P)[:, :, bass.ds(c * P, w)])\
                        .then_inc(s["y"], 16)

                def finish(b):
                    sp.wait_ge(s["me"], b + 1)
                    sp.sem_inc(s["gate_sp"], 1)
                    sp.dma_start(io["shift"][b], turned[:]).then_inc(s["out"], 16)
                    sp.wait_ge(s["out"], b * 16 + 16)
                    sp.sem_inc(s["gate_sp"], 1)

                sp.sem_inc(s["krd"], ONE)
                rounds(sp, nothing, chunk, finish)

            @block.tensor
            def _(pe):
                def chunk(b, c, w):
                    n = step(b, c)
                    pe.wait_ge(s["y"], n * 16)
                    for k in range(KC):
                        for part in (g.wk_hi, g.wk_lo):
                            last = pe.matmul(psum[0:w, K_BANK, :], y[:, k, 0:w], part[:, k, :].bitcast(F32),
                                             start=(k == 0 and part is g.wk_hi), stop=(k == KC - 1 and part is g.wk_lo))
                    last.then_inc(s["kp"], 1)
                    pe.wait_ge(s["km"], n)
                    transposes(pe, psum[:, TR_BANK, :], kn, g.ident[:]).then_inc(s["tr"], 1)
                    pe.wait_ge(s["ke"], n)
                    scores(w, kT[:, :, 0:w])

                def scores(w, keys):
                    for p in range(PAIRS):
                        lhs = queries[:, p // 2, (p % 2) * P:(p % 2 + 1) * P]
                        last = pe.matmul(psum[:, S_BANK + p // 4, (p % 4) * w:(p % 4 + 1) * w], lhs, keys[:, p // 2, :],
                                         start=True, stop=True)
                    last.then_inc(s["sc"], 1)

                def start(b):
                    pe.wait_ge(s["q"], b * 4 + 4)
                    pe.sem_inc(s["gate"], 1)

                def finish(b):
                    pe.wait_ge(s["best"], (b + 1) * CH)
                    scores(DCA, g.kd[:, :, bass.ds(b * DCA, DCA)])
                    pe.wait_ge(s["neg"], b + 1)
                    pe.transpose(psum[0:2 * PAIRS, M_BANK, 0:P], best[:].rearrange("p n q -> p (n q)"), g.ident[:])\
                        .then_inc(s["mt"], 1)

                rounds(pe, start, chunk, finish)

            @block.scalar
            def _(act):
                def chunk(b, c, w):
                    n = step(b, c)
                    act.wait_ge(s["krd"], n + ONE)
                    rsqrt_seed(nc, act, seed[0:w], klog[0:w], ss[0:w], g.cols[0:w, 8:9], s["klog"], n).then_inc(s["seed"], 1)
                    act.wait_ge(s["tr"], n)
                    nc.scalar.activation(kT[:, :, 0:w], psum[:, TR_BANK, :].rearrange("p (g t) -> p g t", g=GROUPS)[:, :, 0:w],
                                         ACT.Identity, scale=g.cols[:, 2:3], bias=g.cols[:, 3:4]).then_inc(s["ke"], 1)

                def finish(b):
                    act.wait_ge(s["mt"], b + 1)
                    nc.scalar.copy(turned[:], psum[0:2 * PAIRS, M_BANK, 0:P]).then_inc(s["me"], 1)

                act.preload_act_table_set(TABLES)
                rounds(act, nothing, chunk, finish)

            @block.gpsimd
            def _(pool):
                for sem in g.spent:
                    pool.sem_clear(sem)
                pool.wait_ge(s["over"], 4 * ONE)

            @block.vector
            def _(dve):
                links = s["link"]

                def start(b):
                    nc.vector.memset(queries[:], 0.0).then_inc(s["clear"], 1)
                    dve.wait_ge(s["clear"], b + 1)
                    for i in range(4):
                        rows, at = slice(i * HD, (i + 1) * HD), slice(i * SQ, (i + 1) * SQ)
                        nc.vector.tensor_copy(queries[rows, :, at], g.q[rows, :, bass.ds(b * SQ, SQ)]).then_inc(s["q"], 1)
                    nc.vector.memset(best[:, 0], MASKED).then_inc(s["fresh"], 1)

                def chunk(b, c, w):
                    n = step(b, c)
                    dve.wait_ge(s["kp"], n)
                    nc.vector.tensor_tensor(kc[0:w], psum[0:w, K_BANK, :], g.bk[0:w], ALU.add).then_inc(links, 1)
                    dve.wait_ge(links, b * (3 * CH) + (c * 3 + 1))
                    nc.vector.tensor_tensor(sq[0:w], kc[0:w], kc[0:w], ALU.mult).then_inc(links, 1)
                    dve.wait_ge(links, b * (3 * CH) + (c * 3 + 2))
                    nc.vector.tensor_reduce(ss[0:w], head_view(sq[0:w]), AX_X, ALU.add).then_inc(s["krd"], 1)
                    dve.wait_ge(s["seed"], n)
                    rsqrt_refine(nc, dve, kr[0:w], tmp[0:w], ss[0:w], HD * HEAD_EPS, seed[0:w], s["kn1"], s["kn2"], n)\
                        .then_inc(links, 1)
                    dve.wait_ge(links, b * (3 * CH) + (c * 3 + 3))
                    nc.vector.scalar_tensor_tensor(out=head_view(kn[0:w]), in0=head_view(kc[0:w]), scalar=HD ** 0.5,
                                                   in1=spread(kr[0:w], HD), op0=ALU.mult, op1=ALU.mult).then_inc(s["km"], 1)
                    dve.wait_ge(s["sc"], b + n)
                    reduce(top[:], w).then_inc(s["topd"], 1)
                    dve.wait_ge(s["topd"], n)
                    dve.wait_ge(s["fresh"], b + 1)
                    nc.vector.tensor_tensor(best[:, 0], best[:, 0], top[:], ALU.max).then_inc(s["best"], 1)
                    dve.wait_ge(s["best"], n)

                def reduce(out, w):
                    for n in range(2):
                        last = nc.vector.tensor_reduce(out[:, n * 4:(n + 1) * 4],
                                                       psum[:, S_BANK + n, 0:4 * w].rearrange("p (q t) -> p q t", q=4),
                                                       AX_X, ALU.max)
                    return last

                def finish(b):
                    dve.wait_ge(s["sc"], (b + 1) * (CH + 1))
                    reduce(best[:, 1], DCA).then_inc(s["second"], 1)
                    dve.wait_ge(s["second"], b + 1)
                    nc.vector.tensor_scalar(best[:], best[:], -1.0, None, ALU.mult).then_inc(s["neg"], 1)
                    dve.wait_ge(s["mt"], b + 1)

                rounds(dve, start, chunk, finish)


def cross_attention(nc, io, g, psum):
    K_BANK, V_BANK, TR_BANK, S_BANK, O_BANK = 0, 1, 2, 3, 5
    
    with ExitStack() as ctx:
        def sb(name, shape, dt=F32):
            return ctx.enter_context(nc.sbuf_tensor(name, shape, dt))

        s = Sems(nc, ctx, "xa")
        y = g.y
        kc = sb("kc", [P, 3, D])
        sq = sb("ksq", [P, 3, D])
        ss = sb("kss", [P, 3, H])
        kr = sb("kr", [P, 3, H])
        klog = sb("klog", [P, 3, H])
        kseed = sb("kseed", [P, 3, H])
        ktmp = sb("ktmp", [P, 3, H])
        kn = sb("kn", [P, 3, D])
        k32 = sb("k32", [P, 3, GROUPS, P])
        probs = sb("probs", [P, 3, H * SQ])
        o_sb = sb("o_sb", [P, PAIRS, 2 * PW])
        rinv = sb("rinv", [P, PAIRS, 2])
        od = sb("od", [P, PAIRS, HD])
        select_raw = sb("select_raw", [2, 2, P])
        shift_raw = sb("shift_raw", [2, H * SQ])
        select = sb("select", [2, 2, P], F32R)
        shift = sb("shift", [2, H * SQ], F32R)

        def buf(c):
            return 2 if c == LAST else c % 2

        def at(b, c):
            return (b, c) if c < CH else (b + 1, c - CH)

        def done(b, c):
            return b * CH + (CH + c + 1)

        def before(b, c):
            return done(b, c - CH if c == LAST else c - 2 if c >= 2 else c - 3)

        def batches(eng, first, steps):
            def run(guarded):
                first(guarded)
                with eng.Fori(0, B - 1) as b:
                    steps(b, CH, guarded)
                steps(B - 1, 0, guarded)

            guard = eng.value_load(g.guard[0:1, 0:1], min_val=0, max_val=1)
            with eng.If(guard != 0):
                run(True)
            with eng.Else():
                run(False)
            eng.sem_inc(s["over"], 1)

        def parts(guarded):
            return 9 if guarded else 8

        def ahead(c, n, room):
            return c + n < CH + room

        o_bank = [psum[:, O_BANK + p // 3, (p % 3) * 2 * PW:(p % 3 + 1) * 2 * PW] for p in range(PAIRS)]

        with nc.Block() as block:
            @block.sync
            def _(sp):
                def second_values(b):
                    sp.wait_ge(s["pv"], done(b, -1))
                    sp.dma_start(g.v_last[DCA_ROW:DCA_ROW + DCA, :, PW:2 * PW - 1],
                                 io["vd"][bass.ds(b * DCA, DCA), :].rearrange("t (p n) -> t p n", p=PAIRS))\
                        .then_inc(s["vd"], 16)

                def shifts(b):
                    if not isinstance(b, int):
                        sp.wait_ge(s["qb"], b * parts(True))
                    sp.dma_start(shift_raw[:], io["shift"][b].rearrange("(s q) n -> s (q n)", s=2)).then_inc(s["shift"], 16)

                for dst, src in ((g.sa_wq, io["sa_wq"]), (g.sa_wk, io["sa_wk"]), (g.sa_wo, io["sa_wo"])):
                    sp.dma_start(dst[:], src.rearrange("(k p) n -> p k n", p=P)).then_inc(s["sa_w"], 16)
                second_values(0)
                sp.dma_start(select_raw[:].rearrange("s n p -> s (n p)"), io["select"]).then_inc(s["select"], 16)

                def batch(b, guarded):
                    def free(c):
                        sp.wait_ge(s["yhi"], done(b, c - CH))
                        sp.wait_ge(s["ylo"], done(b, c - CH))

                    load_context(sp, io, g, b, free)
                    second_values(b)
                    if guarded:
                        shifts(b)

                guard = sp.value_load(g.guard[0:1, 0:1], min_val=0, max_val=1)
                with sp.If(guard != 0):
                    shifts(0)
                    with sp.Fori(1, B) as b:
                        batch(b, True)
                with sp.Else():
                    with sp.Fori(1, B) as b:
                        batch(b, False)
                sp.wait_ge(s["sa_w"], 48)
                sp.wait_ge(s["select"], 16)

            @block.scalar
            def _(act):
                act.preload_act_table_set(TABLES)
                for stage in ("yhi", "ke", "ve", "ex", "klog", "kseed"):
                    act.sem_inc(s[stage], CH)
                act.sem_inc(s["oe"], 1)

                def y_high(b, c):
                    b, c = at(b, c)
                    n = next(n for n, (lo, hi) in enumerate(LANDING) if lo <= c < hi)
                    w = min(P, SM - c * P)
                    act.wait_ge(g.landed[n], b * 16 + 16)
                    act.wait_ge(s["vp"], before(b, c))
                    nc.scalar.copy(g.y_hi[:, buf(c), :, 0:w], y[:, :, c * P:c * P + w]).then_inc(s["yhi"], 1)

                def k_evac(b, c):
                    b, c = at(b, c)
                    w = DCA_ROW if c == LAST else P
                    act.wait_ge(s["tr"], done(b, c))
                    act.wait_ge(s["klo"], before(b, c))
                    nc.scalar.activation(k32[:, buf(c), :, 0:w],
                                         psum[:, TR_BANK, :].rearrange("p (g t) -> p g t", g=GROUPS)[:, :, 0:w],
                                         ACT.Identity, scale=g.cols[:, 2:3], bias=g.cols[:, 3:4]).then_inc(s["ke"], 1)

                def v_evac(b, c):
                    b, c = at(b, c)
                    bank = psum[:, V_BANK, :].rearrange("p (q n) -> p q n", q=PAIRS)
                    act.wait_ge(s["vp"], done(b, c))
                    act.wait_ge(s["pv"], before(b, c))
                    if c == LAST:
                        nc.scalar.copy(g.v_last[0:DCA_ROW, :, 0:PW - 1], bank[0:DCA_ROW]).then_inc(s["ve"], 1)
                    else:
                        nc.scalar.copy(g.v[:, buf(c), :, 0:PW - 1], bank).then_inc(s["ve"], 1)

                def seed(b, c):
                    b, c = at(b, c)
                    act.wait_ge(s["krd"], done(b, c))
                    act.wait_ge(s["krs"], before(b, c))
                    rsqrt_seed(nc, act, kseed[:, buf(c)], klog[:, buf(c)], ss[:, buf(c)], g.cols[:, 8:9], s["klog"],
                               done(b, c)).then_inc(s["kseed"], 1)

                def exps(b, c):
                    b, c = at(b, c)
                    act.wait_ge(s["sc"], done(b, c))
                    act.wait_ge(s["pv"], before(b, c))
                    nc.scalar.activation(probs[:, buf(c), :], psum[:, S_BANK:S_BANK + 2, :].rearrange("p a n -> p (a n)"),
                                         ACT.Exp, scale=SCALE).then_inc(s["ex"], 1)

                def o_evac(b):
                    act.wait_ge(s["pv"], done(b, LAST))
                    act.wait_ge(s["on"], b * 1 + 1)
                    for bank, (lo, hi) in enumerate(((0, 3), (3, 6), (6, PAIRS))):
                        last = nc.scalar.copy(o_sb[:, lo:hi, :],
                                              psum[:, O_BANK + bank, 0:(hi - lo) * 2 * PW]
                                              .rearrange("p (q n) -> p q n", n=2 * PW))
                    last.then_inc(s["oe"], 1)

                def ctx_evac(b):
                    act.wait_ge(s["ct"], b + 1)
                    nc.scalar.copy(g.ctxT[:, :, :, bass.ds(b * SQ, SQ)],
                                   psum[:, TR_BANK, 0:2 * P].rearrange("p (g j q) -> p g j q", g=2, j=2)).then_inc(s["ce"], 1)

                def first(guarded):
                    y_high(0, 0)
                    y_high(0, 1)
                    y_high(0, 2)
                    v_evac(0, 0)
                    seed(0, 0)
                    k_evac(0, 0)
                    v_evac(0, 1)
                    seed(0, 1)
                    exps(0, 0)

                def steps(b, room, guarded):
                    for c in range(CH):
                        if ahead(c, 3, room):
                            y_high(b, c + 3)
                        if ahead(c, 1, room):
                            k_evac(b, c + 1)
                        if ahead(c, 2, room):
                            v_evac(b, c + 2)
                            seed(b, c + 2)
                        if c == LAST:
                            o_evac(b)
                        if ahead(c, 1, room):
                            exps(b, c + 1)
                        if c == 2:
                            ctx_evac(b)

                batches(act, first, steps)
                ctx_evac(B)

            @block.gpsimd
            def _(pool):
                for stage in ("ylo", "ksq"):
                    pool.sem_inc(s[stage], CH)
                pool.sem_inc(s["on"], 1)

                def y_low(b, c):
                    b, c = at(b, c)
                    w = min(P, SM - c * P)
                    pool.wait_ge(s["yhi"], done(b, c))
                    pool.wait_ge(s["vp"], before(b, c))
                    nc.gpsimd.tensor_tensor(g.y_lo[:, buf(c), :, 0:w], y[:, :, c * P:c * P + w],
                                            g.y_hi[:, buf(c), :, 0:w].bitcast(F32), ALU.subtract).then_inc(s["ylo"], 1)

                def square(b, c):
                    b, c = at(b, c)
                    pool.wait_ge(s["kb"], done(b, c))
                    pool.wait_ge(s["krd"], before(b, c))
                    nc.gpsimd.tensor_tensor(sq[:, buf(c)], kc[:, buf(c)], kc[:, buf(c)], ALU.mult).then_inc(s["ksq"], 1)

                def normalise(b):
                    pool.wait_ge(s["rc"], b + 1)
                    pool.wait_ge(s["ct"], b + 1)
                    for j in range(2):
                        rows = slice(j * SQ, (j + 1) * SQ)
                        for n, dst in enumerate((g.ctx, od)):
                            nc.gpsimd.tensor_tensor(dst[rows], o_sb[rows, :, n * PW + j * HD:n * PW + (j + 1) * HD],
                                                    rinv[rows, :, n:n + 1].to_broadcast([SQ, PAIRS, HD]),
                                                    ALU.mult).then_inc(s["onp"], 1)
                    pool.wait_ge(s["onp"], b * 4 + 4)
                    nc.gpsimd.tensor_tensor(g.ctx[:], g.ctx[:], od[:], ALU.add).then_inc(s["on"], 1)

                def first(guarded):
                    y_low(0, 0)
                    y_low(0, 1)
                    square(0, 0)
                    y_low(0, 2)
                    square(0, 1)

                def steps(b, room, guarded):
                    for c in range(CH):
                        if ahead(c, 3, room):
                            y_low(b, c + 3)
                        if ahead(c, 2, room):
                            square(b, c + 2)
                        if c == LAST:
                            normalise(b)

                batches(pool, first, steps)

            @block.vector
            def _(dve):
                for stage in ("kb", "krd", "kn1", "kn2", "krs", "km", "khi", "klo"):
                    dve.sem_inc(s[stage], CH)
                dve.wait_ge(s["select"], 16)
                nc.vector.tensor_copy(select[:], select_raw[:]).then_inc(s["selected"], 1)

                def k_bias(b, c):
                    b, c = at(b, c)
                    dve.wait_ge(s["kp"], done(b, c))
                    dve.wait_ge(s["km"], before(b, c))
                    nc.vector.tensor_tensor(kc[:, buf(c)], psum[:, K_BANK, :], g.bk[:], ALU.add).then_inc(s["kb"], 1)

                def k_reduce(b, c):
                    b, c = at(b, c)
                    dve.wait_ge(s["ksq"], done(b, c))
                    dve.wait_ge(s["krs"], before(b, c))
                    nc.vector.tensor_reduce(ss[:, buf(c)], head_view(sq[:, buf(c)]), AX_X, ALU.add).then_inc(s["krd"], 1)

                def k_norm(b, c):
                    b, c = at(b, c)
                    dve.wait_ge(s["kseed"], done(b, c))
                    rsqrt_refine(nc, dve, kr[:, buf(c)], ktmp[:, buf(c)], ss[:, buf(c)], HD * HEAD_EPS, kseed[:, buf(c)],
                                 s["kn1"], s["kn2"], done(b, c)).then_inc(s["krs"], 1)
                    dve.wait_ge(s["krs"], done(b, c))
                    dve.wait_ge(s["tr"], before(b, c))
                    nc.vector.scalar_tensor_tensor(out=head_view(kn[:, buf(c)]), in0=head_view(kc[:, buf(c)]),
                                                   scalar=HD ** 0.5, in1=spread(kr[:, buf(c)], HD),
                                                   op0=ALU.mult, op1=ALU.mult).then_inc(s["km"], 1)

                def k_split(b, c):
                    b, c = at(b, c)
                    w = DCA_ROW if c == LAST else P
                    src = k32[:, buf(c), :, 0:w]
                    hi, lo = g.k_hi[:, buf(c), :, 0:w], g.k_lo[:, buf(c), :, 0:w]
                    dve.wait_ge(s["ke"], done(b, c))
                    dve.wait_ge(s["sc"], before(b, c))
                    nc.vector.tensor_copy(hi, src).then_inc(s["khi"], 1)
                    dve.wait_ge(s["khi"], done(b, c))
                    nc.vector.tensor_tensor(lo, src, hi.bitcast(F32), ALU.subtract).then_inc(s["klo"], 1)

                def queries(b, guarded):
                    dve.wait_ge(s["sc"], done(b, -1))
                    blocks = [(slice(i * HD, (i + 1) * HD), slice(i * SQ, (i + 1) * SQ)) for i in range(4)]
                    for rows, at in blocks:
                        nc.vector.tensor_copy(g.qbd_hi[rows, :, at], g.q[rows, :, bass.ds(b * SQ, SQ)]).then_inc(s["qb"], 1)
                    dve.wait_ge(s["qb"], b * parts(guarded) + 4)
                    for rows, at in blocks:
                        nc.vector.tensor_tensor(g.qbd_lo[rows, :, at], g.q[rows, :, bass.ds(b * SQ, SQ)],
                                                g.qbd_hi[rows, :, at].bitcast(F32), ALU.subtract).then_inc(s["qb"], 1)
                    if guarded:
                        dve.wait_ge(s["shift"], b * 16 + 16)
                        nc.vector.tensor_copy(shift[:], shift_raw[:]).then_inc(s["qb"], 1)

                def second_keys(b):
                    dve.wait_ge(s["sc"], done(b, -1))
                    hi, lo = (k[:, 2, :, DCA_ROW:DCA_ROW + DCA] for k in (g.k_hi, g.k_lo))
                    kd = g.kd[:, :, bass.ds(b * DCA, DCA)]
                    nc.vector.tensor_copy(hi, kd).then_inc(s["kd"], 1)
                    dve.wait_ge(s["kd"], b * 2 + 1)
                    nc.vector.tensor_tensor(lo, kd, hi.bitcast(F32), ALU.subtract).then_inc(s["kd"], 1)

                def first(guarded):
                    queries(0, guarded)
                    k_bias(0, 0)
                    k_reduce(0, 0)
                    k_norm(0, 0)
                    k_bias(0, 1)
                    k_split(0, 0)
                    k_reduce(0, 1)
                    k_norm(0, 1)

                def steps(b, room, guarded):
                    for c in range(CH):
                        if c == LAST and room:
                            queries(b + 1, guarded)
                        if ahead(c, 2, room):
                            k_bias(b, c + 2)
                        if ahead(c, 1, room):
                            k_split(b, c + 1)
                        if ahead(c, 2, room):
                            k_reduce(b, c + 2)
                            k_norm(b, c + 2)
                        if c == 5:
                            second_keys(b)
                        if c == LAST:
                            dve.wait_ge(s["oe"], b + 2)
                            nc.vector.reciprocal(rinv[:], o_sb[:, :, PW - 1:2 * PW:PW]).then_inc(s["rc"], 1)

                batches(dve, first, steps)

            @block.tensor
            def _(pe):
                for stage in ("kp", "vp", "tr", "sc", "pv"):
                    pe.sem_inc(s[stage], CH)

                def project(b, c, bank, w_hi, w_lo, free, stage):
                    b, c = at(b, c)
                    pe.wait_ge(s["yhi"], done(b, c))
                    pe.wait_ge(s["ylo"], done(b, c))
                    pe.wait_ge(s[free], done(b, c - 1))
                    split_product(pe, psum[:, bank, :],
                                  [(g.y_hi[:, buf(c), k, :], g.y_lo[:, buf(c), k, :], w_hi[:, k, :], w_lo[:, k, :])
                                   for k in range(KC)]).then_inc(s[stage], 1)

                def keys(b, c):
                    project(b, c, K_BANK, g.wk_hi, g.wk_lo, "kb", "kp")

                def values(b, c):
                    project(b, c, V_BANK, g.wv_hi, g.wv_lo, "ve", "vp")

                def turn(b, c):
                    b, c = at(b, c)
                    pe.wait_ge(s["km"], done(b, c))
                    pe.wait_ge(s["ke"], done(b, c - 1))
                    if c == 4:
                        pe.wait_ge(s["ce"], b + 1)
                    transposes(pe, psum[:, TR_BANK, :], kn[:, buf(c), :], g.ident[:]).then_inc(s["tr"], 1)

                def scores(b, c, guarded):
                    b, c = at(b, c)
                    pe.wait_ge(s["khi"], done(b, c))
                    pe.wait_ge(s["klo"], done(b, c))
                    pe.wait_ge(s["ex"], done(b, c - 1))
                    if c == 0:
                        pe.wait_ge(s["qb"], b * parts(guarded) + parts(guarded))
                        pe.wait_ge(s["selected"], 1)
                    if c == LAST:
                        pe.wait_ge(s["kd"], b * 2 + 2)
                    for n in range(GROUPS):
                        out = psum[:, S_BANK + n // 2, (n % 2) * 4 * SQ:(n % 2 + 1) * 4 * SQ]
                        less = [(select[:, int(c == LAST), :], shift[:, n * 4 * SQ:(n + 1) * 4 * SQ])] if guarded else []
                        last = split_product(pe, out, [(g.k_hi[:, buf(c), n, :], g.k_lo[:, buf(c), n, :],
                                                        g.qbd_hi[:, n, :], g.qbd_lo[:, n, :])], less)
                    last.then_inc(s["sc"], 1)

                def weighted(b, c):
                    pe.wait_ge(s["ex"], done(b, c))
                    pe.wait_ge(s["ve"], done(b, c))
                    if c == 0:
                        pe.wait_ge(s["oe"], b + 1)
                    if c == LAST:
                        pe.wait_ge(s["vd"], b * 16 + 16)
                    for p in range(PAIRS):
                        v = g.v_last[:, p, :] if c == LAST else g.v[:, buf(c), p, :]
                        last = pe.matmul(o_bank[p][:, 0:v.shape[1]], probs[:, buf(c), p * P:(p + 1) * P], v,
                                         start=(c == 0 and p % 3 == 0), stop=(c == LAST), skip_group_check=True)
                    last.then_inc(s["pv"], 1)

                def turn_ctx(b):
                    pe.wait_ge(s["on"], b + 1)
                    if isinstance(b, int) and b == B:
                        pe.wait_ge(s["ke"], done(B - 1, LAST))
                    else:
                        pe.wait_ge(s["ke"], done(b, 3))
                    transposes(pe, psum[:, TR_BANK, :], g.ctx[:].rearrange("p q d -> p (q d)"), g.ident[:],
                               2).then_inc(s["ct"], 1)

                def first(guarded):
                    keys(0, 0)
                    values(0, 0)
                    keys(0, 1)
                    turn(0, 0)
                    values(0, 1)
                    scores(0, 0, guarded)

                def steps(b, room, guarded):
                    for c in range(CH):
                        if ahead(c, 2, room):
                            keys(b, c + 2)
                        if ahead(c, 1, room):
                            turn(b, c + 1)
                        if ahead(c, 2, room):
                            values(b, c + 2)
                        weighted(b, c)
                        if ahead(c, 1, room):
                            scores(b, c + 1, guarded)
                        if c == 2:
                            turn_ctx(b)

                batches(pe, first, steps)
                turn_ctx(B)


def self_attention(nc, io, g, psum):
    VW = HD + 1
    OP, TR, QB, KB, SB, PB = 0, 1, 2, 3, 4, 6

    with ExitStack() as ctx:
        def sb(name, shape, dt=F32):
            return ctx.enter_context(nc.sbuf_tensor(name, shape, dt))

        s = Sems(nc, ctx, "sa")
        wo, wq, wk, wo2 = g.wo, g.sa_wq, g.sa_wk, g.sa_wo
        wv = sb("sa_wv", [P, KD, P])
        mask = sb("mask", [P, SQ])
        cx = sb("cx", [P, 2, KD, P])
        t1 = sb("t1", [P, 2, D])
        st = sb("sa_st", [P, 2, 6])
        mv = sb("sa_mv", [P, 2, 2])
        rs = sb("sa_rs", [P, 2, 1])
        rlog = sb("sa_rlog", [P, 2, 1])
        rseed = sb("sa_rseed", [P, 2, 1])
        rtmp = sb("sa_rtmp", [P, 2, 1])
        xn = sb("sa_xn", [P, 2, D])
        xT = sb("sa_xT", [P, 2, KD, P])
        qT = sb("sa_qT", [P, 2, GROUPS, P])
        kT = sb("sa_kT", [P, 2, KV, 2, 4, SQ])
        vv = sb("sa_v", [P, 2, KV, VW])
        sm = sb("sa_s", [P, 2, H, SQ])
        mx = sb("sa_mx", [P, 2, H])
        pr = sb("sa_p", [P, 2, H, P])
        pT = sb("sa_pT", [P, 2, H, P])
        ri = sb("sa_ri", [P, 2, H])
        co = sb("sa_o", [P, 2, D])
        cT = sb("sa_oT", [P, 2, KD, P])

        def done(i, u):
            return i * 2 + (u + 3)

        def before(i, u):
            return i * 2 + (u + 1)

        def last_one(i, u):
            return i * 2 + (u + 2)

        with nc.Block() as block:
            @block.sync
            def _(sp):
                sp.dma_start(mask[:], io["mask"]).then_inc(s["mask"], 16)
                sp.dma_start(wv[:], io["sa_wv"].rearrange("(k p) n -> p k n", p=P)).then_inc(s["wv"], 16)

            @block.gpsimd
            def _(pool):
                nc.gpsimd.memset(vv[:], 1.0).then_inc(s["set"], 1)
                nc.gpsimd.memset(pr[:], 0.0).then_inc(s["set"], 1)
                nc.gpsimd.memset(kT[:], 0.0).then_inc(s["set"], 1)

            @block.scalar
            def _(act):
                act.preload_act_table_set(TABLES)
                for stage in ("cx", "xe", "qe", "ve", "ex", "pe0", "pe1", "pe2", "pe3", "cte", "rlog", "rseed"):
                    act.sem_inc(s[stage], 2)
                act.wait_ge(s["set"], 3)

                def ctx_chunk(i, u):
                    act.wait_ge(s["op"], before(i, u))
                    nc.scalar.copy(cx[:, u].rearrange("p (g j) t -> p g j t", g=2),
                                   g.ctxT[:, :, :, bass.ds((i * 2 + u) * P + SQ, P)]).then_inc(s["cx"], 1)

                def seed(i, u):
                    act.wait_ge(s["ba"], done(i, u))
                    act.wait_ge(s["rs"], before(i, u))
                    rsqrt_seed(nc, act, rseed[:, u], rlog[:, u], mv[:, u, 1:2], g.cols[:, 9:10], s["rlog"],
                               done(i, u)).then_inc(s["rseed"], 1)

                def x_evac(i, u):
                    act.wait_ge(s["trx"], done(i, u))
                    act.wait_ge(s["vp"], before(i, u))
                    nc.scalar.copy(xT[:, u], psum[:, TR, :].rearrange("p (k t) -> p k t", k=KD)).then_inc(s["xe"], 1)

                def qv_evac(i, u):
                    act.wait_ge(s["qp"], done(i, u))
                    act.wait_ge(s["sp"], before(i, u))
                    nc.scalar.copy(qT[:, u], psum[:, QB, :].rearrange("p (g t) -> p g t", g=GROUPS)).then_inc(s["qe"], 1)
                    act.wait_ge(s["vp"], done(i, u))
                    act.wait_ge(s["pv"], before(i, u))
                    nc.scalar.copy(vv[:, u, :, 0:HD], psum[:, OP, 0:P].rearrange("p (h d) -> p h d", h=KV)).then_inc(s["ve"], 1)

                def exps(i, u):
                    act.wait_ge(s["sb"], done(i, u))
                    act.wait_ge(s["pt3"], before(i, u))
                    for j in range(2):
                        rows = slice(j * SQ, (j + 1) * SQ)
                        last = nc.scalar.activation(pr[rows, u, :, rows], sm[rows, u], ACT.Exp)
                    last.then_inc(s["ex"], 1)

                def p_evac(i, u, n):
                    act.wait_ge(s[f"pt{n}"], done(i, u))
                    act.wait_ge(s["pv"], before(i, u))
                    nc.scalar.copy(pT[:, u, 4 * n:4 * n + 4, :],
                                   psum[:, (QB, KB)[n % 2], :].rearrange("p (h t) -> p h t", h=4)).then_inc(s[f"pe{n}"], 1)

                def o_evac(i, u):
                    act.wait_ge(s["trc"], done(i, u))
                    act.wait_ge(s["op2"], before(i, u))
                    nc.scalar.copy(cT[:, u], psum[:, TR, :].rearrange("p (k t) -> p k t", k=KD)).then_inc(s["cte"], 1)

                with act.Fori(0, NT // 2) as i:
                    for u in range(2):
                        ctx_chunk(i, u)
                    for u in range(2):
                        seed(i, u)
                    for u in range(2):
                        x_evac(i, u)
                    for u in range(2):
                        qv_evac(i, u)
                    for u in range(2):
                        exps(i, u)
                        for n in range(4):
                            p_evac(i, u, n)
                    for u in range(2):
                        o_evac(i, u)

            @block.vector
            def _(dve):
                for stage in ("tp", "x1", "bs", "ba", "rn1", "rn2", "rs", "xn", "ke", "sm", "mx", "sb", "ri", "co", "x2"):
                    dve.sem_inc(s[stage], 2)
                dve.wait_ge(s["mask"], 16)
                dve.wait_ge(s["set"], 3)

                def residual(i, u):
                    dve.wait_ge(s["op"], done(i, u))
                    dve.wait_ge(s["x1"], before(i, u))
                    nc.vector.tensor_tensor(t1[:, u], psum[:, OP, :], g.bo[:], ALU.add).then_inc(s["tp"], 1)
                    dve.wait_ge(s["tp"], done(i, u))
                    x = g.x[:, i * 2 + u, :]
                    nc.vector.tensor_tensor(x, x, t1[:, u], ALU.add).then_inc(s["x1"], 1)

                def stats(i, u):
                    dve.wait_ge(s["x1"], done(i, u))
                    dve.wait_ge(s["ba"], before(i, u))
                    dve.sem_inc(s["gate"], 1)
                    nc.vector.bn_stats(st[:, u], g.x[:, i * 2 + u, :]).then_inc(s["bs"], 1)
                    dve.wait_ge(s["bs"], done(i, u))
                    dve.wait_ge(s["xn"], before(i, u))
                    dve.sem_inc(s["gate"], 1)
                    nc.vector.bn_aggr(mv[:, u], st[:, u]).then_inc(s["ba"], 1)

                def norm(i, u):
                    dve.wait_ge(s["rseed"], done(i, u))
                    rsqrt_refine(nc, dve, rs[:, u], rtmp[:, u], mv[:, u, 1:2], LN_EPS, rseed[:, u],
                                 s["rn1"], s["rn2"], done(i, u)).then_inc(s["rs"], 1)
                    dve.wait_ge(s["rs"], done(i, u))
                    dve.wait_ge(s["trx"], before(i, u))
                    nc.vector.tensor_scalar(xn[:, u], g.x[:, i * 2 + u, :], mv[:, u, 0:1], rs[:, u],
                                            ALU.subtract, ALU.mult).then_inc(s["xn"], 1)

                def keys(i, u):
                    dve.wait_ge(s["kp"], done(i, u))
                    dve.wait_ge(s["sp"], before(i, u))
                    bank = psum[:, KB, :].rearrange("p (h b t) -> p h b t", h=KV, b=2)
                    for n in range(4):
                        rows = slice(n * HD, (n + 1) * HD)
                        last = nc.vector.tensor_copy(kT[rows, u, :, :, n, :], bank[rows])
                    last.then_inc(s["ke"], 1)

                def softmax(i, u):
                    dve.wait_ge(s["sp"], done(i, u))
                    dve.wait_ge(s["ex"], before(i, u))
                    nc.vector.scalar_tensor_tensor(
                        out=sm[:, u], in0=psum[:, SB:SB + 2, :].rearrange("p a (h t) -> p (a h) t", t=SQ), scalar=SCALE,
                        in1=mask[:].unsqueeze(1).to_broadcast([P, H, SQ]), op0=ALU.mult, op1=ALU.add).then_inc(s["sm"], 1)
                    dve.wait_ge(s["sm"], done(i, u))
                    dve.wait_ge(s["sb"], before(i, u))
                    nc.vector.tensor_reduce(mx[:, u], sm[:, u], AX_X, ALU.max).then_inc(s["mx"], 1)
                    dve.wait_ge(s["mx"], done(i, u))
                    nc.vector.tensor_tensor(sm[:, u], sm[:, u], spread(mx[:, u], SQ), ALU.subtract).then_inc(s["sb"], 1)

                def normalise(i, u):
                    dve.wait_ge(s["pv"], done(i, u))
                    dve.wait_ge(s["co"], before(i, u))
                    for a in range(2):
                        bank = psum[:, PB + a, 0:8 * VW].rearrange("p (h n) -> p h n", n=VW)
                        last = nc.vector.reciprocal(ri[:, u, 8 * a:8 * a + 8], bank[:, :, HD])
                    last.then_inc(s["ri"], 1)
                    dve.wait_ge(s["ri"], done(i, u))
                    dve.wait_ge(s["trc"], before(i, u))
                    for a in range(2):
                        bank = psum[:, PB + a, 0:8 * VW].rearrange("p (h n) -> p h n", n=VW)
                        last = nc.vector.tensor_tensor(head_view(co[:, u])[:, 8 * a:8 * a + 8, :], bank[:, :, 0:HD],
                                                       spread(ri[:, u, 8 * a:8 * a + 8], HD), ALU.mult)
                    last.then_inc(s["co"], 1)

                def residual2(i, u):
                    dve.wait_ge(s["op2"], done(i, u))
                    x = g.x[:, i * 2 + u, :]
                    nc.vector.tensor_tensor(x, x, psum[:, OP, :], ALU.add).then_inc(s["x2"], 1)

                with dve.Fori(0, NT // 2) as i:
                    for u in range(2):
                        residual(i, u)
                    for u in range(2):
                        stats(i, u)
                    for u in range(2):
                        norm(i, u)
                    for u in range(2):
                        keys(i, u)
                        softmax(i, u)
                    for u in range(2):
                        normalise(i, u)
                    for u in range(2):
                        residual2(i, u)

            @block.tensor
            def _(pe):
                for stage in ("op", "trx", "qp", "kp", "vp", "sp", "pt0", "pt1", "pt2", "pt3", "pv", "trc", "op2"):
                    pe.sem_inc(s[stage], 2)

                def out_product(i, u):
                    pe.wait_ge(s["cx"], done(i, u))
                    if u:
                        pe.wait_ge(s["tp"], last_one(i, u))
                    else:
                        pe.wait_ge(s["x2"], last_one(i, u))
                    product(pe, psum[:, OP, :], cx[:, u], wo[:]).then_inc(s["op"], 1)

                def turn_x(i, u):
                    pe.wait_ge(s["xn"], done(i, u))
                    if u:
                        pe.wait_ge(s["xe"], last_one(i, u))
                    else:
                        pe.wait_ge(s["cte"], last_one(i, u))
                    transposes(pe, psum[:, TR, :], xn[:, u, :], g.ident[:]).then_inc(s["trx"], 1)

                def heads_T(bank, w, u):
                    for n in range(GROUPS):
                        for k in range(KD):
                            last = pe.matmul(psum[:, bank, n * P:(n + 1) * P], w[:, k, n * P:(n + 1) * P], xT[:, u, k, :],
                                             start=(k == 0), stop=(k == KD - 1))
                    return last

                def qkv(i, u):
                    pe.wait_ge(s["xe"], done(i, u))
                    if u:
                        pe.wait_ge(s["qe"], last_one(i, u))
                        pe.wait_ge(s["ke"], last_one(i, u))
                        pe.wait_ge(s["ve"], last_one(i, u))
                    else:
                        pe.wait_ge(s["pe2"], last_one(i, u))
                        pe.wait_ge(s["pe3"], last_one(i, u))
                        pe.wait_ge(s["tp"], done(i, 1))
                    heads_T(QB, wq, u).then_inc(s["qp"], 1)
                    heads_T(KB, wk, u).then_inc(s["kp"], 1)
                    product(pe, psum[:, OP, 0:P], xT[:, u], wv[:]).then_inc(s["vp"], 1)

                def scores(i, u):
                    pe.wait_ge(s["qe"], done(i, u))
                    pe.wait_ge(s["ke"], done(i, u))
                    pe.wait_ge(s["sm"], last_one(i, u))
                    for n in range(GROUPS):
                        for j in range(2):
                            rows = slice(j * SQ, (j + 1) * SQ)
                            last = pe.matmul(psum[rows, SB + n // 2, (n % 2) * 4 * SQ:(n % 2 + 1) * 4 * SQ],
                                             qT[:, u, n, rows], kT[:, u, n, j].rearrange("p a t -> p (a t)"),
                                             start=True, stop=True)
                    last.then_inc(s["sp"], 1)

                def turn_probs(i, u):
                    pe.wait_ge(s["ex"], done(i, u))
                    for n in range(4):
                        if n >= 2:
                            pe.wait_ge(s[f"pe{n - 2}"], done(i, u))
                        elif u:
                            pe.wait_ge(s[f"pe{n + 2}"], last_one(i, u))
                        else:
                            pe.wait_ge(s[("qe", "ke")[n]], done(i, 1))
                        transposes(pe, psum[:, (QB, KB)[n % 2], :],
                                   pr[:, u, 4 * n:4 * n + 4, :].rearrange("p h t -> p (h t)"), g.ident[:]).then_inc(s[f"pt{n}"], 1)

                def weighted(i, u):
                    pe.wait_ge(s["ve"], done(i, u))
                    pe.wait_ge(s["co"], last_one(i, u))
                    for h in range(H):
                        if h % 4 == 0:
                            pe.wait_ge(s[f"pe{h // 4}"], done(i, u))
                        last = pe.matmul(psum[:, PB + h // 8, (h % 8) * VW:(h % 8 + 1) * VW], pT[:, u, h, :],
                                         vv[:, u, h // 4, :], start=True, stop=True)
                    last.then_inc(s["pv"], 1)

                def turn_out(i, u):
                    pe.wait_ge(s["co"], done(i, u))
                    if u:
                        pe.wait_ge(s["cte"], last_one(i, u))
                    else:
                        pe.wait_ge(s["xe"], done(i, 1))
                    transposes(pe, psum[:, TR, :], co[:, u, :], g.ident[:]).then_inc(s["trc"], 1)

                def out_product2(i, u):
                    pe.wait_ge(s["cte"], done(i, u))
                    if u:
                        pe.wait_ge(s["x2"], last_one(i, u))
                    else:
                        pe.wait_ge(s["ve"], done(i, 1))
                    product(pe, psum[:, OP, :], cT[:, u], wo2[:]).then_inc(s["op2"], 1)

                pe.wait_ge(s["wv"], 16)
                with pe.Fori(0, NT // 2) as i:
                    for stage in (out_product, turn_x):
                        for u in range(2):
                            stage(i, u)
                    for u in range(2):
                        qkv(i, u)
                        scores(i, u)
                    for u in range(2):
                        turn_probs(i, u)
                        weighted(i, u)
                    for stage in (turn_out, out_product2):
                        for u in range(2):
                            stage(i, u)


def experts(nc, io, g, psum):
    UP, TR, DN = 2, 4, 6

    with ExitStack() as ctx:
        def sb(name, shape, dt=F32):
            return ctx.enter_context(nc.sbuf_tensor(name, shape, dt))

        s = Sems(nc, ctx, "moe")
        wr = sb("wr", [P, KD, E_])
        iota = sb("iota", [P, E_])
        st = sb("moe_st", [P, NT, 6])
        mv = sb("moe_mv", [P, NT, 2])
        rs = sb("moe_rs", [P, NT])
        rlog = sb("moe_rlog", [P, NT])
        rseed = sb("moe_rseed", [P, NT])
        rtmp = sb("moe_rtmp", [P, NT])
        xn = sb("moe_xn", [P, 2, D])
        xT = sb("moe_xT", [P, 2, KD, P])
        x_hi = sb("moe_xhi", [P, NT, KD, P], F32R)
        x_lo = sb("moe_xlo", [P, NT, KD, P], F32R)
        sc = sb("moe_sc", [P, NT, E_])
        top = sb("moe_top", [P, NT, 8])
        idx = sb("moe_idx", [P, NT, 8], U32)
        idf = sb("moe_idf", [P, NT, 2])
        gap = sb("moe_gap", [P, NT])
        ex = sb("moe_ex", [P, NT])
        ex1 = sb("moe_ex1", [P, NT])
        w12 = sb("moe_w12", [P, 2, NT])
        pick = sb("moe_pick", [P, 2, NT, E_])
        wt = sb("moe_wt", [P, NT, E_])
        raw = sb("moe_raw", [P, 3, KD * EW])
        wg_hi = sb("wg_hi", [P, 2, KD, EW], F32R)
        wg_lo = sb("wg_lo", [P, 2, KD, EW], F32R)
        wu_hi = sb("wu_hi", [P, 2, KD, EW], F32R)
        wu_lo = sb("wu_lo", [P, 2, KD, EW], F32R)
        wd_hi = sb("wd_hi", [P, 2, EC, D], F32R)
        wd_lo = sb("wd_lo", [P, 2, EC, D], F32R)
        act_g = sb("moe_g", [P, 2, EW])
        hid = sb("moe_h", [P, 2, EW])
        h_hi = sb("moe_hhi", [P, 2, EC, P], F32R)
        h_lo = sb("moe_hlo", [P, 2, EC, P], F32R)
        weights = ((wg_hi, wg_lo), (wu_hi, wu_lo), (wd_hi, wd_lo))

        def chunk(i, v, t):
            return i * (2 * NT) + (v * NT + t + 3)

        with nc.Block() as block:
            @block.sync
            def _(sp):
                sp.dma_start(wr[:], io["wr"].rearrange("(k p) n -> p k n", p=P)).then_inc(s["wr"], 16)
                sp.dma_start(iota[:], io["iota"].partition_broadcast(P)).then_inc(s["wr"], 16)
                with sp.Fori(0, EP) as e:
                    for n, name in enumerate(("wg", "wu")):
                        sp.wait_ge(s["wlo"], e * 3 + (n + 1))
                        sp.dma_start(raw[:, n, :].rearrange("p (k n) -> p k n", k=KD),
                                     io[name].rearrange("(k p) n -> p k n", p=P)[:, :, bass.ds(e * EW, EW)])\
                            .then_inc(s[name], 16)
                    sp.wait_ge(s["wlo"], e * 3 + 3)
                    sp.dma_start(raw[:, 2, :].rearrange("p (k n) -> p k n", k=EC),
                                 io["wd"][bass.ds(e * EW, EW), :].rearrange("(k p) n -> p k n", p=P)).then_inc(s["wd"], 16)
                for t in range(NT):
                    sp.wait_ge(s["ya"], chunk(1, 1, t))
                    sp.dma_start(io["out"].rearrange("(t p) d -> p t d", p=P)[:, t, :], g.x[:, t, :]).then_inc(s["out"], 16)
                sp.wait_ge(s["out"], 16 * NT)

            @block.gpsimd
            def _(pool):
                pool.sem_inc(s["wlo"], 3)
                with pool.Fori(0, EP // 2) as i:
                    for v in range(2):
                        for n, (hi, lo) in enumerate(weights):
                            pool.wait_ge(s["whi"], i * 6 + (v * 3 + n + 1))
                            nc.gpsimd.tensor_tensor(lo[:, v].rearrange("p k n -> p (k n)"), raw[:, n, :],
                                                    hi[:, v].rearrange("p k n -> p (k n)").bitcast(F32),
                                                    ALU.subtract).then_inc(s["wlo"], 1)

            @block.scalar
            def _(act):
                act.preload_act_table_set(TABLES)
                act.wait_ge(s["ba"], NT)
                rsqrt_seed(nc, act, rseed[:], rlog[:], mv[:, :, 1], g.cols[:, 9:10], s["rlog"], 1).then_inc(s["rseed"], 1)
                for t in range(NT):
                    u = t % 2
                    act.wait_ge(s["trx"], t + 1)
                    if t >= 2:
                        act.wait_ge(s["rp"], t - 1)
                        act.wait_ge(s["xlo"], t - 1)
                    nc.scalar.copy(xT[:, u], psum[:, u, :].rearrange("p (k t) -> p k t", k=KD)).then_inc(s["xe"], 1)
                    act.wait_ge(s["xe"], t + 1)
                    nc.scalar.copy(x_hi[:, t], xT[:, u]).then_inc(s["xhi"], 1)
                act.wait_ge(s["gap"], 1)
                nc.scalar.activation(ex[:], gap[:], ACT.Exp).then_inc(s["ex"], 1)
                for stage in ("sg", "hhi"):
                    act.sem_inc(s[stage], 2)
                act.preload_act_table(ACT.Silu)

                def silu(i, v, t):
                    act.wait_ge(s["gp"], chunk(i, v, t))
                    act.wait_ge(s["hd"], chunk(i, v, t - 2))
                    nc.scalar.activation(act_g[:, t % 2], psum[:, t % 2, 0:EW], ACT.Silu).then_inc(s["sg"], 1)

                def high(i, v, t):
                    act.wait_ge(s["trh"], chunk(i, v, t))
                    act.wait_ge(s["dp"], chunk(i, v, t - 2))
                    nc.scalar.copy(h_hi[:, t % 2], psum[:, TR + t % 2, 0:EW].rearrange("p (k t) -> p k t", k=EC)).then_inc(s["hhi"], 1)

                with act.Fori(0, EP // 2) as i:
                    for v in range(2):
                        for t in range(NT):
                            silu(i, v, t)
                            if t:
                                high(i, v, t - 1)
                        high(i, v, NT - 1)

            @block.vector
            def _(dve):
                for stage in ("hd", "hlo", "ya"):
                    dve.sem_inc(s[stage], 2)
                for t in range(NT):
                    nc.vector.bn_stats(st[:, t, :], g.x[:, t, :]).then_inc(s["bs"], 1)
                for t in range(NT):
                    dve.wait_ge(s["bs"], t + 1)
                    nc.vector.bn_aggr(mv[:, t, :], st[:, t, :]).then_inc(s["ba"], 1)
                dve.wait_ge(s["rseed"], 1)
                rsqrt_refine(nc, dve, rs[:], rtmp[:], mv[:, :, 1], LN_EPS, rseed[:], s["rn1"], s["rn2"], 1).then_inc(s["rs"], 1)
                dve.wait_ge(s["rs"], 1)
                for t in range(NT):
                    if t >= 2:
                        dve.wait_ge(s["trx"], t - 1)
                    nc.vector.tensor_scalar(xn[:, t % 2], g.x[:, t, :], mv[:, t, 0:1], rs[:, t:t + 1],
                                            ALU.subtract, ALU.mult).then_inc(s["xn"], 1)
                    if t:
                        dve.wait_ge(s["xhi"], t)
                        nc.vector.tensor_tensor(x_lo[:, t - 1], xT[:, (t - 1) % 2], x_hi[:, t - 1].bitcast(F32),
                                                ALU.subtract).then_inc(s["xlo"], 1)
                dve.wait_ge(s["xhi"], NT)
                nc.vector.tensor_tensor(x_lo[:, NT - 1], xT[:, (NT - 1) % 2], x_hi[:, NT - 1].bitcast(F32),
                                        ALU.subtract).then_inc(s["xlo"], 1)

                chain = [0]

                def link(ins):
                    chain[0] += 1
                    ins.then_inc(s["chain"], 1)
                    dve.wait_ge(s["chain"], chain[0])

                dve.wait_ge(s["rp"], NT)
                dve.wait_ge(s["wr"], 32)
                link(nc.vector.tensor_copy(sc[:], psum[:, 2, 0:NT * E_].rearrange("p (t e) -> p t e", t=NT)))
                for t in range(NT):
                    last = nc.vector.max(out=top[:, t, :], in_=sc[:, t, :])
                link(last)
                for t in range(NT):
                    last = nc.vector.max_index(out=idx[:, t, :], in_max=top[:, t, :], in_values=sc[:, t, :])
                link(last)
                link(nc.vector.tensor_copy(idf[:], idx[:, :, 0:2]))
                nc.vector.tensor_tensor(gap[:], top[:, :, 1], top[:, :, 0], ALU.subtract).then_inc(s["gap"], 1)
                dve.wait_ge(s["ex"], 1)
                link(nc.vector.tensor_scalar(ex1[:], ex[:], 1.0, None, ALU.add))
                link(nc.vector.reciprocal(w12[:, 0], ex1[:]))
                link(nc.vector.tensor_tensor(w12[:, 1], ex[:], w12[:, 0], ALU.mult))
                for n in range(2):
                    link(nc.vector.tensor_tensor(pick[:, n], iota[:].unsqueeze(1).to_broadcast([P, NT, E_]),
                                                 spread(idf[:, :, n], E_), ALU.is_equal))
                    link(nc.vector.tensor_tensor(pick[:, n], pick[:, n], spread(w12[:, n], E_), ALU.mult))
                link(nc.vector.tensor_tensor(wt[:], pick[:, 0], pick[:, 1], ALU.add))

                def weights_high(i, v):
                    for n, (hi, _) in enumerate(weights):
                        dve.wait_ge(s[("wg", "wu", "wd")[n]], i * 32 + (v * 16 + 16))
                        nc.vector.tensor_copy(hi[:, v].rearrange("p k n -> p (k n)"), raw[:, n, :]).then_inc(s["whi"], 1)

                def hidden(i, v, t):
                    dve.wait_ge(s["sg"], chunk(i, v, t))
                    dve.wait_ge(s["gp"], chunk(i, v, t))
                    dve.wait_ge(s["trh"], chunk(i, v, t - 2))
                    for n in range(2):
                        cols = slice(n * F, (n + 1) * F)
                        last = nc.vector.scalar_tensor_tensor(
                            out=hid[:, t % 2, cols], in0=act_g[:, t % 2, cols],
                            scalar=wt[:, t, bass.ds(i * 4 + (v * 2 + n), 1)],
                            in1=psum[:, UP + t % 2, cols], op0=ALU.mult, op1=ALU.mult)
                    last.then_inc(s["hd"], 1)

                def low(i, v, t):
                    dve.wait_ge(s["hhi"], chunk(i, v, t))
                    dve.wait_ge(s["dp"], chunk(i, v, t - 2))
                    nc.vector.tensor_tensor(h_lo[:, t % 2], psum[:, TR + t % 2, 0:EW].rearrange("p (k t) -> p k t", k=EC),
                                            h_hi[:, t % 2].bitcast(F32), ALU.subtract).then_inc(s["hlo"], 1)

                def add(i, v, t):
                    dve.wait_ge(s["dp"], chunk(i, v, t))
                    nc.vector.tensor_tensor(g.x[:, t, :], g.x[:, t, :], psum[:, DN + t % 2, :], ALU.add).then_inc(s["ya"], 1)

                with dve.Fori(0, EP // 2) as i:
                    for v in range(2):
                        weights_high(i, v)
                        for t in range(NT):
                            hidden(i, v, t)
                            if t:
                                low(i, v, t - 1)
                            if t >= 2:
                                add(i, v, t - 2)
                        low(i, v, NT - 1)
                        add(i, v, NT - 2)
                        add(i, v, NT - 1)

            @block.tensor
            def _(pe):
                for t in range(NT):
                    u = t % 2
                    pe.wait_ge(s["xn"], t + 1)
                    if t >= 2:
                        pe.wait_ge(s["xe"], t - 1)
                    transposes(pe, psum[:, u, :], xn[:, u, :], g.ident[:]).then_inc(s["trx"], 1)
                    if t == 0:
                        pe.wait_ge(s["wr"], 32)
                    pe.wait_ge(s["xe"], t + 1)
                    product(pe, psum[:, 2, t * E_:(t + 1) * E_], xT[:, u], wr[:]).then_inc(s["rp"], 1)
                for stage in ("gp", "trh", "dp"):
                    pe.sem_inc(s[stage], 2)
                pe.wait_ge(s["xlo"], NT)
                pe.wait_ge(s["chain"], 1)

                def gate_up(i, v, t):
                    pe.wait_ge(s["hd"], chunk(i, v, t - 2))
                    for bank, (hi, lo) in ((t % 2, weights[0]), (UP + t % 2, weights[1])):
                        last = split_product(pe, psum[:, bank, 0:EW],
                                             [(x_hi[:, t, k, :], x_lo[:, t, k, :], hi[:, v, k, :], lo[:, v, k, :])
                                              for k in range(KD)])
                    last.then_inc(s["gp"], 1)

                def down(i, v, t):
                    pe.wait_ge(s["hd"], chunk(i, v, t))
                    pe.wait_ge(s["hlo"], chunk(i, v, t - 2))
                    transposes(pe, psum[:, TR + t % 2, :], hid[:, t % 2, :], g.ident[:], EC).then_inc(s["trh"], 1)

                def down2(i, v, t):
                    pe.wait_ge(s["hhi"], chunk(i, v, t))
                    pe.wait_ge(s["hlo"], chunk(i, v, t))
                    pe.wait_ge(s["ya"], chunk(i, v, t - 2))
                    split_product(pe, psum[:, DN + t % 2, :],
                                  [(h_hi[:, t % 2, k, :], h_lo[:, t % 2, k, :], wd_hi[:, v, k, :], wd_lo[:, v, k, :])
                                   for k in range(EC)]).then_inc(s["dp"], 1)

                with pe.Fori(0, EP // 2) as i:
                    for v in range(2):
                        pe.wait_ge(s["wlo"], i * 6 + (v * 3 + 6))
                        for t in range(NT + 2):
                            if t < NT:
                                gate_up(i, v, t)
                            if 1 <= t <= NT:
                                down(i, v, t - 1)
                            if t >= 2:
                                down2(i, v, t - 2)


def build(nc, io):
    with ExitStack() as ctx:
        psum = ctx.enter_context(nc.psum_tensor("psum", [P, 8, 512], F32))

        class Shared:
            pass
        g = Shared()

        def sb(stack, name, shape, dt=F32):
            return stack.enter_context(nc.sbuf_tensor(name, shape, dt))

        g.x = sb(ctx, "x_sb", [P, NT, D])
        g.ident = sb(ctx, "ident_sb", [P, P])
        g.cols = sb(ctx, "cols_sb", [P, 10])
        with ExitStack() as out_ctx:
            g.bo = sb(out_ctx, "bo_sb", [P, D])
            g.ctxT = sb(out_ctx, "ctxT", [P, 2, 2, T + SQ])
            g.wo = sb(out_ctx, "xa_wo", [P, KD, D])
            g.sa_wq = sb(out_ctx, "sa_wq", [P, KD, D])
            g.sa_wk = sb(out_ctx, "sa_wk", [P, KD, D])
            g.sa_wo = sb(out_ctx, "sa_wo", [P, KD, D])
            g.landed = [out_ctx.enter_context(nc.semaphore(f"context_{n}")) for n in range(len(LANDING))]
            with ExitStack() as xa:
                g.guard = sb(xa, "guard", [1, 1], I32)
                g.bk = sb(xa, "bk_sb", [P, D])
                g.wk_hi = sb(xa, "wk_hi", [P, KC, D], F32R)
                g.wk_lo = sb(xa, "wk_lo", [P, KC, D], F32R)
                g.wv_hi = sb(xa, "wv_hi", [P, KC, D], F32R)
                g.wv_lo = sb(xa, "wv_lo", [P, KC, D], F32R)
                g.q = sb(xa, "q_sb", [P, GROUPS, T])
                g.kd = sb(xa, "kd_sb", [P, GROUPS, B * DCA])
                g.y = sb(xa, "y_sb", [P, KC, SM])
                g.qbd_hi = sb(xa, "qbd_hi", [P, GROUPS, 4 * SQ], F32R)
                g.qbd_lo = sb(xa, "qbd_lo", [P, GROUPS, 4 * SQ], F32R)
                g.y_hi = sb(xa, "y_hi", [P, 3, KC, P], F32R)
                g.y_lo = sb(xa, "y_lo", [P, 3, KC, P], F32R)
                g.k_hi = sb(xa, "k_hi", [P, 3, GROUPS, P], F32R)
                g.k_lo = sb(xa, "k_lo", [P, 3, GROUPS, P], F32R)
                g.v = sb(xa, "v_sb", [P, 2, PAIRS, PW])
                g.v_last = sb(xa, "v_last", [P, PAIRS, 2 * PW])
                g.ctx = sb(xa, "ctx_sb", [P, PAIRS, HD])
                prepare(nc, io, g, psum)
                score_maxima(nc, io, g, psum)
                cross_attention(nc, io, g, psum)
            self_attention(nc, io, g, psum)
        experts(nc, io, g, psum)


def kernel(**inputs):
    import numpy as np
    import concourse.bacc as bacc
    from concourse.bass_utils import run_bass_kernel_spmd

    a = {k: np.asarray(v) for k, v in inputs.items()}
    f32 = np.float32
    G2 = PAIRS // 4

    kv_w = np.concatenate([a["L0_xattn_Wk"], a["L0_xattn_Wv"]], 1).reshape(DC, H, 2, HD)
    kv_b = np.concatenate([a["L0_xattn_bk"], a["L0_xattn_bv"]]).reshape(H, 2, HD)
    dca_w = a["L0_xattn_Wkv_dca"].reshape(DC, 2, D)
    dca_b = a["L0_xattn_bkv_dca"].reshape(2, D)

    def by_pair(v):
        return v.reshape((G2, 4, 2, HD) + v.shape[1:]).swapaxes(1, 2).reshape((KD, P) + v.shape[1:])

    rows = np.arange(P)
    cols = np.stack([np.tile(a[f"L0_xattn_{n}"], 4) for n in ("qn_w", "qn_b", "kn_w", "kn_b", "kn_dca_w", "kn_dca_b")]
                    + [(rows < LM).astype(f32), ((rows >= DCA_ROW) & (rows < DCA_ROW + DCA)).astype(f32),
                       np.full(P, HD * HEAD_EPS, f32), np.full(P, LN_EPS, f32)], 1)
    context = a["ctx_1024"]
    arrays = {
        "x": a["x"].reshape(T, D),
        "y": context[:, :SM].transpose(0, 2, 1),
        "yd": context[:, SM:].transpose(2, 0, 1).reshape(DC, B * DCA),
        "wq": a["L0_xattn_Wq"], "bq": a["L0_xattn_bq"],
        "wk": kv_w[:, :, 0].reshape(DC, D), "wv": kv_w[:, :, 1].reshape(DC, D), "bk": kv_b[:, 0].reshape(D),
        "wkd": dca_w[:, 0], "wvd": dca_w[:, 1], "bkd": dca_b[0],
        "bv": np.concatenate([by_pair(kv_b[:, 1].reshape(D)), by_pair(dca_b[1])], 0).T,
        "wo": by_pair(a["L0_xattn_Wo"]), "bo": a["L0_xattn_bo"],
        "cols": cols,
        "norms": np.concatenate([a[f"L0_xattn_{n}"] for n in ("qn_w", "qn_b", "kn_w", "kn_b", "kn_dca_w", "kn_dca_b")])[None],
        "select": np.stack([np.ones(P), np.zeros(P), rows < DCA_ROW, rows >= DCA_ROW]).reshape(2, 2, P)
                    .swapaxes(0, 1).reshape(2, 2 * P).astype(f32),
        "ident": np.eye(P, dtype=f32),
        "mask": np.where(np.arange(SQ)[None] <= rows[:, None] % SQ, 0.0, MASKED).astype(f32),
        "iota": np.arange(E_, dtype=f32),
        "sa_wq": a["L0_attn_Wq"],
        "sa_wk": np.repeat(a["L0_attn_Wk"].reshape(D, KV, 1, HD), 4, 2).reshape(D, D),
        "sa_wv": a["L0_attn_Wv"], "sa_wo": a["L0_attn_Wo"],
        "wr": a["L0_ffn_w_gate_router"].T,
        "wg": a["L0_ffn_w_gate_proj"].transpose(2, 0, 1).reshape(D, E_ * F),
        "wu": a["L0_ffn_w_up_proj"].transpose(2, 0, 1).reshape(D, E_ * F),
        "wd": a["L0_ffn_w_down_proj"].transpose(0, 2, 1).reshape(E_ * F, D),
    }
    arrays = {f"in_{k}": np.ascontiguousarray(v) for k, v in arrays.items()}
    nc = bacc.Bacc("TRN2", target_bir_lowering=False, num_devices=1)
    io = {k[3:]: nc.dram_tensor(k, v.shape, F32, kind="ExternalInput").ap() for k, v in arrays.items()}
    io["out"] = nc.dram_tensor("out_dram", (T, D), F32, kind="ExternalOutput").ap()
    io["shift"] = nc.dram_tensor("shift_dram", (B, 2 * PAIRS, P), F32, kind="Internal").ap()
    io["vd"] = nc.dram_tensor("vd_dram", (B * DCA, D), F32, kind="Internal").ap()
    build(nc, io)
    r = run_bass_kernel_spmd(nc, [arrays], core_ids=[0])
    return r.results[0]["out_dram"].reshape(B, SQ, D)
```

```python
from contextlib import ExitStack

import concourse.bass as bass
from concourse import mybir

ALU = mybir.AluOpType
ACT = mybir.ActivationFunctionType
AX_X = mybir.AxisListType.X
F32 = mybir.dt.float32
F32R = mybir.dt.float32r
U32 = mybir.dt.uint32
I32 = mybir.dt.int32

P = 128
B, SQ, D = 16, 64, 512
SK, DC, DCA = 1601, 256, 16
H, HD = 16, 32
T = B * SQ
NT = T // P
KD = D // P
KC = DC // P
SM = SK - DCA
CH = -(-SM // P)
LAST = CH - 1
LM = SM - LAST * P
DCA_ROW = 64
PAIRS = H // 2
GROUPS = H // 4
PW = 2 * HD + 1
KV = 4
E_, F = 8, 192
EP = 4
EW = 2 * F
EC = EW // P
SCALE = HD ** -0.5
LN_EPS = 1e-5
HEAD_EPS = 1e-6
MASKED = -1e30
SAFE_SCORE = 70.0
TABLES = "natural_log_exp_and_others"


def head_view(ap):
    return ap.rearrange("p (h d) -> p h d", d=HD)


def spread(ap, n):
    return ap.unsqueeze(2).to_broadcast([ap.shape[0], ap.shape[1], n])


class Sems:

    def __init__(self, nc, ctx, phase):
        self.nc, self.ctx, self.phase, self.made = nc, ctx, phase, {}

    def __getitem__(self, name):
        if name not in self.made:
            self.made[name] = self.ctx.enter_context(self.nc.semaphore(f"{self.phase}_{name}"))
        return self.made[name]


def transposes(pe, bank, src, ident, n=KD):
    for k in range(n):
        last = pe.transpose(bank[:, k * P:(k + 1) * P], src[:, k * P:(k + 1) * P], ident)
    return last


def product(pe, bank, lhs, rhs):
    n = rhs.shape[1]
    for k in range(n):
        last = pe.matmul(bank, lhs[:, k, :], rhs[:, k, :], start=(k == 0), stop=(k == n - 1))
    return last


def split_product(pe, bank, terms, exact=()):
    todo = list(exact)
    for lhi, llo, rhi, rlo in terms:
        todo += [(lhi, rhi), (lhi, rlo), (llo, rhi)]
    for n, (lhs, rhs) in enumerate(todo):
        last = pe.matmul(bank, lhs, rhs, start=(n == 0), stop=(n == len(todo) - 1))
    return last


def rsqrt_seed(nc, act, seed, log, v, eps, done, count):
    nc.scalar.activation(log, v, ACT.Ln, bias=eps).then_inc(done, 1)
    act.wait_ge(done, count)
    return nc.scalar.activation(seed, log, ACT.Exp, scale=-0.5)


def rsqrt_refine(nc, dve, out, tmp, v, eps, seed, first, second, count):
    nc.vector.scalar_tensor_tensor(out=tmp, in0=v, scalar=eps, in1=seed, op0=ALU.add, op1=ALU.mult).then_inc(first, 1)
    dve.wait_ge(first, count)
    nc.vector.scalar_tensor_tensor(out=tmp, in0=tmp, scalar=-0.5, in1=seed, op0=ALU.mult, op1=ALU.mult).then_inc(second, 1)
    dve.wait_ge(second, count)
    return nc.vector.scalar_tensor_tensor(out=out, in0=tmp, scalar=1.5, in1=seed, op0=ALU.add, op1=ALU.mult)


EARLY = 2


def early_buffer(c):
    return c % 2


LANDING = ((0, 4), (4, 8), (8, CH))


def load_context(sp, io, g, b, free=None):
    for n, (lo, hi) in enumerate(LANDING):
        end = min(hi * P, SM)
        if free:
            free(hi - 1)
        sp.dma_start(g.y[:, :, lo * P:end], io["y"][b].rearrange("(k p) t -> p k t", p=P)[:, :, lo * P:end])\
            .then_inc(g.landed[n], 16)


def prepare(nc, io, g, psum):
    with ExitStack() as ctx:
        def sb(name, shape, dt=F32):
            return ctx.enter_context(nc.sbuf_tensor(name, shape, dt))

        s = Sems(nc, ctx, "prep")
        wk = sb("wk_raw", [P, KC, D])
        wv = sb("wv_raw", [P, KC, D])
        wkd = sb("wkd", [P, KC, D])
        wvd = sb("wvd", [P, KC, D])
        wq = sb("wq", [P, KD, D])
        yd = sb("yd", [P, KC, B * DCA])
        bq = sb("bq", [P, D])
        bkd = sb("bkd", [P, D])
        bvs = sb("bvs", [P, 2 * KD])
        bvt = sb("bvt", [P, KD])
        bvb = sb("bvb", [P, KD, P])
        msum = sb("msum", [P, KD, H])
        st = sb("st", [P, NT, 6])
        mv = sb("mv", [P, NT, 2])
        rs = sb("rs", [P, NT])
        rlog = sb("rlog", [P, NT])
        rseed = sb("rseed", [P, NT])
        rtmp = sb("rtmp", [P, NT])
        qlog = sb("qlog", [P, 2, H])
        qseed = sb("qseed", [P, 2, H])
        qtmp = sb("qtmp", [P, 2, H])
        xn = sb("xn", [P, 2, D])
        xT = sb("xT", [P, 2, KD, P])
        qc = sb("qc", [P, 2, D])
        sq = sb("sq", [P, 2, D])
        ss = sb("ss", [P, 2, H])
        qr = sb("qr", [P, 2, H])
        qn = sb("qn", [P, 2, D])
        norms = g.ctxT[0:1, 0, 1, 0:6 * HD].rearrange("p (n d) -> p n d", n=6)
        cross = g.ctxT[0:1, 0, 0, 0:8 * HD].rearrange("p (i n d) -> p i n d", i=2, n=4)
        peak = sb("peak", [1, 2, 4])
        power = sb("power", [1, 2, 4])
        vd = xn

        PARTS = ((0, 2), (2, NT))

        def read_guard(eng, name):
            eng.wait_ge(s["guard"], 1)
            eng.sem_inc(s["guard_read"], 1)
            g.guards[name] = eng.value_load(g.guard[0:1, 0:1], min_val=0, max_val=1)

        def done(i, u):
            return i * 2 + (u + 3)

        def before(i, u):
            return i * 2 + (u + 1)

        with nc.Block() as block:
            @block.sync
            def _(sp):
                for n, (lo, hi) in enumerate(PARTS):
                    sp.dma_start(g.x[:, lo:hi, :], io["x"].rearrange("(t p) d -> p t d", p=P)[:, lo:hi, :]).then_inc(s[f"x{n}"], 16)
                    if n == 0:
                        for k in range(KD):
                            sp.dma_start(wq[:, k, :], io["wq"][k * P:(k + 1) * P, :]).then_inc(s[f"wq{k}"], 16)
                        sp.dma_start(bq[:], io["bq"].partition_broadcast(P)).then_inc(s["bq"], 16)
                sp.dma_start(wkd[:], io["wkd"].rearrange("(k p) n -> p k n", p=P)).then_inc(s["wkd"], 16)
                sp.dma_start(wvd[:], io["wvd"].rearrange("(k p) n -> p k n", p=P)).then_inc(s["wvd"], 16)
                sp.dma_start(yd[:], io["yd"].rearrange("(k p) n -> p k n", p=P)).then_inc(s["yd"], 16)
                sp.dma_start(bkd[:], io["bkd"].partition_broadcast(P)).then_inc(s["bias"], 16)
                sp.dma_start(g.bk[:], io["bk"].partition_broadcast(P)).then_inc(s["bias"], 16)
                sp.dma_start(wk[:], io["wk"].rearrange("(k p) n -> p k n", p=P)).then_inc(s["wk"], 16)
                sp.dma_start(wv[:], io["wv"].rearrange("(k p) n -> p k n", p=P)).then_inc(s["wv"], 16)
                sp.dma_start(g.wo[:], io["wo"].rearrange("k p n -> p k n")).then_inc(s["wo"], 16)
                sp.dma_start(g.bo[:], io["bo"].partition_broadcast(P)).then_inc(s["bo"], 16)
                load_context(sp, io, g, 0)
                read_guard(sp, "sp")
                for u in range(2):
                    sp.wait_ge(s["vd"], u + 1)
                    sp.dma_start(io["vd"][u * P:(u + 1) * P, :], vd[:, u, :]).then_inc(s["vd_out"], 16)
                sp.wait_ge(s["vd_out"], 32)

            @block.scalar
            def _(act):
                act.preload_act_table_set(TABLES)
                act.dma_start(g.ident[:], io["ident"]).then_inc(s["ident"], 16)
                act.dma_start(g.cols[:], io["cols"]).then_inc(s["cols"], 16)
                act.dma_start(norms, io["norms"].rearrange("p (n d) -> p n d", n=6)).then_inc(s["norms"], 16)
                act.dma_start(bvs[:], io["bv"]).then_inc(s["bv"], 16)
                act.wait_ge(s["cols"], 16)
                for stage in ("xe", "qe", "qlog", "qseed"):
                    act.sem_inc(s[stage], 2)

                def x_seed(n):
                    lo, hi = PARTS[n]
                    act.wait_ge(s["ba"], hi)
                    rsqrt_seed(nc, act, rseed[:, lo:hi], rlog[:, lo:hi], mv[:, lo:hi, 1], g.cols[:, 9:10],
                               s["rlog"], n + 1).then_inc(s["rseed"], 1)

                def evac_xT(i, u):
                    act.wait_ge(s["trx"], done(i, u))
                    act.wait_ge(s["qp"], before(i, u))
                    nc.scalar.copy(xT[:, u], psum[:, u, :].rearrange("p (k t) -> p k t", k=KD)).then_inc(s["xe"], 1)

                def evac_heads(i, u, dst, w, b):
                    act.wait_ge(s["trq"], done(i, u))
                    nc.scalar.activation(dst, psum[:, 4 + u, :].rearrange("p (k t) -> p k t", k=GROUPS),
                                         ACT.Identity, scale=g.cols[:, w:w + 1], bias=g.cols[:, b:b + 1]).then_inc(s["qe"], 1)

                def evac_queries(i, u):
                    evac_heads(i, u, g.q[:, :, bass.ds((i * 2 + u) * P, P)], 0, 1)

                def seed(i, u):
                    act.wait_ge(s["qrd"], done(i, u))
                    act.wait_ge(s["qm"], before(i, u))
                    rsqrt_seed(nc, act, qseed[:, u], qlog[:, u], ss[:, u], g.cols[:, 8:9], s["qlog"],
                               done(i, u)).then_inc(s["qseed"], 1)

                x_seed(0)
                evac_xT(0, 0)
                evac_xT(0, 1)
                x_seed(1)
                read_guard(act, "act")
                evac_xT(1, 0)
                evac_xT(1, 1)
                seed(0, 0)
                seed(0, 1)

                def steps(i, more):
                    evac_queries(i - 1, 0)
                    evac_queries(i - 1, 1)
                    for u in range(2):
                        if more:
                            evac_xT(i + 1, u)
                        seed(i, u)

                with act.Fori(1, NT // 2 - 1) as i:
                    steps(i, True)
                steps(NT // 2 - 1, False)
                end = NT // 2
                evac_queries(end - 1, 0)
                seed(end, 0)
                evac_queries(end - 1, 1)
                seed(end, 1)
                for u in range(2):
                    act.wait_ge(s["vdp"], u + 1)
                    nc.scalar.copy(vd[:, u, :], psum[:, 6 + u, :]).then_inc(s["vd"], 1)
                for u in range(2):
                    evac_heads(end, u, g.kd[:, :, u * P:(u + 1) * P], 4, 5)
                    if u == 0:
                        act.wait_ge(g.landed[0], 16)
                        for c in range(EARLY):
                            nc.scalar.copy(g.y_hi[:, early_buffer(c)], g.y[:, :, c * P:(c + 1) * P]).then_inc(s["yhi"], 1)

            @block.gpsimd
            def _(pool):
                pool.sem_inc(s["qsq"], 2)

                def square(i, u):
                    pool.wait_ge(s["qb"], done(i, u))
                    pool.wait_ge(s["qrd"], before(i, u))
                    nc.gpsimd.tensor_tensor(sq[:, u], qc[:, u], qc[:, u], ALU.mult).then_inc(s["qsq"], 1)

                nc.gpsimd.memset(g.qbd_hi[:].bitcast(F32), 0.0)
                nc.gpsimd.memset(g.qbd_lo[:].bitcast(F32), 0.0)
                nc.gpsimd.memset(g.y_hi[:, 2].bitcast(F32), 0.0)
                nc.gpsimd.memset(g.y_lo[:, 2].bitcast(F32), 0.0)
                nc.gpsimd.memset(g.k_hi[:, 2].bitcast(F32), 0.0)
                nc.gpsimd.memset(g.k_lo[:, 2].bitcast(F32), 0.0)
                nc.gpsimd.memset(g.v[:], 1.0)
                nc.gpsimd.memset(g.ctx[:], 0.0)
                nc.gpsimd.memset(g.v_last[:], 0.0).then_inc(s["zero"], 1)
                pool.wait_ge(s["zero"], 1)
                pool.wait_ge(s["cols"], 16)
                for n, col in enumerate((PW - 1, 2 * PW - 1)):
                    nc.gpsimd.tensor_tensor(g.v_last[:, :, col], g.v_last[:, :, col],
                                            g.cols[:, 6 + n:7 + n].to_broadcast([P, PAIRS]), ALU.add)
                read_guard(pool, "pool")
                square(0, 0)
                square(0, 1)
                pool.wait_ge(s["wv"], 16)
                nc.gpsimd.tensor_copy(g.wv_hi[:], wv[:]).then_inc(s["wv_hi"], 1)
                with pool.Fori(1, NT // 2) as i:
                    square(i, 0)
                    square(i, 1)
                for u in range(2):
                    square(NT // 2, u)
                pool.wait_ge(s["wv_hi"], 1)
                nc.gpsimd.tensor_tensor(g.wv_lo[:], wv[:], g.wv_hi[:].bitcast(F32), ALU.subtract).then_inc(s["wv_lo"], 1)
                for c in range(EARLY):
                    pool.wait_ge(s["yhi"], c + 1)
                    nc.gpsimd.tensor_tensor(g.y_lo[:, early_buffer(c)], g.y[:, :, c * P:(c + 1) * P],
                                            g.y_hi[:, early_buffer(c)].bitcast(F32), ALU.subtract)

            @block.vector
            def _(dve):
                chain = [0]

                def link(ins):
                    chain[0] += 1
                    ins.then_inc(s["chain"], 1)
                    dve.wait_ge(s["chain"], chain[0])

                for stage in ("xn", "qb", "qrd", "qn1", "qn2", "qrs", "qm"):
                    dve.sem_inc(s[stage], 2)

                def statistics(n):
                    lo, hi = PARTS[n]
                    dve.wait_ge(s[f"x{n}"], 16)
                    for t in range(lo, hi):
                        nc.vector.bn_stats(st[:, t, :], g.x[:, t, :]).then_inc(s["bs"], 1)
                    for t in range(lo, hi):
                        dve.wait_ge(s["bs"], t + 1)
                        nc.vector.bn_aggr(mv[:, t, :], st[:, t, :]).then_inc(s["ba"], 1)

                def x_rstd(n):
                    lo, hi = PARTS[n]
                    dve.wait_ge(s["rseed"], n + 1)
                    link(rsqrt_refine(nc, dve, rs[:, lo:hi], rtmp[:, lo:hi], mv[:, lo:hi, 1], LN_EPS, rseed[:, lo:hi],
                                      s["rn1"], s["rn2"], n + 1))

                def normalise_x(i, u):
                    t = i * 2 + u
                    dve.wait_ge(s["trx"], before(i, u))
                    nc.vector.tensor_scalar(xn[:, u], g.x[:, t, :], mv[:, t, 0:1], rs[:].unsqueeze(2)[:, t, :],
                                            ALU.subtract, ALU.mult).then_inc(s["xn"], 1)

                def center(w):
                    rows, n = w.shape[0], w.shape[1] // HD
                    sums = msum[:].rearrange("p k h -> p (k h)")[0:rows, 0:n]
                    link(nc.vector.tensor_reduce(sums, head_view(w), AX_X, ALU.add))
                    link(nc.vector.scalar_tensor_tensor(out=head_view(w), in0=spread(sums, HD), scalar=-1.0 / HD,
                                                        in1=head_view(w), op0=ALU.mult, op1=ALU.add))

                def split(hi, lo, w):
                    link(nc.vector.tensor_copy(hi, w))
                    nc.vector.tensor_tensor(lo, w, hi.bitcast(F32), ALU.subtract)

                def score_range():
                    dve.wait_ge(s["norms"], 16)
                    for n in range(2):
                        last = nc.vector.tensor_tensor(cross[:, n], norms[:, 2:6, :], norms[:, n:n + 1, :].to_broadcast([1, 4, HD]),
                                                       ALU.mult)
                    link(last)
                    link(nc.vector.tensor_tensor(cross, cross, cross, ALU.mult))
                    nc.vector.tensor_reduce(peak[:], cross, AX_X, ALU.max)
                    link(nc.vector.tensor_reduce(power[:], cross, AX_X, ALU.add))
                    link(nc.vector.tensor_scalar(power[:, 0, 0:4:2], peak[:, 0, 0:4:2], 1.25 * HD / 15, None, ALU.mult))
                    link(nc.vector.tensor_tensor(power[:, 0], power[:, 0], power[:, 1], ALU.add))
                    link(nc.vector.tensor_tensor(power[:, 0, 0:4:2], power[:, 0, 0:4:2], power[:, 0, 1:4:2], ALU.add))
                    link(nc.vector.tensor_tensor(power[:, 0, 0:1], power[:, 0, 0:1], power[:, 0, 2:3], ALU.max))
                    link(nc.vector.tensor_scalar(power[:, 0, 0:1], power[:, 0, 0:1], SAFE_SCORE ** 2 / (SCALE ** 2 * HD * 15),
                                                 None, ALU.is_gt))
                    nc.vector.tensor_copy(g.guard[:], power[:, 0, 0:1]).then_inc(s["guard"], 1)

                statistics(0)
                x_rstd(0)
                for u in range(2):
                    normalise_x(0, u)
                score_range()
                read_guard(dve, "dve")
                for k in range(KD):
                    dve.wait_ge(s[f"wq{k}"], 16)
                    center(wq[:, k, :])
                    dve.sem_inc(s["wq_c"], 1)
                dve.wait_ge(s["bq"], 16)
                center(bq[:])

                def bias(i, u, b):
                    dve.wait_ge(s["qp"], done(i, u))
                    dve.wait_ge(s["qm"], before(i, u))
                    nc.vector.tensor_tensor(qc[:, u], psum[:, 2 + u, :], b, ALU.add).then_inc(s["qb"], 1)

                def reduce(i, u):
                    dve.wait_ge(s["qsq"], done(i, u))
                    dve.wait_ge(s["qrs"], before(i, u))
                    nc.vector.tensor_reduce(ss[:, u], head_view(sq[:, u]), AX_X, ALU.add).then_inc(s["qrd"], 1)

                def scale_heads(i, u):
                    dve.wait_ge(s["qseed"], done(i, u))
                    rsqrt_refine(nc, dve, qr[:, u], qtmp[:, u], ss[:, u], HD * HEAD_EPS, qseed[:, u],
                                 s["qn1"], s["qn2"], done(i, u)).then_inc(s["qrs"], 1)
                    dve.wait_ge(s["qrs"], done(i, u))
                    dve.wait_ge(s["trq"], before(i, u))
                    nc.vector.scalar_tensor_tensor(out=head_view(qn[:, u]), in0=head_view(qc[:, u]), scalar=HD ** 0.5,
                                                   in1=spread(qr[:, u], HD), op0=ALU.mult, op1=ALU.mult).then_inc(s["qm"], 1)

                def head_norm(i, b, more=False):
                    for u in range(2):
                        bias(i, u, b)
                        if more:
                            normalise_x(i + 1, u)
                    for u in range(2):
                        reduce(i, u)
                    for u in range(2):
                        scale_heads(i, u)

                statistics(1)
                x_rstd(1)
                for u in range(2):
                    normalise_x(1, u)
                head_norm(0, bq[:])
                with dve.Fori(1, NT // 2 - 1) as i:
                    head_norm(i, bq[:], True)
                dve.wait_ge(s["bias"], 32)
                center(bkd[:])
                center(g.bk[:])
                dve.wait_ge(s["wkd"], 16)
                center(wkd[:].rearrange("p k n -> p (k n)"))
                dve.sem_inc(s["wkd_c"], 1)
                dve.wait_ge(s["bv"], 16)
                link(nc.vector.tensor_tensor(bvt[:], bvs[:, 0:KD], bvs[:, KD:2 * KD], ALU.add))
                nc.vector.tensor_copy(bvb[:], spread(bvt[:], P)).then_inc(s["bvb"], 1)
                head_norm(NT // 2 - 1, bq[:])
                dve.wait_ge(s["wk"], 16)
                center(wk[:].rearrange("p k n -> p (k n)"))
                head_norm(NT // 2, bkd[:])
                split(g.wk_hi[:], g.wk_lo[:], wk[:])
                dve.wait_ge(s["bop"], 1)
                dve.wait_ge(s["bo"], 16)
                nc.vector.tensor_tensor(g.bo[:], g.bo[:], psum[:, 0, :], ALU.add)

            @block.tensor
            def _(pe):
                for stage in ("trx", "qp", "trq"):
                    pe.sem_inc(s[stage], 2)
                pe.wait_ge(s["ident"], 16)

                def turn_x(i, u):
                    pe.wait_ge(s["xn"], done(i, u))
                    pe.wait_ge(s["xe"], before(i, u))
                    transposes(pe, psum[:, u, :], xn[:, u, :], g.ident[:]).then_inc(s["trx"], 1)

                def project(i, u):
                    pe.wait_ge(s["xe"], done(i, u))
                    pe.wait_ge(s["qb"], before(i, u))
                    product(pe, psum[:, 2 + u, :], xT[:, u], wq[:]).then_inc(s["qp"], 1)

                def turn_heads(i, u):
                    pe.wait_ge(s["qm"], done(i, u))
                    pe.wait_ge(s["qe"], before(i, u))
                    transposes(pe, psum[:, 4 + u, :], qn[:, u, :], g.ident[:]).then_inc(s["trq"], 1)

                def steps(i, heads, more):
                    for u in range(2):
                        project(i, u)
                        if heads:
                            turn_heads(i - 1, u)
                        if more and u:
                            turn_x(i + 1, 0)
                    if more:
                        turn_x(i + 1, 1)

                turn_x(0, 0)
                turn_x(0, 1)
                read_guard(pe, "pe")
                pe.wait_ge(s["wq_c"], KD)
                steps(0, False, True)
                with pe.Fori(1, NT // 2 - 1) as i:
                    steps(i, True, True)
                steps(NT // 2 - 1, True, False)
                pe.wait_ge(s["yd"], 16)
                pe.wait_ge(s["wvd"], 16)
                pe.wait_ge(s["wkd_c"], 1)
                i = NT // 2
                for u in range(2):
                    pe.wait_ge(s["qb"], before(i, u))
                    product(pe, psum[:, 2 + u, :], yd[:, :, u * P:(u + 1) * P], wkd[:]).then_inc(s["qp"], 1)
                    turn_heads(i - 1, u)
                for u in range(2):
                    product(pe, psum[:, 6 + u, :], yd[:, :, u * P:(u + 1) * P], wvd[:]).then_inc(s["vdp"], 1)
                pe.wait_ge(s["bvb"], 1)
                pe.wait_ge(s["wo"], 16)
                pe.wait_ge(s["xe"], done(i - 1, 0))
                product(pe, psum[:, 0, :], bvb[:], g.wo[:]).then_inc(s["bop"], 1)
                for u in range(2):
                    turn_heads(i, u)
        g.spent = list(s.made.values())


def score_maxima(nc, io, g, psum):
    K_BANK, TR_BANK, S_BANK, M_BANK = 0, 1, 2, 4

    with ExitStack() as ctx:
        def sb(name, shape, dt=F32):
            return ctx.enter_context(nc.sbuf_tensor(name, shape, dt))

        s = Sems(nc, ctx, "max")
        y = sb("max_y", [P, KC, P])
        kc = sb("max_kc", [P, D])
        sq = sb("max_sq", [P, D])
        ss = sb("max_ss", [P, H])
        klog = sb("max_log", [P, H])
        seed = sb("max_seed", [P, H])
        tmp = sb("max_tmp", [P, H])
        kr = sb("max_kr", [P, H])
        kn = sb("max_kn", [P, D])
        kT = sb("max_kT", [P, GROUPS, P])
        top = sb("max_top", [P, PAIRS])
        best = sb("max_best", [P, 2, PAIRS])
        turned = sb("max_turned", [2 * PAIRS, P])
        queries = sb("max_q", [P, GROUPS, 4 * SQ])

        def step(b, c):
            return b * CH + (c + 1)

        def rounds(eng, name, start, chunk, finish):
            with eng.If(g.guards[name] != 0):
                with eng.Fori(0, B) as b:
                    start(b)
                    with eng.Fori(0, LAST) as c:
                        chunk(b, c, P)
                    chunk(b, LAST, LM)
                    finish(b)
            eng.sem_inc(s["over"], 1)

        def nothing(*_):
            pass

        with nc.Block() as block:
            @block.sync
            def _(sp):
                def chunk(b, c, w):
                    sp.wait_ge(s["krd"], step(b, c))
                    sp.sem_inc(s["gate_sp"], 1)
                    sp.dma_start(y[:, :, 0:w], io["y"][b].rearrange("(k p) t -> p k t", p=P)[:, :, bass.ds(c * P, w)])\
                        .then_inc(s["y"], 16)

                def finish(b):
                    sp.wait_ge(s["me"], b + 1)
                    sp.sem_inc(s["gate_sp"], 1)
                    sp.dma_start(io["shift"][b], turned[:]).then_inc(s["out"], 16)
                    sp.wait_ge(s["out"], b * 16 + 16)
                    sp.sem_inc(s["gate_sp"], 1)

                sp.sem_inc(s["krd"], 1)
                rounds(sp, "sp", nothing, chunk, finish)

            @block.tensor
            def _(pe):
                def chunk(b, c, w):
                    n = step(b, c)
                    pe.wait_ge(s["y"], n * 16)
                    for k in range(KC):
                        for part in (g.wk_hi, g.wk_lo):
                            last = pe.matmul(psum[0:w, K_BANK, :], y[:, k, 0:w], part[:, k, :].bitcast(F32),
                                             start=(k == 0 and part is g.wk_hi), stop=(k == KC - 1 and part is g.wk_lo))
                    last.then_inc(s["kp"], 1)
                    pe.wait_ge(s["km"], n)
                    transposes(pe, psum[:, TR_BANK, :], kn, g.ident[:]).then_inc(s["tr"], 1)
                    pe.wait_ge(s["ke"], n)
                    scores(w, kT[:, :, 0:w])

                def scores(w, keys):
                    for p in range(PAIRS):
                        lhs = queries[:, p // 2, (p % 2) * P:(p % 2 + 1) * P]
                        last = pe.matmul(psum[:, S_BANK + p // 4, (p % 4) * w:(p % 4 + 1) * w], lhs, keys[:, p // 2, :],
                                         start=True, stop=True)
                    last.then_inc(s["sc"], 1)

                def start(b):
                    pe.wait_ge(s["q"], b * 4 + 4)
                    pe.sem_inc(s["gate"], 1)

                def finish(b):
                    pe.wait_ge(s["best"], (b + 1) * CH)
                    scores(DCA, g.kd[:, :, bass.ds(b * DCA, DCA)])
                    pe.wait_ge(s["neg"], b + 1)
                    pe.transpose(psum[0:2 * PAIRS, M_BANK, 0:P], best[:].rearrange("p n q -> p (n q)"), g.ident[:])\
                        .then_inc(s["mt"], 1)

                rounds(pe, "pe", start, chunk, finish)

            @block.scalar
            def _(act):
                def chunk(b, c, w):
                    n = step(b, c)
                    act.wait_ge(s["krd"], n + 1)
                    rsqrt_seed(nc, act, seed[0:w], klog[0:w], ss[0:w], g.cols[0:w, 8:9], s["klog"], n).then_inc(s["seed"], 1)
                    act.wait_ge(s["tr"], n)
                    nc.scalar.activation(kT[:, :, 0:w], psum[:, TR_BANK, :].rearrange("p (g t) -> p g t", g=GROUPS)[:, :, 0:w],
                                         ACT.Identity, scale=g.cols[:, 2:3], bias=g.cols[:, 3:4]).then_inc(s["ke"], 1)

                def finish(b):
                    act.wait_ge(s["mt"], b + 1)
                    nc.scalar.copy(turned[:], psum[0:2 * PAIRS, M_BANK, 0:P]).then_inc(s["me"], 1)

                rounds(act, "act", nothing, chunk, finish)

            @block.gpsimd
            def _(pool):
                pool.wait_ge(s["over"], 4)

            @block.vector
            def _(dve):
                links = s["link"]

                def start(b):
                    nc.vector.memset(queries[:], 0.0).then_inc(s["clear"], 1)
                    dve.wait_ge(s["clear"], b + 1)
                    for i in range(4):
                        rows, at = slice(i * HD, (i + 1) * HD), slice(i * SQ, (i + 1) * SQ)
                        nc.vector.tensor_copy(queries[rows, :, at], g.q[rows, :, bass.ds(b * SQ, SQ)]).then_inc(s["q"], 1)
                    nc.vector.memset(best[:, 0], MASKED).then_inc(s["fresh"], 1)

                def chunk(b, c, w):
                    n = step(b, c)
                    dve.wait_ge(s["kp"], n)
                    nc.vector.tensor_tensor(kc[0:w], psum[0:w, K_BANK, :], g.bk[0:w], ALU.add).then_inc(links, 1)
                    dve.wait_ge(links, b * (3 * CH) + (c * 3 + 1))
                    nc.vector.tensor_tensor(sq[0:w], kc[0:w], kc[0:w], ALU.mult).then_inc(links, 1)
                    dve.wait_ge(links, b * (3 * CH) + (c * 3 + 2))
                    nc.vector.tensor_reduce(ss[0:w], head_view(sq[0:w]), AX_X, ALU.add).then_inc(s["krd"], 1)
                    dve.wait_ge(s["seed"], n)
                    rsqrt_refine(nc, dve, kr[0:w], tmp[0:w], ss[0:w], HD * HEAD_EPS, seed[0:w], s["kn1"], s["kn2"], n)\
                        .then_inc(links, 1)
                    dve.wait_ge(links, b * (3 * CH) + (c * 3 + 3))
                    nc.vector.scalar_tensor_tensor(out=head_view(kn[0:w]), in0=head_view(kc[0:w]), scalar=HD ** 0.5,
                                                   in1=spread(kr[0:w], HD), op0=ALU.mult, op1=ALU.mult).then_inc(s["km"], 1)
                    dve.wait_ge(s["sc"], b + n)
                    reduce(top[:], w).then_inc(s["topd"], 1)
                    dve.wait_ge(s["topd"], n)
                    dve.wait_ge(s["fresh"], b + 1)
                    nc.vector.tensor_tensor(best[:, 0], best[:, 0], top[:], ALU.max).then_inc(s["best"], 1)
                    dve.wait_ge(s["best"], n)

                def reduce(out, w):
                    for n in range(2):
                        last = nc.vector.tensor_reduce(out[:, n * 4:(n + 1) * 4],
                                                       psum[:, S_BANK + n, 0:4 * w].rearrange("p (q t) -> p q t", q=4),
                                                       AX_X, ALU.max)
                    return last

                def finish(b):
                    dve.wait_ge(s["sc"], (b + 1) * (CH + 1))
                    reduce(best[:, 1], DCA).then_inc(s["second"], 1)
                    dve.wait_ge(s["second"], b + 1)
                    nc.vector.tensor_scalar(best[:], best[:], -1.0, None, ALU.mult).then_inc(s["neg"], 1)
                    dve.wait_ge(s["mt"], b + 1)

                rounds(dve, "dve", start, chunk, finish)


def cross_attention(nc, io, g, psum):
    K_BANK, V_BANK, TR_BANK, S_BANK, O_BANK = 0, 1, 2, 3, 5

    with ExitStack() as ctx:
        def sb(name, shape, dt=F32):
            return ctx.enter_context(nc.sbuf_tensor(name, shape, dt))

        s = Sems(nc, ctx, "xa")
        y = g.y
        kc = sb("kc", [P, 3, D])
        sq = sb("ksq", [P, 3, D])
        ss = sb("kss", [P, 3, H])
        kr = sb("kr", [P, 3, H])
        klog = sb("klog", [P, 3, H])
        kseed = sb("kseed", [P, 3, H])
        ktmp = sb("ktmp", [P, 3, H])
        kn = sb("kn", [P, 3, D])
        k32 = sb("k32", [P, 3, GROUPS, P])
        probs = sb("probs", [P, 3, H * SQ])
        o_sb = sb("o_sb", [P, PAIRS, 2 * PW])
        rinv = sb("rinv", [P, PAIRS, 2])
        od = sb("od", [P, PAIRS, HD])
        select_raw = sb("select_raw", [2, 2, P])
        shift_raw = sb("shift_raw", [2, H * SQ])
        select = sb("select", [2, 2, P], F32R)
        shift = sb("shift", [2, H * SQ], F32R)

        def buf(c):
            return 2 if c == LAST else c % 2

        def at(b, c):
            return (b, c) if c < CH else (b + 1, c - CH)

        def done(b, c):
            return b * CH + (CH + c + 1)

        def before(b, c):
            return done(b, c - CH if c == LAST else c - 2 if c >= 2 else c - 3)

        def batches(eng, name, first, steps):
            def run(guarded):
                first(guarded)
                with eng.Fori(0, B - 1) as b:
                    steps(b, CH, guarded)
                steps(B - 1, 0, guarded)

            with eng.If(g.guards[name] != 0):
                run(True)
            with eng.Else():
                run(False)
            eng.sem_inc(s["over"], 1)

        blocks = [(slice(i * HD, (i + 1) * HD), slice(i * SQ, (i + 1) * SQ)) for i in range(4)]

        def parts(guarded):
            return 9 if guarded else 8

        def ahead(c, n, room):
            return c + n < CH + room

        def normalise(b, wait, engine):
            for j in range(2):
                rows = slice(j * SQ, (j + 1) * SQ)
                for n, dst in enumerate((g.ctx, od)):
                    engine.tensor_tensor(dst[rows], o_sb[rows, :, n * PW + j * HD:n * PW + (j + 1) * HD],
                                         rinv[rows, :, n:n + 1].to_broadcast([SQ, PAIRS, HD]),
                                         ALU.mult).then_inc(s["onp"], 1)
            wait.wait_ge(s["onp"], b * 4 + 4)
            engine.tensor_tensor(g.ctx[:], g.ctx[:], od[:], ALU.add).then_inc(s["on"], 1)

        o_bank = [psum[:, O_BANK + p // 3, (p % 3) * 2 * PW:(p % 3 + 1) * 2 * PW] for p in range(PAIRS)]

        with nc.Block() as block:
            @block.sync
            def _(sp):
                def second_values(b):
                    sp.wait_ge(s["pv"], done(b, -1))
                    sp.dma_start(g.v_last[DCA_ROW:DCA_ROW + DCA, :, PW:2 * PW - 1],
                                 io["vd"][bass.ds(b * DCA, DCA), :].rearrange("t (p n) -> t p n", p=PAIRS))\
                        .then_inc(s["vd"], 16)

                def shifts(b):
                    if not isinstance(b, int):
                        sp.wait_ge(s["qb"], b * parts(True))
                    sp.dma_start(shift_raw[:], io["shift"][b].rearrange("(s q) n -> s (q n)", s=2)).then_inc(s["shift"], 16)

                sp.dma_start(g.mask[:], io["mask"]).then_inc(s["sa_w"], 16)
                for dst, src in ((g.sa_wq, io["sa_wq"]), (g.sa_wk, io["sa_wk"]), (g.sa_wv, io["sa_wv"]), (g.sa_wo, io["sa_wo"])):
                    sp.dma_start(dst[:], src.rearrange("(k p) n -> p k n", p=P)).then_inc(s["sa_w"], 16)
                second_values(0)
                sp.dma_start(select_raw[:].rearrange("s n p -> s (n p)"), io["select"]).then_inc(s["select"], 16)

                def batch(b, guarded):
                    def free(c):
                        sp.wait_ge(s["yhi"], done(b, c - CH))
                        sp.wait_ge(s["ylo"], done(b, c - CH))

                    load_context(sp, io, g, b, free)
                    second_values(b)
                    if guarded:
                        shifts(b)

                with sp.If(g.guards["sp"] != 0):
                    shifts(0)
                    with sp.Fori(1, B) as b:
                        batch(b, True)
                with sp.Else():
                    with sp.Fori(1, B) as b:
                        batch(b, False)
                sp.wait_ge(s["sa_w"], 80)
                sp.wait_ge(s["select"], 16)

            @block.scalar
            def _(act):
                act.sem_inc(s["yhi"], CH + EARLY)
                for stage in ("ke", "ve", "ex", "klog", "kseed"):
                    act.sem_inc(s[stage], CH)
                act.sem_inc(s["oe"], 1)

                def y_high(b, c):
                    b, c = at(b, c)
                    n = next(n for n, (lo, hi) in enumerate(LANDING) if lo <= c < hi)
                    w = min(P, SM - c * P)
                    act.wait_ge(g.landed[n], b * 16 + 16)
                    act.wait_ge(s["vp"], before(b, c))
                    nc.scalar.copy(g.y_hi[:, buf(c), :, 0:w], y[:, :, c * P:c * P + w]).then_inc(s["yhi"], 1)

                def k_evac(b, c):
                    b, c = at(b, c)
                    w = DCA_ROW if c == LAST else P
                    act.wait_ge(s["tr"], done(b, c))
                    act.wait_ge(s["klo"], before(b, c))
                    nc.scalar.activation(k32[:, buf(c), :, 0:w],
                                         psum[:, TR_BANK, :].rearrange("p (g t) -> p g t", g=GROUPS)[:, :, 0:w],
                                         ACT.Identity, scale=g.cols[:, 2:3], bias=g.cols[:, 3:4]).then_inc(s["ke"], 1)

                def v_evac(b, c):
                    b, c = at(b, c)
                    bank = psum[:, V_BANK, :].rearrange("p (q n) -> p q n", q=PAIRS)
                    act.wait_ge(s["vp"], done(b, c))
                    act.wait_ge(s["pv"], before(b, c))
                    if c == LAST:
                        nc.scalar.copy(g.v_last[0:DCA_ROW, :, 0:PW - 1], bank[0:DCA_ROW]).then_inc(s["ve"], 1)
                    else:
                        nc.scalar.copy(g.v[:, buf(c), :, 0:PW - 1], bank).then_inc(s["ve"], 1)

                def seed(b, c):
                    b, c = at(b, c)
                    act.wait_ge(s["krd"], done(b, c))
                    act.wait_ge(s["krs"], before(b, c))
                    rsqrt_seed(nc, act, kseed[:, buf(c)], klog[:, buf(c)], ss[:, buf(c)], g.cols[:, 8:9], s["klog"],
                               done(b, c)).then_inc(s["kseed"], 1)

                def exps(b, c):
                    b, c = at(b, c)
                    act.wait_ge(s["sc"], done(b, c))
                    act.wait_ge(s["pv"], before(b, c))
                    nc.scalar.activation(probs[:, buf(c), :], psum[:, S_BANK:S_BANK + 2, :].rearrange("p a n -> p (a n)"),
                                         ACT.Exp, scale=SCALE).then_inc(s["ex"], 1)

                def o_evac(b):
                    act.wait_ge(s["pv"], done(b, LAST))
                    act.wait_ge(s["on"], b * 1 + 1)
                    for bank, (lo, hi) in enumerate(((0, 3), (3, 6), (6, PAIRS))):
                        last = nc.scalar.copy(o_sb[:, lo:hi, :],
                                              psum[:, O_BANK + bank, 0:(hi - lo) * 2 * PW]
                                              .rearrange("p (q n) -> p q n", n=2 * PW))
                    last.then_inc(s["oe"], 1)

                def ctx_evac(b):
                    act.wait_ge(s["ct"], b + 1)
                    nc.scalar.copy(g.ctxT[:, :, :, bass.ds(b * SQ, SQ)],
                                   psum[:, TR_BANK, 0:2 * P].rearrange("p (g j q) -> p g j q", g=2, j=2)).then_inc(s["ce"], 1)

                def first(guarded):
                    y_high(0, 2)
                    v_evac(0, 0)
                    seed(0, 0)
                    k_evac(0, 0)
                    v_evac(0, 1)
                    seed(0, 1)
                    exps(0, 0)

                def steps(b, room, guarded):
                    for c in range(CH):
                        if ahead(c, 3, room):
                            y_high(b, c + 3)
                        if ahead(c, 1, room):
                            k_evac(b, c + 1)
                        if ahead(c, 2, room):
                            seed(b, c + 2)
                            v_evac(b, c + 2)
                        if c == LAST:
                            o_evac(b)
                        if ahead(c, 1, room):
                            exps(b, c + 1)
                        if c == 2:
                            ctx_evac(b)

                batches(act, "act", first, steps)
                ctx_evac(B)

            @block.gpsimd
            def _(pool):
                pool.sem_inc(s["ksq"], CH)
                pool.sem_inc(s["ylo"], CH + EARLY)
                pool.sem_inc(s["on"], 1)

                def y_low(b, c):
                    b, c = at(b, c)
                    w = min(P, SM - c * P)
                    pool.wait_ge(s["yhi"], done(b, c))
                    pool.wait_ge(s["vp"], before(b, c))
                    nc.gpsimd.tensor_tensor(g.y_lo[:, buf(c), :, 0:w], y[:, :, c * P:c * P + w],
                                            g.y_hi[:, buf(c), :, 0:w].bitcast(F32), ALU.subtract).then_inc(s["ylo"], 1)

                def square(b, c):
                    b, c = at(b, c)
                    pool.wait_ge(s["kb"], done(b, c))
                    pool.wait_ge(s["krd"], before(b, c))
                    nc.gpsimd.tensor_tensor(sq[:, buf(c)], kc[:, buf(c)], kc[:, buf(c)], ALU.mult).then_inc(s["ksq"], 1)

                def first(guarded):
                    square(0, 0)
                    y_low(0, 2)
                    square(0, 1)
                    y_low(0, 3)
                    square(0, 2)

                def steps(b, room, guarded):
                    for c in range(1, CH + 1 if room else CH):
                        if ahead(c, 3, room):
                            y_low(b, c + 3)
                        if ahead(c, 2, room):
                            square(b, c + 2)
                        if c == CH:
                            pool.wait_ge(s["ylo"], done(b, CH + 3))
                            pool.wait_ge(s["ksq"], done(b, CH + 2))
                            pool.wait_ge(s["rc"], b + 1)
                            pool.wait_ge(s["ct"], b + 1)
                            normalise(b, pool, nc.gpsimd)

                batches(pool, "pool", first, steps)
                for sem in g.spent:
                    pool.sem_clear(sem)

            @block.vector
            def _(dve):
                for stage in ("kb", "krd", "kn1", "kn2", "krs", "km", "khi", "klo"):
                    dve.sem_inc(s[stage], CH)

                def k_bias(b, c):
                    b, c = at(b, c)
                    dve.wait_ge(s["kp"], done(b, c))
                    dve.wait_ge(s["km"], before(b, c))
                    nc.vector.tensor_tensor(kc[:, buf(c)], psum[:, K_BANK, :], g.bk[:], ALU.add).then_inc(s["kb"], 1)

                def k_reduce(b, c):
                    b, c = at(b, c)
                    dve.wait_ge(s["ksq"], done(b, c))
                    dve.wait_ge(s["krs"], before(b, c))
                    nc.vector.tensor_reduce(ss[:, buf(c)], head_view(sq[:, buf(c)]), AX_X, ALU.add).then_inc(s["krd"], 1)

                def k_norm(b, c):
                    b, c = at(b, c)
                    dve.wait_ge(s["kseed"], done(b, c))
                    rsqrt_refine(nc, dve, kr[:, buf(c)], ktmp[:, buf(c)], ss[:, buf(c)], HD * HEAD_EPS, kseed[:, buf(c)],
                                 s["kn1"], s["kn2"], done(b, c)).then_inc(s["krs"], 1)
                    dve.wait_ge(s["krs"], done(b, c))
                    dve.wait_ge(s["tr"], before(b, c))
                    nc.vector.scalar_tensor_tensor(out=head_view(kn[:, buf(c)]), in0=head_view(kc[:, buf(c)]),
                                                   scalar=HD ** 0.5, in1=spread(kr[:, buf(c)], HD),
                                                   op0=ALU.mult, op1=ALU.mult).then_inc(s["km"], 1)

                def k_split(b, c):
                    b, c = at(b, c)
                    w = LM if c == LAST else P
                    src = k32[:, buf(c), :, 0:w]
                    hi, lo = g.k_hi[:, buf(c), :, 0:w], g.k_lo[:, buf(c), :, 0:w]
                    dve.wait_ge(s["ke"], done(b, c))
                    dve.wait_ge(s["sc"], before(b, c))
                    nc.vector.tensor_copy(hi, src).then_inc(s["khi"], 1)
                    dve.wait_ge(s["khi"], done(b, c))
                    nc.vector.tensor_tensor(lo, src, hi.bitcast(F32), ALU.subtract).then_inc(s["klo"], 1)

                def queries(b, guarded):
                    dve.wait_ge(s["sc"], done(b, -1))
                    for rows, at in blocks:
                        nc.vector.tensor_copy(g.qbd_hi[rows, :, at], g.q[rows, :, bass.ds(b * SQ, SQ)]).then_inc(s["qb"], 1)
                    dve.wait_ge(s["qb"], b * parts(guarded) + 4)
                    for rows, at in blocks:
                        nc.vector.tensor_tensor(g.qbd_lo[rows, :, at], g.q[rows, :, bass.ds(b * SQ, SQ)],
                                                g.qbd_hi[rows, :, at].bitcast(F32), ALU.subtract).then_inc(s["qb"], 1)
                    if guarded:
                        dve.wait_ge(s["shift"], b * 16 + 16)
                        nc.vector.tensor_copy(shift[:], shift_raw[:]).then_inc(s["qb"], 1)

                def second_keys(b):
                    dve.wait_ge(s["sc"], done(b, -1))
                    hi, lo = (k[:, 2, :, DCA_ROW:DCA_ROW + DCA] for k in (g.k_hi, g.k_lo))
                    kd = g.kd[:, :, bass.ds(b * DCA, DCA)]
                    nc.vector.tensor_copy(hi, kd).then_inc(s["kd"], 1)
                    dve.wait_ge(s["kd"], b * 2 + 1)
                    nc.vector.tensor_tensor(lo, kd, hi.bitcast(F32), ALU.subtract).then_inc(s["kd"], 1)

                def first(guarded):
                    if guarded:
                        dve.wait_ge(s["select"], 16)
                        nc.vector.tensor_copy(select[:], select_raw[:]).then_inc(s["selected"], 1)
                    queries(0, guarded)
                    k_bias(0, 0)
                    k_reduce(0, 0)
                    k_norm(0, 0)
                    k_bias(0, 1)
                    k_split(0, 0)
                    k_reduce(0, 1)
                    k_norm(0, 1)

                def steps(b, room, guarded):
                    for c in range(CH):
                        if c == LAST and room:
                            queries(b + 1, guarded)
                        if ahead(c, 2, room):
                            k_bias(b, c + 2)
                        if ahead(c, 1, room):
                            k_split(b, c + 1)
                        if ahead(c, 2, room):
                            k_reduce(b, c + 2)
                            k_norm(b, c + 2)
                        if c == 5:
                            second_keys(b)
                        if c == LAST:
                            dve.wait_ge(s["oe"], b + 2)
                            nc.vector.reciprocal(rinv[:], o_sb[:, :, PW - 1:2 * PW:PW]).then_inc(s["rc"], 1)
                            if not room:
                                dve.wait_ge(s["rc"], B)
                                dve.wait_ge(s["ct"], B)
                                normalise(b, dve, nc.vector)

                batches(dve, "dve", first, steps)

            @block.tensor
            def _(pe):
                for stage in ("kp", "vp", "tr", "sc", "pv"):
                    pe.sem_inc(s[stage], CH)

                def project(b, c, bank, w_hi, w_lo, free, stage):
                    b, c = at(b, c)
                    pe.wait_ge(s["yhi"], done(b, c))
                    pe.wait_ge(s["ylo"], done(b, c))
                    pe.wait_ge(s[free], done(b, c - 1))
                    split_product(pe, psum[:, bank, :],
                                  [(g.y_hi[:, buf(c), k, :], g.y_lo[:, buf(c), k, :], w_hi[:, k, :], w_lo[:, k, :])
                                   for k in range(KC)]).then_inc(s[stage], 1)

                def keys(b, c):
                    project(b, c, K_BANK, g.wk_hi, g.wk_lo, "kb", "kp")

                def values(b, c):
                    project(b, c, V_BANK, g.wv_hi, g.wv_lo, "ve", "vp")

                def turn(b, c):
                    b, c = at(b, c)
                    pe.wait_ge(s["km"], done(b, c))
                    pe.wait_ge(s["ke"], done(b, c - 1))
                    if c == 4:
                        pe.wait_ge(s["ce"], b + 1)
                    transposes(pe, psum[:, TR_BANK, :], kn[:, buf(c), :], g.ident[:]).then_inc(s["tr"], 1)

                def scores(b, c, guarded):
                    b, c = at(b, c)
                    pe.wait_ge(s["khi"], done(b, c))
                    pe.wait_ge(s["klo"], done(b, c))
                    pe.wait_ge(s["ex"], done(b, c - 1))
                    if c == 0:
                        pe.wait_ge(s["qb"], b * parts(guarded) + parts(guarded))
                    if c == 0 and guarded:
                        pe.wait_ge(s["selected"], 1)
                    if c == LAST:
                        pe.wait_ge(s["kd"], b * 2 + 2)
                    for n in range(GROUPS):
                        out = psum[:, S_BANK + n // 2, (n % 2) * 4 * SQ:(n % 2 + 1) * 4 * SQ]
                        less = [(select[:, int(c == LAST), :], shift[:, n * 4 * SQ:(n + 1) * 4 * SQ])] if guarded else []
                        last = split_product(pe, out, [(g.k_hi[:, buf(c), n, :], g.k_lo[:, buf(c), n, :],
                                                        g.qbd_hi[:, n, :], g.qbd_lo[:, n, :])], less)
                    last.then_inc(s["sc"], 1)

                def weighted(b, c):
                    pe.wait_ge(s["ex"], done(b, c))
                    pe.wait_ge(s["ve"], done(b, c))
                    if c == 0:
                        pe.wait_ge(s["oe"], b + 1)
                    if c == LAST:
                        pe.wait_ge(s["vd"], b * 16 + 16)
                    for p in range(PAIRS):
                        v = g.v_last[:, p, :] if c == LAST else g.v[:, buf(c), p, :]
                        last = pe.matmul(o_bank[p][:, 0:v.shape[1]], probs[:, buf(c), p * P:(p + 1) * P], v,
                                         start=(c == 0 and p % 3 == 0), stop=(c == LAST), skip_group_check=True)
                    last.then_inc(s["pv"], 1)

                def turn_ctx(b):
                    pe.wait_ge(s["on"], b + 1)
                    if isinstance(b, int) and b == B:
                        pe.wait_ge(s["ke"], done(B - 1, LAST))
                    else:
                        pe.wait_ge(s["ke"], done(b, 3))
                    transposes(pe, psum[:, TR_BANK, :], g.ctx[:].rearrange("p q d -> p (q d)"), g.ident[:],
                               2).then_inc(s["ct"], 1)

                def first(guarded):
                    keys(0, 0)
                    values(0, 0)
                    keys(0, 1)
                    turn(0, 0)
                    values(0, 1)
                    scores(0, 0, guarded)

                def steps(b, room, guarded):
                    for c in range(CH):
                        if ahead(c, 2, room):
                            keys(b, c + 2)
                        if ahead(c, 1, room):
                            turn(b, c + 1)
                        if ahead(c, 2, room):
                            values(b, c + 2)
                        weighted(b, c)
                        if ahead(c, 1, room):
                            scores(b, c + 1, guarded)
                        if c == 2:
                            turn_ctx(b)

                batches(pe, "pe", first, steps)
                turn_ctx(B)


def load_experts(sp, io, g, e, n):
    if n < 2:
        return sp.dma_start(g.raw[:, n, :].rearrange("p (k n) -> p k n", k=KD),
                            io[("wg", "wu")[n]].rearrange("(k p) n -> p k n", p=P)[:, :, e * EW:(e + 1) * EW])
    return sp.dma_start(g.raw[:, n, :].rearrange("p (k n) -> p k n", k=EC),
                        io["wd"][e * EW:(e + 1) * EW, :].rearrange("(k p) n -> p k n", p=P))


def expert_buffers(nc, stack, v):
    return [[stack.enter_context(nc.sbuf_tensor(f"{name}_{part}{v}", [P, k, n], F32R, side="right")) for part in ("hi", "lo")]
            for name, k, n in (("wg", KD, EW), ("wu", KD, EW), ("wd", EC, D))]


def self_attention(nc, io, g, psum):
    VW = HD + 1
    OP, TR, QB, KB, SB, PB = 0, 1, 2, 3, 4, 6

    with ExitStack() as ctx:
        def sb(name, shape, dt=F32):
            return ctx.enter_context(nc.sbuf_tensor(name, shape, dt))

        s = Sems(nc, ctx, "sa")
        wo, wq, wk, wv, wo2, mask = g.wo, g.sa_wq, g.sa_wk, g.sa_wv, g.sa_wo, g.mask
        cx = sb("cx", [P, 2, KD, P])
        t1 = sb("t1", [P, 2, D])
        st = sb("sa_st", [P, 2, 6])
        mv = sb("sa_mv", [P, 2, 2])
        rs = sb("sa_rs", [P, 2, 1])
        rlog = sb("sa_rlog", [P, 2, 1])
        rseed = sb("sa_rseed", [P, 2, 1])
        rtmp = sb("sa_rtmp", [P, 2, 1])
        xn = sb("sa_xn", [P, 2, D])
        xT = sb("sa_xT", [P, 2, KD, P + SQ])
        qT = sb("sa_qT", [P, 2, GROUPS, P])
        kT = sb("sa_kT", [P, 2, 2, KV, SQ])
        vv = sb("sa_v", [P, 2, 2, KV, 2, VW])
        sm = sb("sa_s", [P, 2, H, SQ])
        mx = sb("sa_mx", [P, 2, H])
        pr = sb("sa_p", [P, 2, H, SQ])
        pT = sb("sa_pT", [P, 2, PAIRS, P])
        ri = sb("sa_ri", [P, 2, H])
        co = sb("sa_o", [P, 2, D])
        cT = sb("sa_oT", [P, 2, KD, P])

        def done(i, u):
            return i * 2 + (u + 3)

        def before(i, u):
            return i * 2 + (u + 1)

        def rounds(eng, steps):
            with eng.Fori(0, NT // 2 - 1) as i:
                steps(i, True)
            steps(NT // 2 - 1, False)

        def last_one(i, u):
            return i * 2 + (u + 2)

        with nc.Block() as block:
            @block.sync
            def _(sp):
                for n in range(3):
                    load_experts(sp, io, g, 0, n).then_inc(s["raw"], 16)
                    sp.wait_ge(s["raw"], 16 * (n + 1))

            @block.gpsimd
            def _(pool):
                nc.gpsimd.memset(vv[:], 0.0).then_inc(s["zero"], 1)
                nc.gpsimd.memset(kT[:], 0.0).then_inc(s["set"], 1)
                pool.wait_ge(s["zero"], 1)
                for b in range(2):
                    pool.wait_ge(s["set"], b + 1)
                    nc.gpsimd.memset(vv[b * SQ:(b + 1) * SQ, :, :, :, b, HD].rearrange("p u j v -> p (u j) v"), 1.0).then_inc(s["set"], 1)
                pool.wait_ge(s["set"], 3)
                for n, (hi, lo) in enumerate(g.experts[0]):
                    hi, lo = (w[:].rearrange("p k n -> p (k n)") for w in (hi, lo))
                    pool.wait_ge(s["raw"], 16 * (n + 1))
                    nc.gpsimd.tensor_copy(hi, g.raw[:, n, :]).then_inc(s["whi"], 1)
                    pool.wait_ge(s["whi"], n + 1)
                    nc.gpsimd.tensor_tensor(lo, g.raw[:, n, :], hi.bitcast(F32), ALU.subtract)

            @block.scalar
            def _(act):
                for stage in ("cx", "xe", "qe", "ve", "ex", "pe0", "pe1", "cte", "rlog", "rseed"):
                    act.sem_inc(s[stage], 2)

                def ctx_chunk(i, u):
                    act.wait_ge(s["op"], before(i, u))
                    nc.scalar.copy(cx[:, u].rearrange("p (g j) t -> p g j t", g=2),
                                   g.ctxT[:, :, :, bass.ds((i * 2 + u) * P + SQ, P)]).then_inc(s["cx"], 1)

                def seed(i, u):
                    act.wait_ge(s["ba"], done(i, u))
                    act.wait_ge(s["rs"], before(i, u))
                    rsqrt_seed(nc, act, rseed[:, u], rlog[:, u], mv[:, u, 1:2], g.cols[:, 9:10], s["rlog"],
                               done(i, u)).then_inc(s["rseed"], 1)

                def x_evac(i, u):
                    act.wait_ge(s["trx"], done(i, u))
                    act.wait_ge(s["vp"], before(i, u))
                    bank = psum[:, TR, :].rearrange("p (k t) -> p k t", k=KD)
                    nc.scalar.copy(xT[:, u, :, 0:P], bank)
                    nc.scalar.copy(xT[:, u, :, P:P + SQ], bank[:, :, 0:SQ]).then_inc(s["xe"], 1)

                def qv_evac(i, u):
                    act.wait_ge(s["qp"], done(i, u))
                    act.wait_ge(s["sp"], before(i, u))
                    nc.scalar.copy(qT[:, u], psum[:, QB, :].rearrange("p (g t) -> p g t", g=GROUPS)).then_inc(s["qe"], 1)
                    act.wait_ge(s["vp"], done(i, u))
                    act.wait_ge(s["pv"], before(i, u))
                    bank = psum[:, OP, 0:2 * P].rearrange("p (r v d) -> p r v d", r=2, v=KV)
                    for b in range(2):
                        rows = slice(b * SQ, (b + 1) * SQ)
                        for r in range(2):
                            last = nc.scalar.copy(vv[rows, u, b ^ r, :, b, 0:HD], bank[rows, r])
                    last.then_inc(s["ve"], 1)

                def exps(i, u):
                    act.wait_ge(s["sb"], done(i, u))
                    act.wait_ge(s["pt1"], before(i, u))
                    nc.scalar.activation(pr[:, u], sm[:, u], ACT.Exp).then_inc(s["ex"], 1)

                def p_evac(i, u, n):
                    act.wait_ge(s[f"pt{n}"], done(i, u))
                    act.wait_ge(s["pv"], before(i, u))
                    nc.scalar.copy(pT[:, u, 4 * n:4 * n + 4, :],
                                   psum[:, (QB, KB)[n], :].rearrange("p (h t) -> p h t", h=4)).then_inc(s[f"pe{n}"], 1)

                def o_evac(i, u):
                    act.wait_ge(s["trc"], done(i, u))
                    act.wait_ge(s["op2"], before(i, u))
                    nc.scalar.copy(cT[:, u], psum[:, TR, :].rearrange("p (k t) -> p k t", k=KD)).then_inc(s["cte"], 1)

                for u in range(2):
                    ctx_chunk(0, u)
                seed(0, 0)
                seed(0, 1)
                x_evac(0, 0)
                x_evac(0, 1)
                act.wait_ge(s["set"], 3)

                def steps(i, more):
                    for u in range(2):
                        qv_evac(i, u)
                    if more:
                        for u in range(2):
                            ctx_chunk(i + 1, u)
                    for u in range(2):
                        exps(i, u)
                        for n in range(2):
                            p_evac(i, u, n)
                    if more:
                        seed(i + 1, 0)
                    o_evac(i, 0)
                    if more:
                        seed(i + 1, 1)
                    o_evac(i, 1)
                    if more:
                        x_evac(i + 1, 0)
                        x_evac(i + 1, 1)

                rounds(act, steps)

            @block.vector
            def _(dve):
                for stage in ("tp", "x1", "bs", "ba", "rn1", "rn2", "rs", "xn", "ke", "sm", "mx", "sb", "ri", "co", "x2"):
                    dve.sem_inc(s[stage], 2)

                def residual(i, u):
                    dve.wait_ge(s["op"], done(i, u))
                    dve.wait_ge(s["x1"], before(i, u))
                    nc.vector.tensor_tensor(t1[:, u], psum[:, OP, :], g.bo[:], ALU.add).then_inc(s["tp"], 1)
                    dve.wait_ge(s["tp"], done(i, u))
                    x = g.x[:, i * 2 + u, :]
                    nc.vector.tensor_tensor(x, x, t1[:, u], ALU.add).then_inc(s["x1"], 1)

                def stats(i, u):
                    dve.wait_ge(s["x1"], done(i, u))
                    dve.wait_ge(s["ba"], before(i, u))
                    dve.sem_inc(s["gate"], 1)
                    nc.vector.bn_stats(st[:, u], g.x[:, i * 2 + u, :]).then_inc(s["bs"], 1)
                    dve.wait_ge(s["bs"], done(i, u))
                    dve.wait_ge(s["xn"], before(i, u))
                    dve.sem_inc(s["gate"], 1)
                    nc.vector.bn_aggr(mv[:, u], st[:, u]).then_inc(s["ba"], 1)

                def norm(i, u):
                    dve.wait_ge(s["rseed"], done(i, u))
                    rsqrt_refine(nc, dve, rs[:, u], rtmp[:, u], mv[:, u, 1:2], LN_EPS, rseed[:, u],
                                 s["rn1"], s["rn2"], done(i, u)).then_inc(s["rs"], 1)
                    dve.wait_ge(s["rs"], done(i, u))
                    dve.wait_ge(s["trx"], before(i, u))
                    nc.vector.tensor_scalar(xn[:, u], g.x[:, i * 2 + u, :], mv[:, u, 0:1], rs[:, u],
                                            ALU.subtract, ALU.mult).then_inc(s["xn"], 1)

                def keys(i, u):
                    dve.wait_ge(s["kp"], done(i, u))
                    dve.wait_ge(s["sp"], before(i, u))
                    bank = psum[:, KB, 0:P].rearrange("p (j t) -> p j t", j=2)
                    for n in range(KV):
                        rows = slice(n * HD, (n + 1) * HD)
                        last = nc.vector.tensor_copy(kT[rows, u, :, n, :], bank[rows])
                    last.then_inc(s["ke"], 1)

                def softmax(i, u):
                    dve.wait_ge(s["sp"], done(i, u))
                    dve.wait_ge(s["ex"], before(i, u))
                    nc.vector.scalar_tensor_tensor(
                        out=sm[:, u], in0=psum[:, SB:SB + 2, :].rearrange("p a (h t) -> p (a h) t", t=SQ), scalar=SCALE,
                        in1=mask[:].unsqueeze(1).to_broadcast([P, H, SQ]), op0=ALU.mult, op1=ALU.add).then_inc(s["sm"], 1)
                    dve.wait_ge(s["sm"], done(i, u))
                    dve.wait_ge(s["sb"], before(i, u))
                    nc.vector.tensor_reduce(mx[:, u], sm[:, u], AX_X, ALU.max).then_inc(s["mx"], 1)
                    dve.wait_ge(s["mx"], done(i, u))
                    nc.vector.tensor_tensor(sm[:, u], sm[:, u], spread(mx[:, u], SQ), ALU.subtract).then_inc(s["sb"], 1)

                def normalise(i, u):
                    dve.wait_ge(s["pv"], done(i, u))
                    dve.wait_ge(s["co"], before(i, u))
                    for a in range(2):
                        bank = psum[:, PB + a, 0:8 * VW].rearrange("p (h n) -> p h n", n=VW)
                        last = nc.vector.reciprocal(ri[:, u, 8 * a:8 * a + 8], bank[:, :, HD])
                    last.then_inc(s["ri"], 1)
                    dve.wait_ge(s["ri"], done(i, u))
                    dve.wait_ge(s["trc"], before(i, u))
                    for a in range(2):
                        bank = psum[:, PB + a, 0:8 * VW].rearrange("p (h n) -> p h n", n=VW)
                        last = nc.vector.tensor_tensor(head_view(co[:, u])[:, 8 * a:8 * a + 8, :], bank[:, :, 0:HD],
                                                       spread(ri[:, u, 8 * a:8 * a + 8], HD), ALU.mult)
                    last.then_inc(s["co"], 1)

                def residual2(i, u):
                    dve.wait_ge(s["op2"], done(i, u))
                    x = g.x[:, i * 2 + u, :]
                    nc.vector.tensor_tensor(x, x, psum[:, (OP, PB)[u], :], ALU.add).then_inc(s["x2"], 1)

                def stats2(i, u):
                    dve.wait_ge(s["x2"], done(i, u))
                    dve.sem_inc(s["gate"], 1)
                    nc.vector.bn_stats(g.st[:, i * 2 + u, :], g.x[:, i * 2 + u, :])

                def first_half(i, u):
                    residual(i, u)
                    stats(i, u)
                    norm(i, u)

                first_half(0, 0)
                first_half(0, 1)
                dve.wait_ge(s["set"], 3)

                def steps(i, more):
                    for u in range(2):
                        keys(i, u)
                    for u in range(2):
                        softmax(i, u)
                    if more:
                        residual(i + 1, 0)
                    normalise(i, 0)
                    if more:
                        stats(i + 1, 0)
                        norm(i + 1, 0)
                    normalise(i, 1)
                    if more:
                        first_half(i + 1, 1)
                    for u in range(2):
                        residual2(i, u)
                    for u in range(2):
                        stats2(i, u)

                rounds(dve, steps)

            @block.tensor
            def _(pe):
                for stage in ("op", "trx", "qp", "kp", "vp", "sp", "pt0", "pt1", "pv", "trc", "op2"):
                    pe.sem_inc(s[stage], 2)

                def out_product(i, u, half):
                    if half == 0:
                        pe.wait_ge(s["cx"], done(i, u))
                        if u:
                            pe.wait_ge(s["tp"], done(i, 0))
                        else:
                            pe.wait_ge(s["ve"], last_one(i, 0))
                    for k in (2 * half, 2 * half + 1):
                        last = pe.matmul(psum[:, OP, :], cx[:, u, k, :], wo[:, k, :], start=(k == 0), stop=(k == KD - 1))
                    if half:
                        last.then_inc(s["op"], 1)

                def turn_x(i, u):
                    pe.wait_ge(s["xn"], done(i, u))
                    if u:
                        pe.wait_ge(s["xe"], last_one(i, u))
                    else:
                        pe.wait_ge(s["cte"], last_one(i, u))
                    transposes(pe, psum[:, TR, :], xn[:, u, :], g.ident[:]).then_inc(s["trx"], 1)

                def qkv(i, u):
                    pe.wait_ge(s["xe"], done(i, u))
                    if u:
                        pe.wait_ge(s["qe"], last_one(i, u))
                    else:
                        pe.wait_ge(s["pe0"], last_one(i, u))
                    for n in range(GROUPS):
                        for k in range(KD):
                            last = pe.matmul(psum[:, QB, n * P:(n + 1) * P], wq[:, k, n * P:(n + 1) * P], xT[:, u, k, 0:P],
                                             start=(k == 0), stop=(k == KD - 1))
                    last.then_inc(s["qp"], 1)
                    if u:
                        pe.wait_ge(s["ke"], last_one(i, u))
                    else:
                        pe.wait_ge(s["pe1"], last_one(i, u))
                    product(pe, psum[:, KB, 0:P], wk, xT[:, u, :, 0:P]).then_inc(s["kp"], 1)
                    if u:
                        pe.wait_ge(s["ve"], last_one(i, u))
                    else:
                        pe.wait_ge(s["tp"], done(i, 1))
                        pe.wait_ge(s["x2"], last_one(i - 1, 1))
                    for r in range(2):
                        last = product(pe, psum[:, OP, r * P:(r + 1) * P], xT[:, u, :, r * SQ:r * SQ + P], wv[:])
                    last.then_inc(s["vp"], 1)

                def scores(i, u):
                    pe.wait_ge(s["qe"], done(i, u))
                    pe.wait_ge(s["ke"], done(i, u))
                    pe.wait_ge(s["sm"], last_one(i, u))
                    for n in range(GROUPS):
                        for j in range(2):
                            rows = slice(j * SQ, (j + 1) * SQ)
                            out = psum[rows, SB + n // 2, :].rearrange("p (v b t) -> p v b t", v=KV, b=2)[:, :, n % 2, :]
                            last = pe.matmul(out, qT[:, u, n, rows], kT[:, u, j], start=True, stop=True)
                    last.then_inc(s["sp"], 1)

                def turn_probs(i, u):
                    pe.wait_ge(s["ex"], done(i, u))
                    for n in range(2):
                        if u:
                            pe.wait_ge(s[f"pe{n}"], last_one(i, u))
                        elif n == 0:
                            pe.wait_ge(s["qe"], done(i, 1))
                        else:
                            pe.wait_ge(s["ke"], done(i, 1))
                        transposes(pe, psum[:, (QB, KB)[n], :],
                                   pr[:, u, 8 * n:8 * n + 8, :].rearrange("p h t -> p (h t)"), g.ident[:]).then_inc(s[f"pt{n}"], 1)

                def weighted(i, u):
                    pe.wait_ge(s["ve"], done(i, u))
                    pe.wait_ge(s["co"], last_one(i, u))
                    if u == 0:
                        pe.wait_ge(s["x2"], last_one(i, u))
                    for p in range(PAIRS):
                        if p % 4 == 0:
                            pe.wait_ge(s[f"pe{p // 4}"], done(i, u))
                        for j in range(2):
                            rows = slice(j * SQ, (j + 1) * SQ)
                            last = pe.matmul(psum[rows, PB + p // 4, (p % 4) * 2 * VW:(p % 4 + 1) * 2 * VW], pT[:, u, p, rows],
                                             vv[:, u, j, p % 4].rearrange("p b n -> p (b n)"), start=True, stop=True)
                    last.then_inc(s["pv"], 1)

                def turn_out(i, u):
                    pe.wait_ge(s["co"], done(i, u))
                    if u:
                        pe.wait_ge(s["cte"], last_one(i, u))
                    else:
                        pe.wait_ge(s["xe"], done(i, 1))
                    transposes(pe, psum[:, TR, :], co[:, u, :], g.ident[:]).then_inc(s["trc"], 1)

                def out_product2(i, u, more):
                    pe.wait_ge(s["cte"], done(i, u))
                    if u:
                        pe.wait_ge(s["co"], done(i, 1))
                    elif more:
                        pe.wait_ge(s["tp"], done(i + 1, 1))
                    else:
                        pe.wait_ge(s["tp"], done(i, 1))
                    product(pe, psum[:, (OP, PB)[u], :], cT[:, u], wo2[:]).then_inc(s["op2"], 1)

                for u in range(2):
                    for half in range(2):
                        out_product(0, u, half)
                turn_x(0, 0)
                turn_x(0, 1)

                def steps(i, more):
                    qkv(i, 0)
                    qkv(i, 1)
                    scores(i, 0)
                    if more:
                        out_product(i + 1, 0, 0)
                    scores(i, 1)
                    if more:
                        out_product(i + 1, 0, 1)
                    turn_probs(i, 0)
                    weighted(i, 0)
                    turn_probs(i, 1)
                    if more:
                        out_product(i + 1, 1, 0)
                    weighted(i, 1)
                    turn_out(i, 0)
                    if more:
                        out_product(i + 1, 1, 1)
                    turn_out(i, 1)
                    out_product2(i, 0, more)
                    if more:
                        turn_x(i + 1, 0)
                    out_product2(i, 1, more)
                    if more:
                        turn_x(i + 1, 1)

                rounds(pe, steps)


def experts(nc, io, g, psum):
    UP, TR, DN = 2, 4, 6

    with ExitStack() as ctx:
        def sb(name, shape, dt=F32):
            return ctx.enter_context(nc.sbuf_tensor(name, shape, dt))

        s = Sems(nc, ctx, "moe")
        wr = sb("wr", [P, KD, E_])
        iota = sb("iota", [P, E_])
        mv = sb("moe_mv", [P, NT, 2])
        rs = sb("moe_rs", [P, NT])
        rlog = sb("moe_rlog", [P, NT])
        rseed = sb("moe_rseed", [P, NT])
        rtmp = sb("moe_rtmp", [P, NT])
        xn = sb("moe_xn", [P, 2, D])
        xT = sb("moe_xT", [P, 2, KD, P])
        x_hi = sb("moe_xhi", [P, NT, KD, P], F32R)
        x_lo = sb("moe_xlo", [P, NT, KD, P], F32R)
        sc = sb("moe_sc", [P, NT, E_])
        top = sb("moe_top", [P, NT, 8])
        idx = sb("moe_idx", [P, NT, 8], U32)
        idf = sb("moe_idf", [P, NT, 2])
        gap = sb("moe_gap", [P, NT])
        ex = sb("moe_ex", [P, NT])
        ex1 = sb("moe_ex1", [P, NT])
        w12 = sb("moe_w12", [P, 2, NT])
        pick = sb("moe_pick", [P, 2, NT, E_])
        wt = sb("moe_wt", [P, NT, E_])
        act_g = sb("moe_g", [P, 2, EW])
        hid = sb("moe_h", [P, 2, EW])
        h_hi = sb("moe_hhi", [P, 2, EC, P], F32R)
        h_lo = sb("moe_hlo", [P, 2, EC, P], F32R)
        weights = g.experts + [expert_buffers(nc, ctx, 1)]

        def flat(w):
            return w[:].rearrange("p k n -> p (k n)")

        def split_done(i, v, n):
            return i * 6 + (v * 3 + n + 4)

        def chunk(i, v, t):
            return i * (2 * NT) + (v * NT + t + 3)

        with nc.Block() as block:
            @block.sync
            def _(sp):
                sp.dma_start(wr[:], io["wr"].rearrange("(k p) n -> p k n", p=P)).then_inc(s["wr"], 16)
                sp.dma_start(iota[:], io["iota"].partition_broadcast(P)).then_inc(s["wr"], 16)
                for e in range(EP):
                    for n in range(3):
                        if e:
                            sp.wait_ge(s["wlo"], e * 3 + (n + 1))
                        load_experts(sp, io, g, (e + 1) % EP, n).then_inc(s[f"raw{n}"], 16)
                for t in range(NT):
                    sp.wait_ge(s["ya"], chunk(1, 1, t))
                    sp.dma_start(io["out"].rearrange("(t p) d -> p t d", p=P)[:, t, :], g.x[:, t, :]).then_inc(s["out"], 16)
                sp.wait_ge(s["out"], 16 * NT)

            @block.gpsimd
            def _(pool):
                with pool.Fori(0, EP // 2) as i:
                    for v in range(2):
                        for n, (hi, lo) in enumerate(weights[1 - v]):
                            pool.wait_ge(s["whi"], split_done(i, v, n))
                            nc.gpsimd.tensor_tensor(flat(lo), g.raw[:, n, :], flat(hi).bitcast(F32),
                                                    ALU.subtract).then_inc(s["wlo"], 1)

            @block.scalar
            def _(act):
                act.preload_act_table_set(TABLES)
                act.wait_ge(s["ba"], NT)
                rsqrt_seed(nc, act, rseed[:], rlog[:], mv[:, :, 1], g.cols[:, 9:10], s["rlog"], 1).then_inc(s["rseed"], 1)
                for t in range(NT):
                    u = t % 2
                    act.wait_ge(s["trx"], t + 1)
                    if t >= 2:
                        act.wait_ge(s["rp"], t - 1)
                        act.wait_ge(s["xlo"], t - 1)
                    nc.scalar.copy(xT[:, u], psum[:, TR + u, :].rearrange("p (k t) -> p k t", k=KD)).then_inc(s["xe"], 1)
                    act.wait_ge(s["xe"], t + 1)
                    nc.scalar.copy(x_hi[:, t], xT[:, u]).then_inc(s["xhi"], 1)
                act.wait_ge(s["gap"], 1)
                nc.scalar.activation(ex[:], gap[:], ACT.Exp).then_inc(s["ex"], 1)
                for stage in ("sg", "hhi"):
                    act.sem_inc(s[stage], 2)
                act.preload_act_table(ACT.Silu)

                def silu(i, v, t):
                    act.wait_ge(s["gp"], chunk(i, v, t))
                    act.wait_ge(s["hd"], chunk(i, v, t - 2))
                    nc.scalar.activation(act_g[:, t % 2], psum[:, t % 2, 0:EW], ACT.Silu).then_inc(s["sg"], 1)

                def high(i, v, t):
                    act.wait_ge(s["trh"], chunk(i, v, t))
                    act.wait_ge(s["dp"], chunk(i, v, t - 2))
                    nc.scalar.copy(h_hi[:, t % 2], psum[:, TR + t % 2, 0:EW].rearrange("p (k t) -> p k t", k=EC)).then_inc(s["hhi"], 1)

                with act.Fori(0, EP // 2) as i:
                    for v in range(2):
                        for t in range(NT):
                            silu(i, v, t)
                            if t:
                                high(i, v, t - 1)
                        high(i, v, NT - 1)

            @block.vector
            def _(dve):
                for stage in ("hd", "hlo", "ya"):
                    dve.sem_inc(s[stage], 2)
                dve.sem_inc(s["whi"], 3)
                for t in range(NT):
                    nc.vector.bn_aggr(mv[:, t, :], g.st[:, t, :]).then_inc(s["ba"], 1)
                dve.wait_ge(s["rseed"], 1)
                rsqrt_refine(nc, dve, rs[:], rtmp[:], mv[:, :, 1], LN_EPS, rseed[:], s["rn1"], s["rn2"], 1).then_inc(s["rs"], 1)
                dve.wait_ge(s["rs"], 1)
                for t in range(NT):
                    if t >= 2:
                        dve.wait_ge(s["trx"], t - 1)
                    nc.vector.tensor_scalar(xn[:, t % 2], g.x[:, t, :], mv[:, t, 0:1], rs[:, t:t + 1],
                                            ALU.subtract, ALU.mult).then_inc(s["xn"], 1)
                    if t:
                        dve.wait_ge(s["xhi"], t)
                        nc.vector.tensor_tensor(x_lo[:, t - 1], xT[:, (t - 1) % 2], x_hi[:, t - 1].bitcast(F32),
                                                ALU.subtract).then_inc(s["xlo"], 1)
                dve.wait_ge(s["xhi"], NT)
                nc.vector.tensor_tensor(x_lo[:, NT - 1], xT[:, (NT - 1) % 2], x_hi[:, NT - 1].bitcast(F32),
                                        ALU.subtract).then_inc(s["xlo"], 1)

                chain = [0]

                def link(ins):
                    chain[0] += 1
                    ins.then_inc(s["chain"], 1)
                    dve.wait_ge(s["chain"], chain[0])

                dve.wait_ge(s["rp"], NT)
                dve.wait_ge(s["wr"], 32)
                link(nc.vector.tensor_copy(sc[:], psum[:, DN + 1, 0:NT * E_].rearrange("p (t e) -> p t e", t=NT)))
                for t in range(NT):
                    last = nc.vector.max(out=top[:, t, :], in_=sc[:, t, :])
                link(last)
                for t in range(NT):
                    last = nc.vector.max_index(out=idx[:, t, :], in_max=top[:, t, :], in_values=sc[:, t, :])
                link(last)
                link(nc.vector.tensor_copy(idf[:], idx[:, :, 0:2]))
                nc.vector.tensor_tensor(gap[:], top[:, :, 1], top[:, :, 0], ALU.subtract).then_inc(s["gap"], 1)
                dve.wait_ge(s["ex"], 1)
                link(nc.vector.tensor_scalar(ex1[:], ex[:], 1.0, None, ALU.add))
                link(nc.vector.reciprocal(w12[:, 0], ex1[:]))
                link(nc.vector.tensor_tensor(w12[:, 1], ex[:], w12[:, 0], ALU.mult))
                for n in range(2):
                    link(nc.vector.tensor_tensor(pick[:, n], iota[:].unsqueeze(1).to_broadcast([P, NT, E_]),
                                                 spread(idf[:, :, n], E_), ALU.is_equal))
                    link(nc.vector.tensor_tensor(pick[:, n], pick[:, n], spread(w12[:, n], E_), ALU.mult))
                link(nc.vector.tensor_tensor(wt[:], pick[:, 0], pick[:, 1], ALU.add))

                def weights_high(i, v, n):
                    dve.wait_ge(s[f"raw{n}"], i * 32 + (v * 16 + 16))
                    dve.wait_ge(s["dp"], chunk(i, v, -1))
                    nc.vector.tensor_copy(flat(weights[1 - v][n][0]), g.raw[:, n, :]).then_inc(s["whi"], 1)

                def hidden(i, v, t):
                    dve.wait_ge(s["sg"], chunk(i, v, t))
                    dve.wait_ge(s["gp"], chunk(i, v, t))
                    dve.wait_ge(s["trh"], chunk(i, v, t - 2))
                    for n in range(2):
                        cols = slice(n * F, (n + 1) * F)
                        last = nc.vector.scalar_tensor_tensor(
                            out=hid[:, t % 2, cols], in0=act_g[:, t % 2, cols],
                            scalar=wt[:, t, bass.ds(i * 4 + (v * 2 + n), 1)],
                            in1=psum[:, UP + t % 2, cols], op0=ALU.mult, op1=ALU.mult)
                    last.then_inc(s["hd"], 1)

                def low(i, v, t):
                    dve.wait_ge(s["hhi"], chunk(i, v, t))
                    dve.wait_ge(s["dp"], chunk(i, v, t - 2))
                    nc.vector.tensor_tensor(h_lo[:, t % 2], psum[:, TR + t % 2, 0:EW].rearrange("p (k t) -> p k t", k=EC),
                                            h_hi[:, t % 2].bitcast(F32), ALU.subtract).then_inc(s["hlo"], 1)

                def add(i, v, t):
                    dve.wait_ge(s["dp"], chunk(i, v, t))
                    nc.vector.tensor_tensor(g.x[:, t, :], g.x[:, t, :], psum[:, DN + t % 2, :], ALU.add).then_inc(s["ya"], 1)

                with dve.Fori(0, EP // 2) as i:
                    for v in range(2):
                        for t in range(NT):
                            hidden(i, v, t)
                            if t:
                                low(i, v, t - 1)
                            if t >= 2:
                                add(i, v, t - 2)
                            if 2 <= t < 5:
                                weights_high(i, v, t - 2)
                        low(i, v, NT - 1)
                        add(i, v, NT - 2)
                        add(i, v, NT - 1)

            @block.tensor
            def _(pe):
                def turn_x(t):
                    pe.wait_ge(s["xn"], t + 1)
                    if t >= 2:
                        pe.wait_ge(s["xe"], t - 1)
                    transposes(pe, psum[:, TR + t % 2, :], xn[:, t % 2, :], g.ident[:]).then_inc(s["trx"], 1)

                def router(t):
                    pe.wait_ge(s["xe"], t + 1)
                    product(pe, psum[:, DN + 1, t * E_:(t + 1) * E_], xT[:, t % 2], wr[:]).then_inc(s["rp"], 1)

                turn_x(0)
                pe.wait_ge(s["wr"], 32)
                for t in range(1, NT):
                    turn_x(t)
                    router(t - 1)
                router(NT - 1)
                for stage in ("gp", "trh", "dp"):
                    pe.sem_inc(s[stage], 2)
                pe.sem_inc(s["wlo"], 3)
                pe.wait_ge(s["xlo"], NT)

                def gate_up(i, v, t):
                    pe.wait_ge(s["hd"], chunk(i, v, t - 2))
                    for bank, (hi, lo) in ((t % 2, weights[v][0]), (UP + t % 2, weights[v][1])):
                        last = split_product(pe, psum[:, bank, 0:EW],
                                             [(x_hi[:, t, k, :], x_lo[:, t, k, :], hi[:, k, :], lo[:, k, :])
                                              for k in range(KD)])
                    last.then_inc(s["gp"], 1)

                def down(i, v, t):
                    pe.wait_ge(s["hd"], chunk(i, v, t))
                    pe.wait_ge(s["hlo"], chunk(i, v, t - 2))
                    transposes(pe, psum[:, TR + t % 2, :], hid[:, t % 2, :], g.ident[:], EC).then_inc(s["trh"], 1)

                def down2(i, v, t):
                    wd_hi, wd_lo = weights[v][2]
                    pe.wait_ge(s["hhi"], chunk(i, v, t))
                    pe.wait_ge(s["hlo"], chunk(i, v, t))
                    pe.wait_ge(s["ya"], chunk(i, v, t - 2))
                    if v == 0 and t == 1:
                        pe.wait_ge(s["chain"], 1)
                    split_product(pe, psum[:, DN + t % 2, :],
                                  [(h_hi[:, t % 2, k, :], h_lo[:, t % 2, k, :], wd_hi[:, k, :], wd_lo[:, k, :])
                                   for k in range(EC)]).then_inc(s["dp"], 1)

                with pe.Fori(0, EP // 2) as i:
                    for v in range(2):
                        pe.wait_ge(s["wlo"], split_done(i, v, -1))
                        for t in range(NT + 2):
                            if t < NT:
                                gate_up(i, v, t)
                            if 1 <= t <= NT:
                                down(i, v, t - 1)
                            if t >= 2:
                                down2(i, v, t - 2)


def build(nc, io):
    with ExitStack() as ctx:
        psum = ctx.enter_context(nc.psum_tensor("psum", [P, 8, 512], F32))

        class Shared:
            pass
        g = Shared()
        g.guards = {}

        def sb(stack, name, shape, dt=F32):
            return stack.enter_context(nc.sbuf_tensor(name, shape, dt))

        g.x = sb(ctx, "x_sb", [P, NT, D])
        g.ident = sb(ctx, "ident_sb", [P, P])
        g.st = sb(ctx, "x_stats", [P, NT, 6])
        g.cols = sb(ctx, "cols_sb", [P, 10])
        moe = ctx.enter_context(ExitStack())
        with ExitStack() as out_ctx:
            g.bo = sb(out_ctx, "bo_sb", [P, D])
            g.ctxT = sb(out_ctx, "ctxT", [P, 2, 2, T + SQ])
            g.wo = sb(out_ctx, "xa_wo", [P, KD, D])
            g.sa_wq = sb(out_ctx, "sa_wq", [P, KD, D])
            g.sa_wk = sb(out_ctx, "sa_wk", [P, KD, P])
            g.sa_wv = sb(out_ctx, "sa_wv", [P, KD, P])
            g.mask = sb(out_ctx, "mask", [P, SQ])
            g.sa_wo = sb(out_ctx, "sa_wo", [P, KD, D])
            g.landed = [out_ctx.enter_context(nc.semaphore(f"context_{n}")) for n in range(len(LANDING))]
            with ExitStack() as xa:
                g.guard = sb(xa, "guard", [1, 1], I32)
                g.bk = sb(xa, "bk_sb", [P, D])
                g.wk_hi = sb(xa, "wk_hi", [P, KC, D], F32R)
                g.wk_lo = sb(xa, "wk_lo", [P, KC, D], F32R)
                g.wv_hi = sb(xa, "wv_hi", [P, KC, D], F32R)
                g.wv_lo = sb(xa, "wv_lo", [P, KC, D], F32R)
                g.q = sb(xa, "q_sb", [P, GROUPS, T])
                g.kd = sb(xa, "kd_sb", [P, GROUPS, B * DCA])
                g.y = sb(xa, "y_sb", [P, KC, SM])
                g.qbd_hi = sb(xa, "qbd_hi", [P, GROUPS, 4 * SQ], F32R)
                g.qbd_lo = sb(xa, "qbd_lo", [P, GROUPS, 4 * SQ], F32R)
                g.y_hi = sb(xa, "y_hi", [P, 3, KC, P], F32R)
                g.y_lo = sb(xa, "y_lo", [P, 3, KC, P], F32R)
                g.k_hi = sb(xa, "k_hi", [P, 3, GROUPS, P], F32R)
                g.k_lo = sb(xa, "k_lo", [P, 3, GROUPS, P], F32R)
                g.v = sb(xa, "v_sb", [P, 2, PAIRS, PW])
                g.v_last = sb(xa, "v_last", [P, PAIRS, 2 * PW])
                g.ctx = sb(xa, "ctx_sb", [P, PAIRS, HD])
                prepare(nc, io, g, psum)
                score_maxima(nc, io, g, psum)
                cross_attention(nc, io, g, psum)
            g.raw = moe.enter_context(nc.sbuf_tensor("expert_raw", [P, 3, KD * EW], F32, side="right"))
            g.experts = [expert_buffers(nc, moe, 0)]
            self_attention(nc, io, g, psum)
        experts(nc, io, g, psum)


def kernel(**inputs):
    import numpy as np
    import concourse.bacc as bacc
    from concourse.bass_utils import run_bass_kernel_spmd

    a = {k: np.asarray(v) for k, v in inputs.items()}
    f32 = np.float32
    G2 = PAIRS // 4

    kv_w = np.concatenate([a["L0_xattn_Wk"], a["L0_xattn_Wv"]], 1).reshape(DC, H, 2, HD)
    kv_b = np.concatenate([a["L0_xattn_bk"], a["L0_xattn_bv"]]).reshape(H, 2, HD)
    dca_w = a["L0_xattn_Wkv_dca"].reshape(DC, 2, D)
    dca_b = a["L0_xattn_bkv_dca"].reshape(2, D)

    def by_pair(v):
        return v.reshape((G2, 4, 2, HD) + v.shape[1:]).swapaxes(1, 2).reshape((KD, P) + v.shape[1:])

    rows = np.arange(P)
    cols = np.stack([np.tile(a[f"L0_xattn_{n}"], 4) for n in ("qn_w", "qn_b", "kn_w", "kn_b", "kn_dca_w", "kn_dca_b")]
                    + [(rows < LM).astype(f32), ((rows >= DCA_ROW) & (rows < DCA_ROW + DCA)).astype(f32),
                       np.full(P, HD * HEAD_EPS, f32), np.full(P, LN_EPS, f32)], 1)
    context = a["ctx_1024"]
    arrays = {
        "x": a["x"].reshape(T, D),
        "y": context[:, :SM].transpose(0, 2, 1),
        "yd": context[:, SM:].transpose(2, 0, 1).reshape(DC, B * DCA),
        "wq": a["L0_xattn_Wq"], "bq": a["L0_xattn_bq"],
        "wk": kv_w[:, :, 0].reshape(DC, D), "wv": kv_w[:, :, 1].reshape(DC, D), "bk": kv_b[:, 0].reshape(D),
        "wkd": dca_w[:, 0], "wvd": dca_w[:, 1], "bkd": dca_b[0],
        "bv": np.concatenate([by_pair(kv_b[:, 1].reshape(D)), by_pair(dca_b[1])], 0).T,
        "wo": by_pair(a["L0_xattn_Wo"]), "bo": a["L0_xattn_bo"],
        "cols": cols,
        "norms": np.concatenate([a[f"L0_xattn_{n}"] for n in ("qn_w", "qn_b", "kn_w", "kn_b", "kn_dca_w", "kn_dca_b")])[None],
        "select": np.stack([np.ones(P), np.zeros(P), rows < LM, (rows >= DCA_ROW) & (rows < DCA_ROW + DCA)]).reshape(2, 2, P)
                    .swapaxes(0, 1).reshape(2, 2 * P).astype(f32),
        "ident": np.eye(P, dtype=f32),
        "mask": np.where(np.arange(SQ)[None] <= rows[:, None] % SQ, 0.0, MASKED).astype(f32),
        "iota": np.arange(E_, dtype=f32),
        "sa_wq": a["L0_attn_Wq"].reshape(D, KV, 4, HD).swapaxes(1, 2).reshape(D, D),
        "sa_wk": a["L0_attn_Wk"], "sa_wv": a["L0_attn_Wv"],
        "sa_wo": a["L0_attn_Wo"].reshape(KV, 2, 2, HD, D).transpose(1, 0, 2, 3, 4).reshape(D, D),
        "wr": a["L0_ffn_w_gate_router"].T,
        "wg": a["L0_ffn_w_gate_proj"].transpose(2, 0, 1).reshape(D, E_ * F),
        "wu": a["L0_ffn_w_up_proj"].transpose(2, 0, 1).reshape(D, E_ * F),
        "wd": a["L0_ffn_w_down_proj"].transpose(0, 2, 1).reshape(E_ * F, D),
    }
    arrays = {f"in_{k}": np.ascontiguousarray(v) for k, v in arrays.items()}
    nc = bacc.Bacc("TRN2", target_bir_lowering=False, num_devices=1)
    io = {k[3:]: nc.dram_tensor(k, v.shape, F32, kind="ExternalInput").ap() for k, v in arrays.items()}
    io["out"] = nc.dram_tensor("out_dram", (T, D), F32, kind="ExternalOutput").ap()
    io["shift"] = nc.dram_tensor("shift_dram", (B, 2 * PAIRS, P), F32, kind="Internal").ap()
    io["vd"] = nc.dram_tensor("vd_dram", (B * DCA, D), F32, kind="Internal").ap()
    build(nc, io)
    r = run_bass_kernel_spmd(nc, [arrays], core_ids=[0])
    return r.results[0]["out_dram"].reshape(B, SQ, D)
```
